# Optimizing a Trainium2 kernel written in Bass

```python
import numpy as np
import jax
import jax.numpy as jnp

def _softmax(x, axis=-1):
    return jax.nn.softmax(x, axis=axis)

def _gelu(x):
    return jax.nn.gelu(x, approximate=True)

def _silu(x):
    return jax.nn.silu(x)

def _sigmoid(x):
    return jax.nn.sigmoid(x)

def _layernorm(x, axis=-1, eps=1e-05):
    m = jnp.mean(x, axis=axis, keepdims=True)
    v = jnp.var(x, axis=axis, keepdims=True)
    return (x - m) / jnp.sqrt(v + eps)

def _scatter_add(tgt, idx, src, axis=0):
    return tgt.at[idx].add(src)

def _segment_sum(src, seg, n):
    return jax.ops.segment_sum(src, seg, n)
kernel_name = 'mk_adaln_d1_jaxref_r4_30316a'

def setup_inputs(seed: int=0):
    np.random.seed(seed)
    _w = jnp.asarray

    def _L0_attn_setup():
        import jax, jax.numpy as jnp
        import numpy as np
        B, L, D_MODEL, NH = (1, 512, 256, 8)
        H = D_MODEL // NH
        SCALE = 0.02
        key = jax.random.key(seed)
        ks = jax.random.split(key, 13)
        d = D_MODEL
        return {'u': jax.random.normal(ks[0], (B, L, d), dtype=jnp.float32), 'Wq': jax.random.normal(ks[1], (d, d), dtype=jnp.float32) * SCALE, 'bq': jax.random.normal(ks[2], (d,), dtype=jnp.float32) * SCALE, 'Wk': jax.random.normal(ks[3], (d, d), dtype=jnp.float32) * SCALE, 'bk': jax.random.normal(ks[4], (d,), dtype=jnp.float32) * SCALE, 'Wv': jax.random.normal(ks[5], (d, d), dtype=jnp.float32) * SCALE, 'bv': jax.random.normal(ks[6], (d,), dtype=jnp.float32) * SCALE, 'ssm_k_kernel': jax.random.normal(ks[7], (d, L), dtype=jnp.float32) * SCALE, 'ssm_k_D': jax.random.normal(ks[8], (d,), dtype=jnp.float32), 'ssm_kernel': jax.random.normal(ks[9], (H, L), dtype=jnp.float32) * SCALE, 'D': jax.random.normal(ks[10], (H,), dtype=jnp.float32), 'Wo': jax.random.normal(ks[11], (d, d), dtype=jnp.float32) * SCALE, 'bo': jax.random.normal(ks[12], (d,), dtype=jnp.float32) * SCALE}
    _L0_attn_in = _L0_attn_setup()

    def _L0_ffn_setup():
        import jax, jax.numpy as jnp
        import numpy as np
        import math
        EMBED_DIM = 256
        FFN_DIM = 1024
        N_EXPERTS = 8
        TOP_K = 2
        CAP_FACTOR = 1.25
        key = jax.random.key(seed)
        k0, k1, k2, k3 = jax.random.split(key, 4)
        B, S = (4, 512)
        x = jax.random.normal(k0, (B, S, EMBED_DIM), dtype=jnp.float32)
        Wr = jax.random.normal(k1, (EMBED_DIM, N_EXPERTS), dtype=jnp.float32) * 0.02
        W1 = jax.random.normal(k2, (N_EXPERTS, EMBED_DIM, FFN_DIM), dtype=jnp.float32) * 0.02
        W2 = jax.random.normal(k3, (N_EXPERTS, FFN_DIM, EMBED_DIM), dtype=jnp.float32) * 0.02
        return {'x': x, 'Wr': Wr, 'W1': W1, 'W2': W2}
    _L0_ffn_in = _L0_ffn_setup()
    _L0_c = _w((lambda *s: np.random.randn(*s).astype(np.float32) * 0.05)(4, 256))
    _L0_wmod = _w((lambda *s: np.random.randn(*s).astype(np.float32) * 0.05)(256, 6 * 256) * 256 ** (-0.5))
    _d = {'L0_attn_u': _L0_attn_in['u'], 'L0_attn_Wq': _L0_attn_in['Wq'], 'L0_attn_bq': _L0_attn_in['bq'], 'L0_attn_Wk': _L0_attn_in['Wk'], 'L0_attn_bk': _L0_attn_in['bk'], 'L0_attn_Wv': _L0_attn_in['Wv'], 'L0_attn_bv': _L0_attn_in['bv'], 'L0_attn_ssm_k_kernel': _L0_attn_in['ssm_k_kernel'], 'L0_attn_ssm_k_D': _L0_attn_in['ssm_k_D'], 'L0_attn_ssm_kernel': _L0_attn_in['ssm_kernel'], 'L0_attn_D': _L0_attn_in['D'], 'L0_attn_Wo': _L0_attn_in['Wo'], 'L0_attn_bo': _L0_attn_in['bo'], 'L0_ffn_Wr': _L0_ffn_in['Wr'], 'L0_ffn_W1': _L0_ffn_in['W1'], 'L0_ffn_W2': _L0_ffn_in['W2'], 'L0_c': _L0_c, 'L0_wmod': _L0_wmod}
    _x0 = _d['L0_attn_u']
    _d['L0_attn_u'] = jax.random.normal(jax.random.fold_in(jax.random.key(seed), 1), (4, 1024, 256), dtype=_x0.dtype)
    del _x0
    return _d

def reference(L0_attn_u, L0_attn_Wq, L0_attn_bq, L0_attn_Wk, L0_attn_bk, L0_attn_Wv, L0_attn_bv, L0_attn_ssm_k_kernel, L0_attn_ssm_k_D, L0_attn_ssm_kernel, L0_attn_D, L0_attn_Wo, L0_attn_bo, L0_ffn_Wr, L0_ffn_W1, L0_ffn_W2, L0_c, L0_wmod):

    def _L0_attn_ref(u, Wq, bq, Wk, bk, Wv, bv, ssm_k_kernel, ssm_k_D, ssm_kernel, D, Wo, bo):
        import jax, jax.numpy as jnp
        import numpy as np
        B, L, D_MODEL, NH = (1, 512, 256, 8)
        H = D_MODEL // NH
        SCALE = 0.02
        b, l, d = u.shape
        nh = NH
        h = d // nh
        n = 2 * l
        q = jnp.einsum('bld,ed->bel', u, Wq) + bq[None, :, None]
        k = jnp.einsum('bld,ed->bel', u, Wk) + bk[None, :, None]
        v = jnp.einsum('bld,ed->bel', u, Wv) + bv[None, :, None]
        kk_f = jnp.fft.rfft(ssm_k_kernel, n=n, axis=-1)
        k_f = jnp.fft.rfft(k, n=n, axis=-1)
        shift_k = jnp.fft.irfft(kk_f * k_f, n=n, axis=-1)[..., :l]
        k = shift_k + ssm_k_D[:, None] * k
        kq = k.reshape(b, h, nh, l).transpose(0, 2, 1, 3)[:, :, None]
        vv = v.reshape(b, h, nh, l).transpose(0, 2, 1, 3)[:, None]
        kv = kq * vv
        kern_f = jnp.fft.rfft(ssm_kernel, n=n, axis=-1)
        y = jnp.fft.irfft(jnp.fft.rfft(kv, n=n, axis=-1) * kern_f, n=n, axis=-1)[..., :l]
        y = y + kv * D[:, None]
        q5 = q.reshape(b, h, nh, l).transpose(0, 2, 1, 3)[:, :, None]
        y = (q5 * y).sum(axis=1)
        y = y.reshape(b, d, l)
        y = y.transpose(0, 2, 1)
        return y @ Wo.T + bo

    def _L0_ffn_ref(x, Wr, W1, W2):
        import jax, jax.numpy as jnp
        import numpy as np
        import math
        EMBED_DIM = 256
        FFN_DIM = 1024
        N_EXPERTS = 8
        TOP_K = 2
        CAP_FACTOR = 1.25
        B, S, D = x.shape
        t = B * S
        xf = x.reshape(t, D)
        probs = jax.nn.softmax(xf.astype(jnp.float32) @ Wr, axis=-1)
        topk_probs, topk_experts = jax.lax.top_k(probs, TOP_K)
        cap = max(math.ceil(t * TOP_K * CAP_FACTOR / N_EXPERTS), 1)
        y = jnp.zeros_like(xf)
        for e in range(N_EXPERTS):
            mask = topk_experts == e
            gate = jnp.sum(jnp.where(mask, topk_probs, 0.0), axis=-1)
            has = jnp.any(mask, axis=-1)
            g_masked = jnp.where(has, gate, -jnp.inf)
            vals, idx = jax.lax.top_k(g_masked, cap)
            g = jnp.where(jnp.isfinite(vals), vals, 0.0)
            xe = xf[idx]
            h = jax.nn.relu(xe @ W1[e]) @ W2[e]
            y = y.at[idx].add(g[:, None] * h)
        return y.reshape(B, S, D)
    x = L0_attn_u
    mod = (_silu(L0_c) @ L0_wmod).reshape(L0_c.shape[0], 6, 1, -1)
    sa, ca, ga, sb, cb, gb = (mod[:, 0], mod[:, 1], mod[:, 2], mod[:, 3], mod[:, 4], mod[:, 5])
    ga = (2 * (ga >= 0) - 1) * jnp.maximum(jnp.abs(ga), 0.25)
    gb = (2 * (gb >= 0) - 1) * jnp.maximum(jnp.abs(gb), 0.25)
    h = _layernorm(x, axis=-1) * (1 + ca) + sa
    x = x + ga * _L0_attn_ref(h, L0_attn_Wq, L0_attn_bq, L0_attn_Wk, L0_attn_bk, L0_attn_Wv, L0_attn_bv, L0_attn_ssm_k_kernel, L0_attn_ssm_k_D, L0_attn_ssm_kernel, L0_attn_D, L0_attn_Wo, L0_attn_bo)
    h = _layernorm(x, axis=-1) * (1 + cb) + sb
    x = x + gb * _L0_ffn_ref(h, L0_ffn_Wr, L0_ffn_W1, L0_ffn_W2)
    return x

_drawn_inputs = setup_inputs


def setup_inputs(seed=0):
    import zlib

    import numpy as np

    out = dict(_drawn_inputs(seed))
    spreads = {}
    factors = {'L0_attn_Wq': 6.529,
     'L0_attn_bq': 8.0,
     'L0_attn_Wk': 6.43,
     'L0_attn_bk': 8.0,
     'L0_attn_Wv': 6.377,
     'L0_attn_bv': 8.0,
     'L0_attn_ssm_k_kernel': 8.0,
     'L0_attn_ssm_k_D': 7.064,
     'L0_attn_ssm_kernel': 8.0,
     'L0_attn_D': 6.567,
     'L0_attn_Wo': 6.367,
     'L0_attn_bo': 64.0,
     'L0_ffn_Wr': 57.984,
     'L0_ffn_W1': 59.84,
     'L0_ffn_W2': 49.744,
     'L0_c': 4.209,
     'L0_wmod': 4.17}
    for name, (base, spread) in spreads.items():
        noise = np.random.default_rng([zlib.crc32(name.encode()), seed]).standard_normal(out[name].shape)
        drawn = base * np.exp(spread * noise) if base else spread * noise
        out[name] = jnp.asarray(drawn.astype(out[name].dtype))
    for name, factor in factors.items():
        out[name] = (out[name] * factor).astype(out[name].dtype)
    return out
```

```python
from contextlib import ExitStack, contextmanager

import numpy as np

import concourse.bass as bass
from concourse import mybir

ALU = mybir.AluOpType
ACT = mybir.ActivationFunctionType
AX = mybir.AxisListType
F32 = mybir.dt.float32
I32 = mybir.dt.int32
U32 = mybir.dt.uint32

P = 128
B, L, D = 4, 1024, 256
TB = L // P
TILES = B * TB
DC = D // P
NJ = 8
HEADS = D // NJ
TAPS = 512
HALF = TAPS
FREQS = 2 * HALF
JT = FREQS // P
JR = JT // 2
CT = HALF // P
OFFS = TAPS // P + 1
TOEP = OFFS * P
PAD = P + TAPS + P
E, F, TOPK = 8, 1024, 2
TOKENS = B * L
CAP = -(-TOKENS * TOPK * 5 // (4 * E))
SLOTS = E * CAP
FC = F // P
GROUP = 256
GT = GROUP // P
GROUPS = CAP // GROUP
BITS = 30
MODS = 6
SA, CA, GA, SB, CB, GB = range(MODS)
EPS = 1e-5
BANK = 512


def constants():
    t = np.arange(HALF)[:, None]
    m = np.arange(HALF)[None, :]
    angle = 2 * np.pi * ((2 * m + 1) * t % (4 * HALF)) / (4 * HALF)
    forward = np.concatenate([np.cos(angle), -np.sin(angle)], axis=1).astype(np.float32)
    p = np.arange(P)
    same = (p[:, None] // 16) == (p[None, :] // 16)
    token = (np.arange(B)[None, None, :] * L + np.arange(TB)[None, :, None] * P + p[:, None, None])
    return {
        "dft": forward,
        "idft": np.ascontiguousarray(forward.T),
        "ident": np.eye(P, dtype=np.float32),
        "sign": np.stack([1.0 - 2.0 * (p % 2), 2.0 * (p % 2) - 1.0], 1).astype(np.float32),
        "group_ones": same.astype(np.float32),
        "group_before": (same & (p[:, None] < p[None, :])).astype(np.float32),
        "bit_int": np.tile((1 << np.arange(BITS - 1, -1, -1)).astype(np.int32), (P, 1)),
        "bit_float": np.tile((2.0 ** np.arange(BITS - 1, -1, -1)).astype(np.float32), (P, 1)),
        "expert_id": np.tile(np.arange(E, dtype=np.float32), (P, 1)),
        "slot_base": ((p // 16) * CAP).astype(np.float32)[:, None],
        "trash_slot": (token.reshape(P, TILES) + SLOTS + 1).astype(np.float32),
    }


class Chain:

    def __init__(self, eng, sem):
        self.eng, self.sem, self.base, self.n = eng, sem, 0, 0

    def link(self, instruction):
        self.n += 1
        instruction.then_inc(self.sem, 1)
        self.eng.wait_ge(self.sem, self.base + self.n)

    @contextmanager
    def loop(self, times, per):
        start = self.base + self.n
        with self.eng.Fori(0, times) as i:
            self.base, self.n = i * per + start, 0
            yield i
            assert self.n == per, (self.n, per)
        self.base, self.n = start + times * per, 0


def adaln_block(nc, u, w_qkv, b_all, k_taps, kD, ssm, sD, w_out, Wr, W1, W2, cT, wmod, K, out):
    with ExitStack() as ctx:
        def sb(name, shape, dt=F32):
            return ctx.enter_context(nc.sbuf_tensor(name, shape, dt))

        def sem(name):
            return ctx.enter_context(nc.semaphore(name))

        qkv = sb("qkv", [P, TILES, 3 * D])
        arena = sb("arena", [P, 27648])
        ps = ctx.enter_context(nc.psum_tensor("ps", [P, 8, BANK], F32))

        def region(start, size):
            return arena[:, start:start + size]

        R1, R2, FT, IT, KK0, WQ0, WO0, MA0, BI0, T0 = (
            0, 4096, 8192, 12288, 16384, 18432, 19968, 20480, 22528, 23552)
        kkT = region(T0, 1024).rearrange("p (c e) -> p c e", c=CT)
        wmod_sb = region(IT, 3072).rearrange("p (c n) -> p c n", c=DC)
        ssm_pad = region(IT + 3072, PAD)
        mod_row = region(R2, MODS * D)
        clamp_a = region(R2 + 2304, D)
        clamp_b = region(R2 + 2560, D)
        kD_row = region(R2 + 2816, D)
        x_buf = [region(R1 + 2048 * i, 2048).rearrange("p (t d) -> p t d", t=TB) for i in range(2)]
        hT_buf = [region(R2 + 2048 * i, 2048).rearrange("p (c t) -> p c t", c=DC) for i in range(2)]
        wqkvT = region(WQ0, 1536).rearrange("p (c n) -> p c n", c=DC)
        woT = region(WO0, 512).rearrange("p (c n) -> p c n", c=DC)
        mod_a = region(MA0, 2048).rearrange("p (b m d) -> p b m d", b=B, m=2)
        bias = region(BI0, 1024)
        dft = region(FT, 4096).rearrange("p (c m) -> p c m", c=CT)
        idft = region(IT, 4096).rearrange("p (j t) -> p j t", j=JT)
        kk_spec = region(KK0, 2048).rearrange("p (j e) -> p j e", j=JT)
        spec = region(R1, 4096).rearrange("p (j h e) -> p j h e", j=JT, h=2)
        prod = region(R2, 4096).rearrange("p (j h e) -> p j h e", j=JT, h=2)
        tmp = [region(T0 + 2048 * i, 2048).rearrange("p (j h e) -> p j h e", j=JR, h=2) for i in range(2)]
        kv_buf = [region(R1 + 2048 * i, 2048).rearrange("p (t i j) -> p t i j", t=TILES, i=NJ) for i in range(2)]
        toep_raw = [region(WQ0 + TOEP * i, TOEP) for i in range(2)]
        toep = [region(KK0 + TOEP * i, TOEP) for i in range(2)]
        qy = [region(T0 + 512 * g, 512).rearrange("p (t i j) -> p t i j", t=2 * B, i=NJ) for g in range(4)]
        zero = region(FT, 2048)
        mod_d = region(R2, 4096).rearrange("p (b m d) -> p b m d", b=B, m=4)
        x_again = region(FT, 2048).rearrange("p (t d) -> p t d", t=TB)
        y_b = region(FT + 2048, 2048).rearrange("p (t d) -> p t d", t=TB)
        x2_b = region(IT, 2048).rearrange("p (t d) -> p t d", t=TB)
        h2_b = region(IT + 2048, 2048).rearrange("p (t d) -> p t d", t=TB)
        yT = region(R1, 2048).rearrange("p (c t) -> p c t", c=DC)
        h2T = region(R1 + 2048, 2048).rearrange("p (c t) -> p c t", c=DC)
        routing = region(MA0, 2048).rearrange("p (a t e) -> p a t e", a=8, t=TILES)
        logits, probs, top_v, top_f, first, second, routed, slot_t = (routing[:, a] for a in range(8))
        gate_l = region(T0, 256)
        is_gt = region(T0 + 256, 256)
        is_eq = region(T0 + 512, 256)
        scan = region(T0 + 768, 256)
        rank = region(T0 + 1024, 256)
        keep = region(T0 + 1280, 256)
        ones_l = region(T0 + 1536, 256)
        junk = region(T0 + 1792, 256)
        picked = region(T0 + 2048, 256).rearrange("p (t e) -> p t e", t=TILES)
        top_i = region(T0 + 2304, 256).bitcast(U32).rearrange("p (t e) -> p t e", t=TILES)
        gate_cols = region(T0 + 2816, 256).rearrange("p (r e b q) -> p r e b q", r=2, e=E, b=B)
        row_max, row_sum, slot_tmp, slot_0, slot_1 = (region(T0 + 2560 + TILES * i, TILES) for i in range(5))
        slot = [slot_0, slot_1]
        w1_sb = [region(FT + 4096 * i, 2048).rearrange("p (c f) -> p c f", c=DC) for i in range(2)]
        w2_sb = [region(FT + 4096 * i + 2048, 2048).rearrange("p (c n) -> p c n", c=FC) for i in range(2)]
        xe = [region(KK0 + 512 * i, 512).rearrange("p (t d) -> p t d", t=GT) for i in range(2)]
        xeT = [region(KK0 + 1024 + 512 * i, 512).rearrange("p (c t) -> p c t", c=DC) for i in range(2)]
        y_sb = [region(WQ0 + 512 * i, 512).rearrange("p (t d) -> p t d", t=GT) for i in range(2)]
        hidT = [region(T0 + 2048 * i, 2048).rearrange("p (f t) -> p f t", f=FC) for i in range(2)]
        o_buf = [region(FT + 2048 * i, 2048).rearrange("p (t d) -> p t d", t=TB) for i in range(2)]
        o_tmp = region(R1, 2048).rearrange("p (t d) -> p t d", t=TB)

        ident = sb("ident_sb", [P, P])
        group_ones = sb("group_ones_sb", [P, P])
        group_before = sb("group_before_sb", [P, P])
        sign = sb("sign_sb", [P, 2])
        eps = sb("eps", [P, 1])
        c_sb = sb("c_sb", [P, DC, B])
        c_exp = sb("c_exp", [P, DC, B])
        siluT = sb("siluT", [P, DC, B])
        stats = sb("stats", [P, TB, 6])
        mean_var = sb("mean_var", [P, TB, 2])
        std = sb("std", [P, TB])
        wr_sb = sb("wr_sb", [P, DC, E])
        sD_sb = sb("sD_sb", [HEADS, 1])
        bit_int = sb("bit_int_sb", [P, BITS], I32)
        bit_float = sb("bit_float_sb", [P, BITS])
        expert_id = sb("expert_id_sb", [P, E])
        slot_base = sb("slot_base_sb", [P, 1])
        trash_slot = sb("trash_slot_sb", [P, TILES])
        theta = sb("theta", [P, 1], I32)
        cand = sb("cand", [P, 1], I32)
        accepted = sb("accepted", [P, 1], I32)
        count = sb("count", [P, 1])
        need = sb("need", [P, 1])
        row_total = sb("row_total", [P, 1])
        before = sb("before", [P, 1])
        weight = [sb(f"weight{r}", [P, TILES]) for r in range(2)]
        to_slot = [sb(f"to_slot{r}", [P, TILES], U32) for r in range(2)]
        from_slot = [sb(f"from_slot{r}", [P, TILES], U32) for r in range(2)]

        mod_dram = nc.dram_tensor("mod_scratch", [B, MODS * D], F32)
        ssm_dram = nc.dram_tensor("ssm_scratch", [HEADS, PAD], F32)
        xe_dram = nc.dram_tensor("xe_scratch", [SLOTS + TOKENS, D], F32)
        ye_dram = nc.dram_tensor("ye_scratch", [SLOTS, D], F32)

        stage_done = [sem(f"stage{k}_done") for k in range(8)]
        chain_v, chain_s, chain_g = sem("vector_chain"), sem("scalar_chain"), sem("gpsimd_chain")
        consts_in, c_in, w_qkv_in, kk_in, kD_in, ssm_in, wmod_in, bias_in, dft_in, idft_in = (
            sem(n) for n in ("consts_in", "c_in", "w_qkv_in", "kk_in", "kD_in", "ssm_in", "wmod_in",
                             "bias_in", "dft_in", "idft_in"))
        eps_set, exp_c, siluT_ready, mod_psum, mod_ready, mod_out, mod_a_in = (
            sem(n) for n in ("eps_set", "exp_c", "siluT_ready", "mod_psum",
                             "mod_ready", "mod_out", "mod_a_in"))
        kkT_ready, kk_spec_psum, ssm_ready, ssm_out = (
            sem(n) for n in ("kkT_ready",
                             "kk_spec_psum", "ssm_ready", "ssm_out"))
        kk_spec_ready = sem("kk_spec_ready")
        x_in = [sem(f"x_in{i}") for i in range(2)]
        var_ready, std_ready, h_ready, hT_psum, hT_ready, qkv_psum, qkv_ready = (
            sem(n) for n in ("var_ready", "std_ready", "h_ready", "hT_psum", "hT_ready", "qkv_psum", "qkv_ready"))
        spec_psum, spec_ready, prod_ready, conv_psum, conv_ready = (
            sem(n) for n in ("spec_psum", "spec_ready", "prod_ready", "conv_psum", "conv_ready"))
        toep_in = [sem(f"toep_in{i}") for i in range(2)]
        toep_ready, kv_ready, mix_psum, mix_read, zero_set, xe_zeroed, mod_d_in = (
            sem(n) for n in ("toep_ready", "kv_ready", "mix_psum", "mix_read", "zero_set", "xe_zeroed", "mod_d_in"))
        x_again_in, y_b_ready, yT_psum, yT_ready, attn_psum, x2_ready, var2_ready, std2_ready = (
            sem(n) for n in ("x_again_in", "y_b_ready", "yT_psum", "yT_ready", "attn_psum", "x2_ready",
                             "var2_ready", "std2_ready"))
        h2_ready, h2_kept, h2T_psum, h2T_ready, logit_psum, logit_ready, x_used = (
            sem(n) for n in ("h2_ready", "h2_kept", "h2T_psum", "h2T_ready", "logit_psum", "logit_ready", "x_used"))
        centred, exp_done, gate_ready, gateT_psum, count_ready, count_psum, slots_ready, slotT_psum = (
            sem(n) for n in ("centred", "exp_done", "gate_ready", "gateT_psum", "count_ready",
                             "count_psum", "slots_ready", "slotT_psum"))
        rows_out = sem("rows_out")
        waited = sem("waited")
        w_in = [sem(f"w_in{i}") for i in range(2)]
        xe_in = [sem(f"xe_in{i}") for i in range(2)]
        xeT_psum, xeT_ready, hid_psum, hid_ready, ye_psum, ye_ready = (
            sem(n) for n in ("xeT_psum", "xeT_ready", "hid_psum", "hid_ready", "ye_psum", "ye_ready"))
        ye_out = [sem(f"ye_out{i}") for i in range(2)]
        rows_in, out_ready = sem("rows_in"), sem("out_ready")
        out_stored = [sem(f"out_stored{i}") for i in range(2)]

        tile_view = qkv[:, :, :].rearrange("p (t b) n -> p t b n", b=B)

        def rows_of(b, lo, hi):
            return tile_view[:, :, bass.ds(b, 1), lo:hi].rearrange("p t o n -> p t (o n)")

        def mod_of(table, b, m, shape):
            return table[:, bass.ds(b, 1), m, :].to_broadcast(shape)

        ALL = [P, TB, D]
        u_tiles = u.rearrange("b (t p) d -> b p t d", p=P)
        out_tiles = out.rearrange("b (t p) d -> b p t d", p=P)

        def stage_end(eng, k):
            eng.drain().then_inc(stage_done[k], 1)
            eng.wait_ge(stage_done[k], 5)

        def backwards(v):
            last = v[:, v.shape[1] - 1:v.shape[1]]
            return bass.AP(last.tensor, last.offset, [last.ap[0], [-1, v.shape[1]]])

        block = ctx.enter_context(nc.Block())

        def store(sp, ye_rows, pair, k):
            n = pair * (2 * GROUPS) + k
            sp.wait_ge(ye_ready, n + 1)
            sp.dma_start(ye_rows[bass.ds(n, 1)].rearrange("o p t d -> (o p) t d"), y_sb[k % 2]).then_inc(ye_out[k % 2], 16)

        @block.sync
        def _(sp):
            sp.dma_start(c_sb[:], cT.rearrange("(c p) b -> p c b", p=P)).then_inc(c_in, 16)
            sp.dma_start(wmod_sb, wmod.rearrange("(c p) n -> p c n", p=P)).then_inc(wmod_in, 16)
            for dst, name in ((ident, "ident"), (sign, "sign"), (group_ones, "group_ones"),
                              (group_before, "group_before"), (bit_int, "bit_int"),
                              (bit_float, "bit_float"), (expert_id, "expert_id"),
                              (slot_base, "slot_base"), (trash_slot, "trash_slot")):
                sp.dma_start(dst[:], K[name]).then_inc(consts_in, 16)
            sp.dma_start(kkT, k_taps.rearrange("(c p) e -> p c e", p=P)).then_inc(kk_in, 16)
            sp.dma_start(wqkvT, w_qkv.rearrange("(c p) n -> p c n", p=P)).then_inc(w_qkv_in, 16)
            sp.dma_start(woT, w_out.rearrange("(c p) n -> p c n", p=P)).then_inc(w_qkv_in, 16)
            sp.dma_start(dft, K["dft"].rearrange("(c p) m -> p c m", p=P)).then_inc(dft_in, 16)
            for b in range(2):
                sp.dma_start(x_buf[b], u_tiles[b]).then_inc(x_in[b], 16)
            sp.dma_start(bias, b_all.to_broadcast([P, 4 * D])).then_inc(bias_in, 16)
            sp.dma_start(wr_sb[:], Wr.rearrange("(c p) e -> p c e", p=P)).then_inc(consts_in, 16)
            sp.wait_ge(mod_ready, 1)
            sp.dma_start(mod_dram[:, :], mod_row[0:B, :]).then_inc(mod_out, 16)
            sp.wait_ge(mod_out, 16)
            for b in range(B):
                sp.dma_start(mod_a[:, b].rearrange("p m d -> p (m d)"),
                             mod_dram[b:b + 1, 0:2 * D].to_broadcast([P, 2 * D])).then_inc(mod_a_in, 16)
            sp.wait_ge(ssm_ready, 2)
            sp.dma_start(ssm_dram[:, :], ssm_pad[0:HEADS, :]).then_inc(ssm_out, 16)
            sp.wait_ge(ssm_out, 16)
            sp.wait_ge(mod_psum, 3)
            sp.dma_start(idft, K["idft"].rearrange("(j p) t -> p j t", p=P)).then_inc(idft_in, 16)
            for b in range(2, B):
                sp.wait_ge(hT_psum, 4 * (b - 1))
                sp.dma_start(x_buf[b % 2], u_tiles[b]).then_inc(x_in[b % 2], 16)
            stage_end(sp, 0)
            stage_end(sp, 1)

            for b in range(B):
                sp.dma_start(mod_d[:, b].rearrange("p m d -> p (m d)"),
                             mod_dram[b:b + 1, 2 * D:6 * D].to_broadcast([P, 4 * D])).then_inc(mod_d_in, 16)
            for h in range(HEADS):
                if h >= 2:
                    sp.wait_ge(toep_ready, h - 1)
                shifted = bass.AP(ssm_dram, h * PAD, [[1, P], [1, TOEP]])
                sp.dma_start(toep_raw[h % 2], shifted).then_inc(toep_in[h % 2], 16)
                if h == 1:
                    sp.wait_ge(zero_set, 1)
                if 1 <= h <= 10:
                    r = SLOTS // 10
                    sp.dma_start(xe_dram[(h - 1) * r:h * r, :].rearrange("(p n) d -> p (n d)", p=P),
                                 zero).then_inc(xe_zeroed, 16)
            sp.wait_ge(xe_zeroed, 160)
            stage_end(sp, 2)

            with sp.Fori(0, B) as b:
                sp.wait_ge(x_used, b + 1)
                sp.dma_start(x_again, u_tiles[bass.ds(b, 1)].rearrange("o p t d -> (o p) t d")).then_inc(x_again_in, 16)
            stage_end(sp, 3)
            stage_end(sp, 4)

            sp.wait_ge(rows_out, 16 * 2 * TILES)
            xe_rows = xe_dram[0:SLOTS, :].rearrange("(n t p) d -> n p t d", t=GT, p=P)
            ye_rows = ye_dram[:, :].rearrange("(n t p) d -> n p t d", t=GT, p=P)
            w1_rows = W1.rearrange("e (c p) f -> e p c f", p=P)
            w2_rows = W2.rearrange("e (c p) n -> e p c n", p=P)
            with sp.Fori(0, E // 2) as pair:
                for q in range(2):
                    e = pair * 2 + q
                    for g in range(GROUPS):
                        n = pair * (2 * GROUPS) + q * GROUPS + g
                        s = (q * GROUPS + g) % 2
                        if g == 0:
                            sp.wait_ge(ye_psum, e * GROUPS + GROUPS + 1)
                            sp.dma_start(w1_sb[q], w1_rows[bass.ds(e, 1)].rearrange("o p c f -> (o p) c f")).then_inc(w_in[q], 16)
                            sp.dma_start(w2_sb[q], w2_rows[bass.ds(e, 1)].rearrange("o p c n -> (o p) c n")).then_inc(w_in[q], 16)
                        sp.wait_ge(xeT_psum, n + 1)
                        sp.dma_start(xe[s], xe_rows[bass.ds(n, 1)].rearrange("o p t d -> (o p) t d")).then_inc(xe_in[s], 16)
                        if q * GROUPS + g >= 1:
                            store(sp, ye_rows, pair, q * GROUPS + g - 1)
                store(sp, ye_rows, pair, 2 * GROUPS - 1)
            for s in range(2):
                sp.wait_ge(ye_out[s], 16 * (E * GROUPS // 2 + 1))
            stage_end(sp, 5)

            with sp.Fori(0, B // 2) as bb:
                for s in range(2):
                    b = bb * 2 + s
                    sp.wait_ge(out_ready, b + 1)
                    sp.dma_start(out_tiles[bass.ds(b, 1)].rearrange("o p t d -> (o p) t d"), o_buf[s]).then_inc(out_stored[s], 16)
            for s in range(2):
                sp.wait_ge(out_stored[s], 16 * (B // 2 + 1))

        @block.gpsimd
        def _(pool):
            chain = Chain(pool, chain_g)
            chain.link(nc.gpsimd.memset(ssm_pad[0:HEADS, :], 0.0))
            pool.dma_start(ssm_pad[0:HEADS, P:P + TAPS], ssm).then_inc(ssm_in, 16)
            pool.dma_start(sD_sb[:], sD.rearrange("(h o) -> h o", o=1)).then_inc(ssm_in, 16)
            pool.dma_start(kD_row[0:1, :], kD.rearrange("(o d) -> o d", o=1)).then_inc(kD_in, 16)
            pool.wait_ge(ssm_in, 32)
            nc.gpsimd.tensor_tensor(ssm_pad[0:HEADS, TOEP - 1:TOEP], ssm_pad[0:HEADS, TOEP - 1:TOEP], sD_sb[:],
                                    ALU.add).then_inc(ssm_ready, 2)
            stage_end(pool, 0)
            stage_end(pool, 1)
            nc.gpsimd.memset(zero, 0.0).then_inc(zero_set, 1)
            stage_end(pool, 2)
            stage_end(pool, 3)
            stage_end(pool, 4)
            pool.wait_ge(xe_zeroed, 160)
            for r in range(2):
                for tile in range(TILES):
                    nc.gpsimd.indirect_dma_start(
                        xe_dram[:, :], bass.IndirectOffsetOnAxis(ap=to_slot[r][:, tile:tile + 1], axis=0),
                        qkv[:, tile, 2 * D:3 * D], None).then_inc(rows_out, 16)
            pool.wait_ge(rows_out, 16 * 2 * TILES)
            stage_end(pool, 5)
            for tile in range(TILES):
                for r in range(2):
                    nc.gpsimd.indirect_dma_start(
                        qkv[:, tile, 2 * D * r:2 * D * r + D], None, ye_dram[:, :],
                        bass.IndirectOffsetOnAxis(ap=from_slot[r][:, tile:tile + 1], axis=0)).then_inc(rows_in, 16)
            pool.wait_ge(rows_in, 16 * 2 * TILES)

        @block.scalar
        def _(act):
            def copy(dst, src):
                return nc.scalar.activation(dst, src, ACT.Copy)

            act.wait_ge(c_in, 16)
            nc.scalar.activation(c_exp[:], c_sb[:], ACT.Exp, scale=-1.0).then_inc(exp_c, 1)
            act.wait_ge(kk_spec_psum, 1)
            nc.scalar.activation(kk_spec.rearrange("p j e -> p (j e)"), ps[:, 0:4].rearrange("p a n -> p (a n)"),
                                 ACT.Copy, scale=1.0 / HALF).then_inc(kk_spec_ready, 1)
            act.wait_ge(eps_set, 1)
            with act.Fori(0, B // 2) as bb:
                for s in range(2):
                    b = bb * 2 + s
                    act.wait_ge(var_ready, b + 1)
                    nc.scalar.activation(std[:], mean_var[:, :, 1], ACT.Sqrt, bias=eps[:]).then_inc(std_ready, 1)
                    for g in range(4):
                        act.wait_ge(hT_psum, 4 * b + g + 1)
                        copy(hT_buf[s][:, g // 2, (g % 2) * BANK:(g % 2 + 1) * BANK], ps[:, g]).then_inc(hT_ready, 1)
            stage_end(act, 0)

            def spec_out(b):
                for j in range(JT):
                    act.wait_ge(spec_psum, JT * b + j + 1)
                    if j == 0:
                        act.wait_ge(prod_ready, b + 1)
                    copy(spec[:, j].rearrange("p h e -> p (h e)"), ps[:, j % 4]).then_inc(spec_ready, 1)

            def conv_out(b):
                for t in range(CT):
                    act.wait_ge(conv_psum, CT * b + t + 2)
                    halves = tile_view[:, t::CT, bass.ds(b, 1), D:2 * D].rearrange("p h o n -> p h (o n)")
                    copy(halves, ps[:, 4 + t].rearrange("p (h e) -> p h e", h=2)).then_inc(conv_ready, 1)

            spec_out(0)
            with act.Fori(0, B - 1) as b:
                spec_out(b + 1)
                conv_out(b)
            conv_out(B - 1)
            stage_end(act, 1)

            with act.Fori(0, HEADS // 2) as hh:
                for s in range(2):
                    h = hh * 2 + s
                    act.wait_ge(toep_in[s], 16 * hh + 16)
                    act.wait_ge(mix_psum, 4 * h + 1)
                    copy(toep[s], backwards(toep_raw[s])).then_inc(toep_ready, 1)
            stage_end(act, 2)

            with act.Fori(0, B) as b:
                act.wait_ge(yT_psum, 4 * b + 1)
                copy(y_b, rows_of(b, 0, D)).then_inc(y_b_ready, 1)
                for g in range(4):
                    act.wait_ge(yT_psum, 4 * b + g + 2)
                    copy(yT[:, g // 2, (g % 2) * BANK:(g % 2 + 1) * BANK], ps[:, 4 + g % 2]).then_inc(yT_ready, 1)
                act.wait_ge(var2_ready, b + 1)
                nc.scalar.activation(std[:], mean_var[:, :, 1], ACT.Sqrt, bias=eps[:]).then_inc(std2_ready, 1)
                act.wait_ge(h2_ready, b + 1)
                copy(rows_of(b, 2 * D, 3 * D), h2_b).then_inc(h2_kept, 1)
                for g in range(4):
                    act.wait_ge(h2T_psum, 4 * b + g + 1)
                    copy(h2T[:, g // 2, (g % 2) * BANK:(g % 2 + 1) * BANK], ps[:, 6]).then_inc(h2T_ready, 1)
            stage_end(act, 3)

            act.wait_ge(centred, 1)
            nc.scalar.activation(probs, logits, ACT.Exp).then_inc(exp_done, 1)
            stage_end(act, 4)

            with act.Fori(0, E // 2) as pair:
                for k in range(2 * GROUPS):
                    n = pair * (2 * GROUPS) + k
                    for a in range(4):
                        act.wait_ge(hid_psum, 4 * n + a + 1)
                        if a == 0:
                            act.wait_ge(ye_psum, n + 2 * GROUPS)
                        nc.scalar.activation(hidT[k % 2][:, 2 * a:2 * a + 2, :], ps[:, a].rearrange("p (f t) -> p f t", f=2),
                                             ACT.Relu).then_inc(hid_ready, 1)
            stage_end(act, 5)

        @block.vector
        def _(dve):
            chain = Chain(dve, chain_v)
            link = chain.link

            def tt(o, a, b_, op):
                return nc.vector.tensor_tensor(o, a, b_, op)

            def norm(x_tiles, h_tiles, var_sem, std_sem, b):
                for t in range(TB):
                    last = nc.vector.bn_stats(stats[:, t, :], x_tiles[:, t, :])
                link(last)
                dve.sem_inc(waited, 1)
                for t in range(TB):
                    last = nc.vector.bn_aggr(mean_var[:, t, :], stats[:, t, :])
                last.then_inc(var_sem, 1)
                dve.wait_ge(var_sem, b + 1)
                dve.wait_ge(std_sem, b + 1)
                link(nc.vector.reciprocal(std[:], std[:]))
                for t in range(TB):
                    last = nc.vector.tensor_scalar(h_tiles[:, t, :], x_tiles[:, t, :], mean_var[:, t, 0:1],
                                                   std[:, t:t + 1], ALU.subtract, ALU.mult)
                link(last)

            dve.sem_inc(prod_ready, 1)
            dve.sem_inc(conv_psum, 1)
            dve.sem_inc(mix_read, 8)
            dve.sem_inc(mix_psum, 5)
            dve.sem_inc(x_used, 1)
            dve.sem_inc(yT_psum, 1)
            dve.sem_inc(ye_psum, 2 * GROUPS + 1)
            dve.sem_inc(xeT_psum, 2)
            for s in range(2):
                dve.sem_inc(ye_out[s], 16)
                dve.sem_inc(out_stored[s], 16)
            nc.vector.memset(eps[:], EPS).then_inc(eps_set, 1)
            dve.wait_ge(exp_c, 1)
            link(nc.vector.tensor_scalar_add(c_exp[:], c_exp[:], 1.0))
            link(nc.vector.reciprocal(c_exp[:], c_exp[:]))
            tt(siluT[:], c_sb[:], c_exp[:], ALU.mult).then_inc(siluT_ready, 1)
            dve.wait_ge(kk_in, 16)
            dve.wait_ge(kD_in, 16)
            tt(kkT[0:1, 0, :], kkT[0:1, 0, :], kD_row[0:1, :], ALU.add).then_inc(kkT_ready, 1)
            dve.wait_ge(mod_psum, 3)
            link(nc.vector.tensor_copy(mod_row[0:B, :], ps[0:B, 5:8].rearrange("p a n -> p (a n)")))
            for m in (CA, CB):
                v = mod_row[0:B, m * D:(m + 1) * D]
                link(nc.vector.tensor_scalar_add(v, v, 1.0))
            for m in (GA, GB):
                v = mod_row[0:B, m * D:(m + 1) * D]
                link(nc.vector.tensor_scalar(clamp_b[0:B, :], v, -1.0, None, ALU.mult))
                link(tt(clamp_b[0:B, :], clamp_b[0:B, :], v, ALU.max))
                link(nc.vector.tensor_scalar_max(clamp_b[0:B, :], clamp_b[0:B, :], 0.25))
                link(nc.vector.tensor_scalar(clamp_a[0:B, :], v, 0.0, 2.0, ALU.is_ge, ALU.mult))
                link(nc.vector.tensor_scalar_add(clamp_a[0:B, :], clamp_a[0:B, :], -1.0))
                last = tt(v, clamp_a[0:B, :], clamp_b[0:B, :], ALU.mult)
                if m == GA:
                    link(last)
            last.then_inc(mod_ready, 1)

            def qkv_out(b):
                for t in range(TB):
                    dve.wait_ge(qkv_psum, TB * b + t + 1)
                    bank = 4 + 2 * (t % 2)
                    tt(tile_view[:, t, bass.ds(b, 1), :].rearrange("p o n -> p (o n)"),
                       ps[:, bank:bank + 2].rearrange("p a n -> p (a n)")[:, 0:3 * D], bias[:, 0:3 * D],
                       ALU.add).then_inc(qkv_ready, 1)

            dve.wait_ge(bias_in, 16)
            with chain.loop(B // 2, 2 * 4) as bb:
                for s in range(2):
                    b = bb * 2 + s
                    dve.wait_ge(x_in[s], bb * 16 + 16)
                    norm(x_buf[s], x_buf[s], var_ready, std_ready, b)
                    dve.wait_ge(mod_a_in, 16 * B)
                    link(tt(x_buf[s], x_buf[s], mod_of(mod_a, b, 1, ALL), ALU.mult))
                    tt(x_buf[s], x_buf[s], mod_of(mod_a, b, 0, ALL), ALU.add).then_inc(h_ready, 1)
                    qkv_out(b)
            stage_end(dve, 0)

            re, im = slice(0, JR), slice(JR, JT)
            PR = [P, JR, 2, D]
            with chain.loop(B, 4) as b:
                dve.wait_ge(spec_ready, JT * (b + 1))
                nc.vector.scalar_tensor_tensor(spec[:, re, 1], spec[:, im, 0], sign[:, 1:2], spec[:, re, 1], ALU.mult, ALU.add)
                link(nc.vector.scalar_tensor_tensor(spec[:, im, 1], spec[:, re, 0], sign[:, 0:1], spec[:, im, 1], ALU.mult, ALU.add))
                k_re = kk_spec[:, re].unsqueeze(2).to_broadcast(PR)
                k_im = kk_spec[:, im].unsqueeze(2).to_broadcast(PR)
                tt(tmp[0], k_re, spec[:, re], ALU.mult)
                link(tt(tmp[1], k_im, spec[:, im], ALU.mult))
                dve.wait_ge(conv_psum, CT * b + 1)
                link(tt(prod[:, re], tmp[0], tmp[1], ALU.subtract))
                tt(tmp[0], k_re, spec[:, im], ALU.mult)
                link(tt(tmp[1], k_im, spec[:, re], ALU.mult))
                tt(prod[:, im], tmp[0], tmp[1], ALU.add).then_inc(prod_ready, 1)
            stage_end(dve, 1)

            def products(h, s):
                for g in range(4):
                    tiles = slice(8 * g, 8 * g + 8)
                    k_i = qkv[:, tiles, bass.ds(h * NJ + D, NJ)].unsqueeze(3).to_broadcast([P, 8, NJ, NJ])
                    v_j = qkv[:, tiles, bass.ds(h * NJ + 2 * D, NJ)].unsqueeze(2).to_broadcast([P, 8, NJ, NJ])
                    tt(kv_buf[s][:, tiles], k_i, v_j, ALU.mult).then_inc(kv_ready, 1)

            def gate_and_sum(h, s):
                for g in range(4):
                    tiles = slice(8 * g, 8 * g + 8)
                    q_i = qkv[:, tiles, bass.ds(h * NJ, NJ)].unsqueeze(3).to_broadcast([P, 8, NJ, NJ])
                    dve.wait_ge(mix_psum, 4 * h + g + 6)
                    tt(qy[g], ps[:, 4 * s + g].rearrange("p (t i j) -> p t i j", t=8, i=NJ), q_i,
                       ALU.mult).then_inc(mix_read, 1)
                    dve.wait_ge(mix_read, 4 * h + g + 1 + 8)
                    dve.sem_inc(waited, 1)
                    nc.vector.tensor_reduce(qkv[:, tiles, bass.ds(h * NJ, NJ)],
                                            qy[g].rearrange("p t i j -> p t j i"), AX.X, ALU.add)

            products(0, 0)
            products(1, 1)
            with dve.Fori(0, HEADS // 2 - 1) as hh:
                for s in range(2):
                    gate_and_sum(hh * 2 + s, s)
                    products(hh * 2 + s + 2, s)
            for s in range(2):
                gate_and_sum(HEADS - 2 + s, s)
            stage_end(dve, 2)

            dve.wait_ge(mod_d_in, 16 * B)
            with chain.loop(B, 7) as b:
                dve.wait_ge(attn_psum, b + 1)
                att = ps[:, 0:4].rearrange("p a n -> p (a n)").rearrange("p (t d) -> p t d", t=TB)
                link(tt(x2_b, att, bias[:, 3 * D:4 * D].unsqueeze(1).to_broadcast(ALL), ALU.add))
                link(tt(x2_b, x2_b, mod_of(mod_d, b, 0, ALL), ALU.mult))
                dve.wait_ge(x_again_in, 16 * b + 16)
                tt(x2_b, x2_b, x_again, ALU.add).then_inc(x_used, 1)
                dve.wait_ge(x_used, b + 2)
                nc.vector.tensor_copy(rows_of(b, D, 2 * D), x2_b)
                norm(x2_b, h2_b, var2_ready, std2_ready, b)
                link(tt(h2_b, h2_b, mod_of(mod_d, b, 2, ALL), ALU.mult))
                tt(h2_b, h2_b, mod_of(mod_d, b, 1, ALL), ALU.add).then_inc(h2_ready, 1)
                dve.wait_ge(logit_psum, b + 1)
                dst = logits.rearrange("p (t b) e -> p t b e", b=B)[:, :, bass.ds(b, 1), :].rearrange("p t o e -> p t (o e)")
                link(nc.vector.tensor_copy(dst, ps[:, 7, 0:TB * E].rearrange("p (t e) -> p t e", t=TB)))
                dve.wait_ge(h2_kept, b + 1)
            stage_end(dve, 3)

            TE = [P, TILES, E]
            link(nc.vector.tensor_reduce(row_max, logits, AX.X, ALU.max))
            tt(logits, logits, row_max.unsqueeze(2).to_broadcast(TE), ALU.subtract).then_inc(centred, 1)
            dve.wait_ge(exp_done, 1)
            link(nc.vector.tensor_reduce(row_sum, probs, AX.X, ALU.add))
            link(nc.vector.reciprocal(row_sum, row_sum))
            link(tt(probs, probs, row_sum.unsqueeze(2).to_broadcast(TE), ALU.mult))
            for t in range(TILES):
                last = nc.vector.max(top_v[:, t, :], probs[:, t, :])
            link(last)
            for t in range(TILES):
                last = nc.vector.max_index(top_i[:, t, :], top_v[:, t, :], probs[:, t, :])
            link(last)
            link(nc.vector.tensor_copy(top_f, top_i))
            ids = expert_id[:].unsqueeze(1).to_broadcast(TE)
            tt(first, ids, top_f[:, :, 0:1].to_broadcast(TE), ALU.is_equal)
            link(tt(second, ids, top_f[:, :, 1:2].to_broadcast(TE), ALU.is_equal))
            link(tt(routed, first, second, ALU.add))
            link(tt(picked, probs, routed, ALU.mult))
            link(nc.vector.tensor_scalar_add(routed, routed, -1.0))
            def chunked(v, r):
                return v.rearrange("p (q r b) e -> p r q b e", r=2, b=B)[:, r]

            for r in range(2):
                last = tt(gate_cols[:, r].rearrange("p e b q -> p q b e"), chunked(picked, r), chunked(routed, r), ALU.add)
            last.then_inc(gate_ready, 1)
            dve.wait_ge(gateT_psum, 1)
            nc.vector.memset(theta[:], 0)
            nc.vector.memset(ones_l, 1.0)
            link(nc.vector.tensor_copy(gate_l, ps[:, 0, 0:256]))
            with chain.loop(BITS, 3) as i:
                link(tt(cand[:], theta[:], bit_int[:, bass.ds(i, 1)], ALU.bitwise_or))
                nc.vector.tensor_scalar(junk, gate_l, cand[:].bitcast(F32), None, ALU.is_ge, ALU.add,
                                        accum_out=count[:]).then_inc(count_ready, 1)
                dve.wait_ge(count_psum, i + 1)
                link(nc.vector.tensor_scalar(accepted[:], ps[:, 1, 0:1], float(CAP), bit_float[:, bass.ds(i, 1)],
                                             ALU.is_ge, ALU.mult))
                link(tt(theta[:], theta[:], accepted[:], ALU.bitwise_or))
            th = theta[:].bitcast(F32)
            nc.vector.tensor_scalar(is_gt, gate_l, th, None, ALU.is_gt, ALU.add,
                                    accum_out=count[:]).then_inc(count_ready, 1)
            link(nc.vector.tensor_scalar(is_eq, gate_l, th, None, ALU.is_equal, ALU.add, accum_out=row_total[:]))
            dve.wait_ge(count_psum, BITS + 1)
            link(nc.vector.tensor_scalar(need[:], ps[:, 1, 0:1], -1.0, float(CAP), ALU.mult, ALU.add))
            nc.vector.tensor_tensor_scan(scan, ones_l, is_eq, 0.0, ALU.mult, ALU.add).then_inc(count_ready, 1)
            dve.wait_ge(count_ready, BITS + 2)
            dve.wait_ge(count_psum, BITS + 2)
            link(nc.vector.tensor_copy(before[:], ps[:, 1, 0:1]))
            link(nc.vector.scalar_tensor_tensor(rank, scan, before[:], is_eq, ALU.add, ALU.subtract))
            link(nc.vector.scalar_tensor_tensor(rank, rank, need[:], is_eq, ALU.is_lt, ALU.mult))
            link(tt(keep, is_gt, rank, ALU.add))
            link(nc.vector.tensor_tensor_scan(scan, ones_l, keep, 0.0, ALU.mult, ALU.add))
            nc.vector.tensor_copy(row_total[:], scan[:, 255:256]).then_inc(count_ready, 1)
            dve.wait_ge(count_psum, BITS + 3)
            link(nc.vector.tensor_scalar(before[:], ps[:, 1, 0:1], slot_base[:], None, ALU.add))
            nc.vector.scalar_tensor_tensor(rank, scan, before[:], keep, ALU.add, ALU.mult).then_inc(slots_ready, 1)
            dve.wait_ge(slotT_psum, 1)
            for par in range(2):
                dst = slot_t.rearrange("p (q r b) e -> p q r b e", r=2, b=B)[:, :, par]
                src = ps[:, 2, par * P:(par + 1) * P].rearrange("p (e b q) -> p q b e", e=E, b=B)
                last = nc.vector.tensor_copy(dst, src)
            link(last)
            for r, mask in enumerate((first, second)):
                link(tt(picked, slot_t, mask, ALU.mult))
                link(nc.vector.tensor_reduce(slot[r], picked, AX.X, ALU.add))
                link(nc.vector.scalar_tensor_tensor(weight[r][:], slot[r], 0.5, top_v[:, :, r], ALU.is_ge, ALU.mult))
                link(nc.vector.tensor_scalar(from_slot[r][:], slot[r], -1.0, 0.0, ALU.add, ALU.max))
                link(nc.vector.scalar_tensor_tensor(slot_tmp, slot[r], 0.5, trash_slot[:], ALU.is_lt, ALU.mult))
                link(tt(slot_tmp, slot_tmp, slot[r], ALU.add))
                link(nc.vector.tensor_scalar_add(to_slot[r][:], slot_tmp, -1.0))
            stage_end(dve, 4)

            with dve.Fori(0, E // 2) as pair:
                for k in range(2 * GROUPS):
                    n = pair * (2 * GROUPS) + k
                    dve.wait_ge(xeT_psum, n + 3)
                    nc.vector.tensor_copy(xeT[k % 2].rearrange("p c t -> p (c t)"), ps[:, 6]).then_inc(xeT_ready, 1)
                    dve.wait_ge(ye_psum, n + 2 * GROUPS + 2)
                    dve.wait_ge(ye_out[k % 2], (pair * GROUPS + k // 2 + 1) * 16)
                    nc.vector.tensor_copy(y_sb[k % 2].rearrange("p t d -> p (t d)"), ps[:, 4 + k % 2]).then_inc(ye_ready, 1)
            stage_end(dve, 5)

            dve.wait_ge(rows_in, 16 * 2 * TILES)
            w_view = [w[:, :].rearrange("p (t b) -> p t b", b=B) for w in weight]
            with chain.loop(B // 2, 2 * 3) as bb:
                for s in range(2):
                    b = bb * 2 + s
                    dve.wait_ge(out_stored[s], bb * 16 + 16)
                    gates = [w[:, :, bass.ds(b, 1)].to_broadcast(ALL) for w in w_view]
                    tt(o_tmp, rows_of(b, 0, D), gates[0], ALU.mult)
                    link(tt(o_buf[s], rows_of(b, 2 * D, 3 * D), gates[1], ALU.mult))
                    link(tt(o_tmp, o_tmp, o_buf[s], ALU.add))
                    link(tt(o_tmp, o_tmp, mod_of(mod_d, b, 3, ALL), ALU.mult))
                    tt(o_buf[s], o_tmp, rows_of(b, D, 2 * D), ALU.add).then_inc(out_ready, 1)
                    dve.wait_ge(out_ready, b + 1)

        @block.tensor
        def _(pe):
            mm, transpose = nc.tensor.matmul, nc.tensor.transpose
            pe.wait_ge(consts_in, 160)
            pe.wait_ge(siluT_ready, 1)
            pe.wait_ge(wmod_in, 16)
            for a in range(3):
                for dc in range(DC):
                    last = mm(ps[0:B, 5 + a, :], siluT[:, dc, :], wmod_sb[:, dc, a * BANK:(a + 1) * BANK],
                              start=dc == 0, stop=dc == DC - 1)
                last.then_inc(mod_psum, 1)
            pe.wait_ge(dft_in, 16)
            pe.wait_ge(kkT_ready, 1)
            for j in range(JT):
                for sc in range(CT):
                    last = mm(ps[:, j // 2, (j % 2) * D:(j % 2 + 1) * D], dft[:, sc, j * P:(j + 1) * P], kkT[:, sc, :],
                              start=sc == 0, stop=sc == CT - 1)
            last.then_inc(kk_spec_psum, 1)
            pe.wait_ge(kk_spec_ready, 1)
            pe.wait_ge(mod_ready, 1)
            pe.wait_ge(w_qkv_in, 32)
            with pe.Fori(0, B // 2) as bb:
                for s in range(2):
                    b = bb * 2 + s
                    pe.wait_ge(h_ready, b + 1)
                    for g in range(4):
                        for t in range(4):
                            tb = (g % 2) * 4 + t
                            last = transpose(ps[:, g, t * P:(t + 1) * P],
                                             x_buf[s][:, tb, (g // 2) * P:(g // 2 + 1) * P], ident[:])
                        last.then_inc(hT_psum, 1)
                    pe.wait_ge(hT_ready, 4 * b + 4)
                    for tb in range(TB):
                        bank = 4 + 2 * (tb % 2)
                        if tb >= 2:
                            pe.wait_ge(qkv_ready, TB * b + tb - 1)
                        for lo, hi in ((0, 512), (512, 768)):
                            for dc in range(DC):
                                last = mm(ps[:, bank + lo // BANK, 0:hi - lo], hT_buf[s][:, dc, tb * P:(tb + 1) * P],
                                          wqkvT[:, dc, lo:hi], start=dc == 0, stop=dc == DC - 1)
                        last.then_inc(qkv_psum, 1)
                    pe.wait_ge(qkv_ready, TB * b + TB)
            stage_end(pe, 0)

            pe.wait_ge(idft_in, 16)

            def forward(b):
                for j in range(JT):
                    if j >= 4:
                        pe.wait_ge(spec_ready, JT * b + j - 3)
                    for t in range(CT):
                        halves = tile_view[:, t::CT, bass.ds(b, 1), D:2 * D].rearrange("p h o n -> p h (o n)")
                        last = mm(ps[:, j % 4].rearrange("p (h e) -> p h e", h=2), dft[:, t, j * P:(j + 1) * P], halves,
                                  start=t == 0, stop=t == CT - 1)
                    last.then_inc(spec_psum, 1)

            def inverse(b):
                pe.wait_ge(prod_ready, b + 2)
                for t in range(CT):
                    for j in range(JT):
                        last = mm(ps[:, 4 + t], idft[:, j, t * P:(t + 1) * P], prod[:, j].rearrange("p h e -> p (h e)"),
                                  start=j == 0, stop=j == JT - 1)
                    last.then_inc(conv_psum, 1)

            forward(0)
            with pe.Fori(0, B - 1) as b:
                pe.wait_ge(spec_ready, JT * b + JT)
                forward(b + 1)
                inverse(b)
                pe.wait_ge(conv_ready, CT * b + CT)
            inverse(B - 1)
            stage_end(pe, 1)

            with pe.Fori(0, HEADS // 2) as hh:
                for s in range(2):
                    h = hh * 2 + s
                    pe.wait_ge(toep_ready, h + 1)
                    for g in range(4):
                        pe.wait_ge(kv_ready, 4 * h + g + 1)
                        pe.wait_ge(mix_read, 4 * h + g + 1)
                        steps = []
                        for o in range(OFFS):
                            lo = max(2 * g, o)
                            if lo <= 2 * g + 1:
                                steps.append((o, lo))
                        for n, (o, lo) in enumerate(steps):
                            cnt = (2 * g + 2 - lo) * B
                            src = kv_buf[s][:, (lo - o) * B:(lo - o) * B + cnt].rearrange("p t i j -> p (t i j)")
                            last = mm(ps[:, 4 * s + g, (lo - 2 * g) * B * 64:BANK], toep[s][:, o * P:(o + 1) * P], src,
                                      start=n == 0, stop=n == len(steps) - 1)
                        last.then_inc(mix_psum, 1)
            stage_end(pe, 2)

            with pe.Fori(0, B) as b:
                pe.wait_ge(y_b_ready, b + 1)
                for g in range(4):
                    if g >= 2:
                        pe.wait_ge(yT_ready, 4 * b + g - 1)
                    for t in range(4):
                        tb = (g % 2) * 4 + t
                        last = transpose(ps[:, 4 + g % 2, t * P:(t + 1) * P],
                                         y_b[:, tb, (g // 2) * P:(g // 2 + 1) * P], ident[:])
                    last.then_inc(yT_psum, 1)
                pe.wait_ge(yT_ready, 4 * b + 4)
                for tb in range(TB):
                    for cc in range(DC):
                        last = mm(ps[:, tb // 2, (tb % 2) * D:(tb % 2 + 1) * D], yT[:, cc, tb * P:(tb + 1) * P], woT[:, cc, :],
                                  start=cc == 0, stop=cc == DC - 1)
                last.then_inc(attn_psum, 1)
                pe.wait_ge(h2_ready, b + 1)
                for g in range(4):
                    if g >= 1:
                        pe.wait_ge(h2T_ready, 4 * b + g)
                    for t in range(4):
                        tb = (g % 2) * 4 + t
                        last = transpose(ps[:, 6, t * P:(t + 1) * P],
                                         h2_b[:, tb, (g // 2) * P:(g // 2 + 1) * P], ident[:])
                    last.then_inc(h2T_psum, 1)
                pe.wait_ge(h2T_ready, 4 * b + 4)
                for tb in range(TB):
                    for cc in range(DC):
                        last = mm(ps[:, 7, tb * E:(tb + 1) * E], h2T[:, cc, tb * P:(tb + 1) * P], wr_sb[:, cc, :],
                                  start=cc == 0, stop=cc == DC - 1)
                last.then_inc(logit_psum, 1)
            stage_end(pe, 3)

            pe.wait_ge(gate_ready, 1)
            for par in range(2):
                cols = gate_cols[:, par].rearrange("p e b q -> p (e b q)")
                last = transpose(ps[:, 0, par * P:(par + 1) * P], cols, ident[:])
            last.then_inc(gateT_psum, 1)
            with pe.Fori(0, BITS) as i:
                pe.wait_ge(count_ready, i + 1)
                mm(ps[:, 1, 0:1], group_ones[:], count[:], start=True, stop=True).then_inc(count_psum, 1)
            pe.wait_ge(count_ready, BITS + 1)
            mm(ps[:, 1, 0:1], group_ones[:], count[:], start=True, stop=True).then_inc(count_psum, 1)
            for n in (2, 3):
                pe.wait_ge(count_ready, BITS + n)
                mm(ps[:, 1, 0:1], group_before[:], row_total[:], start=True, stop=True).then_inc(count_psum, 1)
            pe.wait_ge(slots_ready, 1)
            for par in range(2):
                last = transpose(ps[:, 2, par * P:(par + 1) * P], rank[:, par * P:(par + 1) * P], ident[:])
            last.then_inc(slotT_psum, 1)
            stage_end(pe, 4)

            with pe.Fori(0, E // 2) as pair:
                for k in range(2 * GROUPS):
                    q, g, s = k // GROUPS, k % GROUPS, k % 2
                    n = pair * (2 * GROUPS) + k
                    pe.wait_ge(xe_in[s], (pair * GROUPS + k // 2) * 16 + 16)
                    for dc in range(DC):
                        for t in range(GT):
                            last = transpose(ps[:, 6, dc * GROUP + t * P:dc * GROUP + (t + 1) * P],
                                             xe[s][:, t, dc * P:(dc + 1) * P], ident[:])
                    last.then_inc(xeT_psum, 1)
                    if g == 0:
                        pe.wait_ge(w_in[q], 32 * pair + 32)
                    pe.wait_ge(xeT_ready, n + 1)
                    for f in range(FC):
                        for dc in range(DC):
                            last = mm(ps[:, f // 2, (f % 2) * GROUP:(f % 2 + 1) * GROUP],
                                      w1_sb[q][:, dc, f * P:(f + 1) * P], xeT[s][:, dc, :],
                                      start=dc == 0, stop=dc == DC - 1)
                        if f % 2:
                            last.then_inc(hid_psum, 1)
                    for t in range(GT):
                        for f in range(FC):
                            if t == 0 and f % 2 == 0:
                                pe.wait_ge(hid_ready, 4 * n + f // 2 + 1)
                            last = mm(ps[:, 4 + s, t * D:(t + 1) * D], hidT[s][:, f, t * P:(t + 1) * P], w2_sb[q][:, f, :],
                                      start=f == 0, stop=f == FC - 1)
                    last.then_inc(ye_psum, 1)
            stage_end(pe, 5)


def kernel(**inputs):
    import concourse.bacc as bacc
    from concourse.bass_utils import run_bass_kernel_spmd

    nc = bacc.Bacc("TRN2", target_bir_lowering=False, num_devices=1)
    arrays, args, tables = {}, [], {}
    given = {name: np.asarray(a) for name, a in inputs.items()}
    attn = {name[8:]: a for name, a in given.items() if name.startswith("L0_attn_")}
    wo = attn["Wo"].reshape(D, NJ, HEADS).transpose(2, 1, 0).reshape(D, D)
    laid_out = {
        "u": attn["u"],
        "w_qkv": np.concatenate([attn["Wq"].T, attn["Wk"].T, attn["Wv"].T], axis=1),
        "b_all": np.concatenate([attn["bq"], attn["bk"], attn["bv"], attn["bo"]])[None, :],
        "k_taps": attn["ssm_k_kernel"].T,
        "k_skip": attn["ssm_k_D"],
        "ssm_kernel": attn["ssm_kernel"][:, ::-1],
        "ssm_skip": attn["D"],
        "w_out": wo,
        "w_router": given["L0_ffn_Wr"],
        "w1": given["L0_ffn_W1"],
        "w2": given["L0_ffn_W2"],
        "cT": given["L0_c"].T,
        "wmod": given["L0_wmod"],
    }
    for name, a in laid_out.items():
        a = np.ascontiguousarray(a)
        arrays[f"in_{name}"] = a
        args.append(nc.dram_tensor(f"in_{name}", a.shape, mybir.dt.from_np(a.dtype), kind="ExternalInput").ap())
    for name, a in constants().items():
        arrays[f"const_{name}"] = a
        tables[name] = nc.dram_tensor(f"const_{name}", a.shape, mybir.dt.from_np(a.dtype), kind="ExternalInput").ap()
    out = nc.dram_tensor("out", [B, L, D], F32, kind="ExternalOutput").ap()
    adaln_block(nc, *args, tables, out)
    r = run_bass_kernel_spmd(nc, [arrays], core_ids=[0])
    return r.results[0]["out"]
```

```python
from contextlib import ExitStack, contextmanager

import numpy as np

import concourse.bass as bass
from concourse import mybir

ALU = mybir.AluOpType
ACT = mybir.ActivationFunctionType
AX = mybir.AxisListType
F32 = mybir.dt.float32
I32 = mybir.dt.int32
U32 = mybir.dt.uint32
F32R = mybir.dt.float32r

P = 128
B, L, D = 4, 1024, 256
TB = L // P
TILES = B * TB
DC = D // P
NJ = 8
HEADS = D // NJ
TAPS = 512
HALF = TAPS
FREQS = 2 * HALF
JT = FREQS // P
JR = JT // 2
CT = HALF // P
OFFS = TAPS // P + 1
TOEP = OFFS * P
PAD = P + TAPS + P
E, F, TOPK = 8, 1024, 2
TOKENS = B * L
CAP = -(-TOKENS * TOPK * 5 // (4 * E))
SLOTS = E * CAP
FC = F // P
GROUP = 256
GT = GROUP // P
GROUPS = CAP // GROUP
PAIR = 2 * GROUPS
PIECE = 512
PIECES = 2 * DC * F // PIECE
PASSES = ((0, 0), (0, 1), (1, 0))
BITS = 30
MODS = 6
SA, CA, GA, SB, CB, GB = range(MODS)
EPS = 1e-5
BANK = 512
ARENA = 27648


def constants():
    t = np.arange(HALF)[:, None]
    m = np.arange(HALF)[None, :]
    angle = 2 * np.pi * ((2 * m + 1) * t % (4 * HALF)) / (4 * HALF)
    forward = np.concatenate([np.cos(angle), -np.sin(angle)], axis=1).astype(np.float32)
    p = np.arange(P)
    same = (p[:, None] // 16) == (p[None, :] // 16)
    token = (np.arange(B)[None, None, :] * L + np.arange(TB)[None, :, None] * P + p[:, None, None])
    return {
        "dft": forward,
        "idft": np.ascontiguousarray(forward.T),
        "ident": np.eye(P, dtype=np.float32),
        "sign": np.stack([1.0 - 2.0 * (p % 2), 2.0 * (p % 2) - 1.0], 1).astype(np.float32),
        "group_ones": same.astype(np.float32),
        "group_before": (same & (p[:, None] < p[None, :])).astype(np.float32),
        "bit_int": np.tile((1 << np.arange(BITS - 1, -1, -1)).astype(np.int32), (P, 1)),
        "bit_float": np.tile((2.0 ** np.arange(BITS - 1, -1, -1)).astype(np.float32), (P, 1)),
        "expert_id": np.tile(np.arange(E, dtype=np.float32), (P, 1)),
        "slot_base": ((p // 16) * CAP).astype(np.float32)[:, None],
        "trash_slot": (token.reshape(P, TILES) + SLOTS + 1).astype(np.float32),
    }


class Chain:

    def __init__(self, eng, sem):
        self.eng, self.sem, self.base, self.n = eng, sem, 0, 0

    def link(self, instruction):
        self.n += 1
        instruction.then_inc(self.sem, 1)
        self.eng.wait_ge(self.sem, self.base + self.n)

    @contextmanager
    def loop(self, times, per):
        start = self.base + self.n
        with self.eng.Fori(0, times) as i:
            self.base, self.n = i * per + start, 0
            yield i
            assert self.n == per, (self.n, per)
        self.base, self.n = start + times * per, 0


def adaln_block(nc, u, w_qkv, b_all, k_taps, kD, ssm, sD, w_out, Wr, W1, W2, cT, wmod, K, out):
    with ExitStack() as ctx:
        def sb(name, shape, dt=F32):
            return ctx.enter_context(nc.sbuf_tensor(name, shape, dt))

        def sem(name):
            return ctx.enter_context(nc.semaphore(name))

        qkv = sb("qkv", [P, TILES, 3 * D])
        arena = sb("arena", [P, ARENA])
        arena_at = nc.sbuf_base - 4 * ARENA
        ps = ctx.enter_context(nc.psum_tensor("ps", [P, 8, BANK], F32))

        def parts(name, start, shape):
            size = int(np.prod(shape[1:]))
            return [nc.alloc_sbuf_tensor_at(f"{name}_{part}", shape, F32R, offset=arena_at + 4 * (start + size * i))
                    for i, part in enumerate(("high", "low"))]

        def region(start, size):
            return arena[:, start:start + size]

        R1, R2, FT, IT, KK0, WQ0, WO0, MA0, BI0, T0 = (
            0, 4096, 8192, 12288, 16384, 18432, 19968, 20480, 22528, 23552)
        kkT = region(T0, 1024).rearrange("p (c e) -> p c e", c=CT)
        wmod_sb = region(IT, 3072).rearrange("p (c n) -> p c n", c=DC)
        ssm_pad = region(IT + 3072, PAD)
        mod_row = region(R2, MODS * D)
        clamp_a = region(R2 + 2304, D)
        clamp_b = region(R2 + 2560, D)
        kD_row = region(R2 + 2816, D)
        x_buf = [region(R1 + 2048 * i, 2048).rearrange("p (t d) -> p t d", t=TB) for i in range(2)]
        hT_buf = [region(R2 + 2048 * i, 2048).rearrange("p (c t) -> p c t", c=DC) for i in range(2)]
        wqkvT = region(WQ0, 1536).rearrange("p (c n) -> p c n", c=DC)
        woT = region(WO0, 512).rearrange("p (c n) -> p c n", c=DC)
        mod_a = region(MA0, 2048).rearrange("p (b m d) -> p b m d", b=B, m=2)
        bias = region(BI0, 1024)
        dft = region(FT, 4096).rearrange("p (c m) -> p c m", c=CT)
        idft = region(IT, 4096).rearrange("p (j t) -> p j t", j=JT)
        kk_spec = region(KK0, 2048).rearrange("p (j e) -> p j e", j=JT)
        spec = region(R1, 4096).rearrange("p (j h e) -> p j h e", j=JT, h=2)
        prod = region(R2, 4096).rearrange("p (j h e) -> p j h e", j=JT, h=2)
        tmp = [region(T0 + 2048 * i, 2048).rearrange("p (j h e) -> p j h e", j=JR, h=2) for i in range(2)]
        kv_buf = [region(R1 + 2048 * i, 2048).rearrange("p (t i j) -> p t i j", t=TILES, i=NJ) for i in range(2)]
        kv_parts = [parts(f"kv{i}", FT + 4096 * i, [P, 2048]) for i in range(2)]
        toep_raw = [region(WQ0 + TOEP * i, TOEP) for i in range(2)]
        toep_parts = [parts(f"toep{i}", start, [P, TOEP]) for i, start in enumerate((KK0, MA0))]
        qy = [region(T0 + 512 * g, 512).rearrange("p (t i j) -> p t i j", t=2 * B, i=NJ) for g in range(4)]
        zero = region(T0 + 2048, 2048)
        mod_d = region(R2, 4096).rearrange("p (b m d) -> p b m d", b=B, m=4)
        x_again = region(FT, 2048).rearrange("p (t d) -> p t d", t=TB)
        y_b = region(FT + 2048, 2048).rearrange("p (t d) -> p t d", t=TB)
        x2_b = region(IT, 2048).rearrange("p (t d) -> p t d", t=TB)
        h2_b = region(IT + 2048, 2048).rearrange("p (t d) -> p t d", t=TB)
        yT = region(R1, 2048).rearrange("p (c t) -> p c t", c=DC)
        h2T = region(R1 + 2048, 2048).rearrange("p (c t) -> p c t", c=DC)
        routing = region(MA0, 2048).rearrange("p (a t e) -> p a t e", a=8, t=TILES)
        logits, probs, top_v, top_f, first, second, routed, slot_t = (routing[:, a] for a in range(8))
        gate_l = region(T0, 256)
        is_gt = region(T0 + 256, 256)
        is_eq = region(T0 + 512, 256)
        scan = region(T0 + 768, 256)
        rank = region(T0 + 1024, 256)
        keep = region(T0 + 1280, 256)
        ones_l = region(T0 + 1536, 256)
        junk = region(T0 + 1792, 256)
        picked = region(T0 + 2048, 256).rearrange("p (t e) -> p t e", t=TILES)
        top_i = region(T0 + 2304, 256).bitcast(U32).rearrange("p (t e) -> p t e", t=TILES)
        gate_cols = region(T0 + 2816, 256).rearrange("p (r e b q) -> p r e b q", r=2, e=E, b=B)
        row_max, row_sum, slot_tmp, slot_0, slot_1 = (region(T0 + 2560 + TILES * i, TILES) for i in range(5))
        slot = [slot_0, slot_1]
        w_raw = [qkv[:, 16 * i:16 * i + 16, 0:D] for i in range(2)]
        w1_parts = [parts(f"w1_{i}", start, [P, DC * F]) for i, start in enumerate((R1, IT))]
        w2_parts = [parts(f"w2_{i}", start, [P, FC * D]) for i, start in enumerate((FT, KK0))]
        hid_parts = parts("hidden", 20480, [P, FC * GROUP])
        xeT_parts = parts("xeT", 24576, [P, DC * GROUP])
        xe = [region(25600 + 512 * i, 512).rearrange("p (t d) -> p t d", t=GT) for i in range(2)]
        y_sb = [region(26624 + 512 * i, 512).rearrange("p (t d) -> p t d", t=GT) for i in range(2)]
        o_buf = [region(FT + 2048 * i, 2048).rearrange("p (t d) -> p t d", t=TB) for i in range(2)]

        ident = sb("ident_sb", [P, P])
        group_ones = sb("group_ones_sb", [P, P])
        group_before = sb("group_before_sb", [P, P])
        sign = sb("sign_sb", [P, 2])
        eps = sb("eps", [P, 1])
        c_sb = sb("c_sb", [P, DC, B])
        c_exp = sb("c_exp", [P, DC, B])
        siluT = sb("siluT", [P, DC, B])
        stats = sb("stats", [P, TB, 6])
        mean_var = sb("mean_var", [P, TB, 2])
        std = sb("std", [P, TB])
        wr_sb = sb("wr_sb", [P, DC, E])
        sD_sb = sb("sD_sb", [HEADS, 1])
        bit_int = sb("bit_int_sb", [P, BITS], I32)
        bit_float = sb("bit_float_sb", [P, BITS])
        expert_id = sb("expert_id_sb", [P, E])
        slot_base = sb("slot_base_sb", [P, 1])
        trash_slot = sb("trash_slot_sb", [P, TILES])
        theta = sb("theta", [P, 1], I32)
        cand = sb("cand", [P, 1], I32)
        accepted = sb("accepted", [P, 1], I32)
        count = sb("count", [P, 1])
        need = sb("need", [P, 1])
        row_total = sb("row_total", [P, 1])
        before = sb("before", [P, 1])
        weight = [sb(f"weight{r}", [P, TILES]) for r in range(2)]
        to_slot = [sb(f"to_slot{r}", [P, TILES], U32) for r in range(2)]
        from_slot = [sb(f"from_slot{r}", [P, TILES], U32) for r in range(2)]

        mod_dram = nc.dram_tensor("mod_scratch", [B, MODS * D], F32)
        ssm_dram = nc.dram_tensor("ssm_scratch", [HEADS, PAD], F32)
        xe_dram = nc.dram_tensor("xe_scratch", [SLOTS + TOKENS, D], F32)
        ye_dram = nc.dram_tensor("ye_scratch", [SLOTS, D], F32)

        stage_done = [sem(f"stage{k}_done") for k in range(8)]
        chain_v, chain_s, chain_g = sem("vector_chain"), sem("scalar_chain"), sem("gpsimd_chain")
        consts_in, c_in, w_qkv_in, kk_in, kD_in, ssm_in, wmod_in, bias_in, dft_in, idft_in = (
            sem(n) for n in ("consts_in", "c_in", "w_qkv_in", "kk_in", "kD_in", "ssm_in", "wmod_in",
                             "bias_in", "dft_in", "idft_in"))
        eps_set, exp_c, siluT_ready, mod_psum, mod_ready, mod_out, mod_a_in = (
            sem(n) for n in ("eps_set", "exp_c", "siluT_ready", "mod_psum",
                             "mod_ready", "mod_out", "mod_a_in"))
        kkT_ready, kk_spec_psum, ssm_ready, ssm_out = (
            sem(n) for n in ("kkT_ready",
                             "kk_spec_psum", "ssm_ready", "ssm_out"))
        kk_spec_ready = sem("kk_spec_ready")
        x_in = [sem(f"x_in{i}") for i in range(2)]
        var_ready, std_ready, h_ready, hT_psum, hT_ready, qkv_psum, qkv_ready = (
            sem(n) for n in ("var_ready", "std_ready", "h_ready", "hT_psum", "hT_ready", "qkv_psum", "qkv_ready"))
        spec_psum, spec_ready, prod_ready, conv_psum, conv_ready = (
            sem(n) for n in ("spec_psum", "spec_ready", "prod_ready", "conv_psum", "conv_ready"))
        toep_in = [sem(f"toep_in{i}") for i in range(2)]
        toep_high, toep_low, kv_ready, kv_high, kv_low, mix_psum, mix_read, zero_set, xe_zeroed, mod_d_in = (
            sem(n) for n in ("toep_high", "toep_low", "kv_ready", "kv_high", "kv_low", "mix_psum", "mix_read", "zero_set", "xe_zeroed", "mod_d_in"))
        x_again_in, y_b_ready, yT_psum, yT_ready, attn_psum, x2_ready, var2_ready, std2_ready = (
            sem(n) for n in ("x_again_in", "y_b_ready", "yT_psum", "yT_ready", "attn_psum", "x2_ready",
                             "var2_ready", "std2_ready"))
        h2_ready, h2_kept, h2T_psum, h2T_ready, logit_psum, logit_ready, x_used = (
            sem(n) for n in ("h2_ready", "h2_kept", "h2T_psum", "h2T_ready", "logit_psum", "logit_ready", "x_used"))
        centred, exp_done, gate_ready, gateT_psum, count_ready, count_psum, slots_ready, slotT_psum = (
            sem(n) for n in ("centred", "exp_done", "gate_ready", "gateT_psum", "count_ready",
                             "count_psum", "slots_ready", "slotT_psum"))
        rows_out = [sem(f"rows_out{r}") for r in range(2)]
        w_high, w_low, xeT_high, xeT_low, hid_high, hid_low = (
            sem(n) for n in ("w_high", "w_low", "xeT_high", "xeT_low", "hid_high", "hid_low"))
        waited = sem("waited")
        w_in = [sem(f"w_in{i}") for i in range(2)]
        xe_in = [sem(f"xe_in{i}") for i in range(2)]
        xeT_psum, hid_psum, ye_psum, ye_ready = (sem(n) for n in ("xeT_psum", "hid_psum", "ye_psum", "ye_ready"))
        ye_out = [sem(f"ye_out{i}") for i in range(2)]
        rows_in = [[sem(f"rows_in{r}_{b}") for b in range(B)] for r in range(2)]
        weighted, out_ready = [sem(f"weighted{r}") for r in range(2)], sem("out_ready")
        out_stored = [sem(f"out_stored{i}") for i in range(2)]

        tile_view = qkv[:, :, :].rearrange("p (t b) n -> p t b n", b=B)

        def rows_of(b, lo, hi):
            return tile_view[:, :, bass.ds(b, 1), lo:hi].rearrange("p t o n -> p t (o n)")

        def mod_of(table, b, m, shape):
            return table[:, bass.ds(b, 1), m, :].to_broadcast(shape)

        ALL = [P, TB, D]
        u_tiles = u.rearrange("b (t p) d -> b p t d", p=P)
        out_tiles = out.rearrange("b (t p) d -> b p t d", p=P)

        def stage_end(eng, k):
            eng.drain().then_inc(stage_done[k], 1)
            eng.wait_ge(stage_done[k], 5)

        def backwards(v):
            last = v[:, v.shape[1] - 1:v.shape[1]]
            return bass.AP(last.tensor, last.offset, [last.ap[0], [-1, v.shape[1]]])

        kv_flat = [region(R1 + 2048 * i, 2048) for i in range(2)]

        def w_piece(q, part, piece):
            table = (w1_parts if piece < PIECES // 2 else w2_parts)[q][part]
            start = PIECE * (piece % (PIECES // 2))
            return table[:, start:start + PIECE].rearrange("p (s f) -> p s f", f=D)

        def raw_piece(q, piece):
            return w_raw[q][:, 2 * piece:2 * piece + 2]

        block = ctx.enter_context(nc.Block())

        @block.sync
        def _(sp):
            sp.dma_start(c_sb[:], cT.rearrange("(c p) b -> p c b", p=P)).then_inc(c_in, 16)
            sp.dma_start(wmod_sb, wmod.rearrange("(c p) n -> p c n", p=P)).then_inc(wmod_in, 16)
            for dst, name in ((ident, "ident"), (sign, "sign"), (group_ones, "group_ones"),
                              (group_before, "group_before"), (bit_int, "bit_int"),
                              (bit_float, "bit_float"), (expert_id, "expert_id"),
                              (slot_base, "slot_base"), (trash_slot, "trash_slot")):
                sp.dma_start(dst[:], K[name]).then_inc(consts_in, 16)
            sp.dma_start(kkT, k_taps.rearrange("(c p) e -> p c e", p=P)).then_inc(kk_in, 16)
            sp.dma_start(wqkvT, w_qkv.rearrange("(c p) n -> p c n", p=P)).then_inc(w_qkv_in, 16)
            sp.dma_start(woT, w_out.rearrange("(c p) n -> p c n", p=P)).then_inc(w_qkv_in, 16)
            sp.dma_start(dft, K["dft"].rearrange("(c p) m -> p c m", p=P)).then_inc(dft_in, 16)
            for b in range(2):
                sp.dma_start(x_buf[b], u_tiles[b]).then_inc(x_in[b], 16)
            sp.dma_start(bias, b_all.to_broadcast([P, 4 * D])).then_inc(bias_in, 16)
            sp.dma_start(wr_sb[:], Wr.rearrange("(c p) e -> p c e", p=P)).then_inc(consts_in, 16)
            sp.wait_ge(mod_ready, 1)
            sp.dma_start(mod_dram[:, :], mod_row[0:B, :]).then_inc(mod_out, 16)
            sp.wait_ge(mod_out, 16)
            for b in range(B):
                sp.dma_start(mod_a[:, b].rearrange("p m d -> p (m d)"),
                             mod_dram[b:b + 1, 0:2 * D].to_broadcast([P, 2 * D])).then_inc(mod_a_in, 16)
            sp.wait_ge(ssm_ready, 2)
            sp.dma_start(ssm_dram[:, :], ssm_pad[0:HEADS, :]).then_inc(ssm_out, 16)
            sp.wait_ge(ssm_out, 16)
            sp.wait_ge(mod_psum, 3)
            sp.dma_start(idft, K["idft"].rearrange("(j p) t -> p j t", p=P)).then_inc(idft_in, 16)
            for b in range(2, B):
                sp.wait_ge(hT_psum, 4 * (b - 1))
                sp.dma_start(x_buf[b % 2], u_tiles[b]).then_inc(x_in[b % 2], 16)
            stage_end(sp, 0)
            stage_end(sp, 1)

            for b in range(B):
                sp.dma_start(mod_d[:, b].rearrange("p m d -> p (m d)"),
                             mod_dram[b:b + 1, 2 * D:6 * D].to_broadcast([P, 4 * D])).then_inc(mod_d_in, 16)
            for h in range(HEADS):
                if h >= 2:
                    sp.wait_ge(toep_low, h - 1)
                shifted = bass.AP(ssm_dram, h * PAD, [[1, P], [1, TOEP]])
                sp.dma_start(toep_raw[h % 2], shifted).then_inc(toep_in[h % 2], 16)
                if h == 1:
                    sp.wait_ge(zero_set, 1)
                if 1 <= h <= 10:
                    r = SLOTS // 10
                    sp.dma_start(xe_dram[(h - 1) * r:h * r, :].rearrange("(p n) d -> p (n d)", p=P),
                                 zero).then_inc(xe_zeroed, 16)
            sp.wait_ge(xe_zeroed, 160)
            stage_end(sp, 2)

            with sp.Fori(0, B) as b:
                sp.wait_ge(x_used, b + 1)
                sp.dma_start(x_again, u_tiles[bass.ds(b, 1)].rearrange("o p t d -> (o p) t d")).then_inc(x_again_in, 16)
            stage_end(sp, 3)
            xe_rows = xe_dram[0:SLOTS, :].rearrange("(n t p) d -> n p t d", t=GT, p=P)
            ye_rows = ye_dram[:, :].rearrange("(n t p) d -> n p t d", t=GT, p=P)
            w1_rows = W1.rearrange("e (c p) (s f) -> e p c s f", p=P, f=D)
            w2_rows = W2.rearrange("e (c p) n -> e p c n", p=P)

            def load_weights(e, q):
                for c in range(DC):
                    sp.dma_start(w_raw[q][:, 4 * c:4 * c + 4],
                                 w1_rows[bass.ds(e, 1), :, c].rearrange("o p s f -> (o p) s f")).then_inc(w_in[q], 16)
                sp.dma_start(w_raw[q][:, 8:16],
                             w2_rows[bass.ds(e, 1)].rearrange("o p c n -> (o p) c n")).then_inc(w_in[q], 16)

            def load_rows(n, s):
                sp.wait_ge(xeT_psum, n + 1)
                sp.dma_start(xe[s], xe_rows[bass.ds(n, 1)].rearrange("o p t d -> (o p) t d")).then_inc(xe_in[s], 16)

            def store_rows(n, s):
                sp.wait_ge(ye_ready, n + 1)
                sp.dma_start(ye_rows[bass.ds(n, 1)].rearrange("o p t d -> (o p) t d"), y_sb[s]).then_inc(ye_out[s], 16)

            def pair_of_experts(pair, last):
                for k in range(PAIR):
                    q, g = k // GROUPS, k % GROUPS
                    n = pair * PAIR + k
                    if g == 0 and not (last and q == 1):
                        sp.wait_ge(w_low, PIECES * (pair * 2 + q) + 1)
                        load_weights(pair * 2 + q + 1, 1 - q)
                    if not (last and k >= PAIR - 2):
                        load_rows(n + 2, k % 2)
                    store_rows(n, k % 2)

            load_weights(0, 0)
            stage_end(sp, 4)
            sp.wait_ge(rows_out[0], 16 * TILES)
            load_rows(0, 0)
            load_rows(1, 1)
            sp.wait_ge(rows_out[1], 16 * TILES)
            with sp.Fori(0, E // 2 - 1) as pair:
                pair_of_experts(pair, False)
            pair_of_experts(E // 2 - 1, True)
            for s in range(2):
                sp.wait_ge(ye_out[s], 16 * (E * GROUPS // 2 + 1))
            stage_end(sp, 5)

            with sp.Fori(0, B // 2) as bb:
                for s in range(2):
                    b = bb * 2 + s
                    sp.wait_ge(out_ready, b + 1)
                    sp.dma_start(out_tiles[bass.ds(b, 1)].rearrange("o p t d -> (o p) t d"), o_buf[s]).then_inc(out_stored[s], 16)
            for s in range(2):
                sp.wait_ge(out_stored[s], 16 * (B // 2 + 1))

        @block.gpsimd
        def _(pool):
            chain = Chain(pool, chain_g)
            chain.link(nc.gpsimd.memset(ssm_pad[0:HEADS, :], 0.0))
            pool.dma_start(ssm_pad[0:HEADS, P:P + TAPS], ssm).then_inc(ssm_in, 16)
            pool.dma_start(sD_sb[:], sD.rearrange("(h o) -> h o", o=1)).then_inc(ssm_in, 16)
            pool.dma_start(kD_row[0:1, :], kD.rearrange("(o d) -> o d", o=1)).then_inc(kD_in, 16)
            pool.wait_ge(ssm_in, 32)
            nc.gpsimd.tensor_tensor(ssm_pad[0:HEADS, TOEP - 1:TOEP], ssm_pad[0:HEADS, TOEP - 1:TOEP], sD_sb[:],
                                    ALU.add).then_inc(ssm_ready, 2)
            stage_end(pool, 0)
            stage_end(pool, 1)
            nc.gpsimd.memset(zero, 0.0).then_inc(zero_set, 1)

            with pool.Fori(0, HEADS // 2) as hh:
                for s in range(2):
                    h = hh * 2 + s
                    pool.wait_ge(toep_high, h + 1)
                    nc.gpsimd.tensor_tensor(toep_parts[s][1][:], backwards(toep_raw[s]), toep_parts[s][0][:].bitcast(F32),
                                            ALU.subtract).then_inc(toep_low, 1)
                    for g in range(4):
                        pool.wait_ge(kv_high, 4 * h + g + 1)
                        quarter = slice(512 * g, 512 * g + 512)
                        nc.gpsimd.tensor_tensor(kv_parts[s][1][:, quarter], kv_flat[s][:, quarter],
                                                kv_parts[s][0][:, quarter].bitcast(F32), ALU.subtract).then_inc(kv_low, 1)
            stage_end(pool, 2)
            stage_end(pool, 3)

            def weights_low(e, q, pieces):
                for piece in pieces:
                    pool.wait_ge(w_high, PIECES * e + piece + 1)
                    nc.gpsimd.tensor_tensor(w_piece(q, 1, piece), raw_piece(q, piece), w_piece(q, 0, piece).bitcast(F32),
                                            ALU.subtract).then_inc(w_low, 1)

            weights_low(0, 0, range(PIECES))
            stage_end(pool, 4)
            pool.wait_ge(xe_zeroed, 160)
            for r in range(2):
                for tile in range(TILES):
                    nc.gpsimd.indirect_dma_start(
                        xe_dram[:, :], bass.IndirectOffsetOnAxis(ap=to_slot[r][:, tile:tile + 1], axis=0),
                        qkv[:, tile, 2 * D:3 * D], None).then_inc(rows_out[r], 16)

            with pool.Fori(0, E // 2 - 1) as pair:
                for q in range(2):
                    weights_low(pair * 2 + q + 1, 1 - q, range(PIECES))
            weights_low(E - 1, 1, range(PIECES))
            for s in range(2):
                stored = (E - 1) * GROUPS
                pool.wait_ge(ye_out[s], 16 * ((stored + 1 - s) // 2 + 1))
            pool.wait_ge(rows_out[0], 16 * TILES)
            pool.wait_ge(rows_out[1], 16 * TILES)
            for r in range(2):
                if r == 1:
                    stage_end(pool, 5)
                for b in range(B):
                    for t in range(TB):
                        tile = t * B + b
                        nc.gpsimd.indirect_dma_start(
                            qkv[:, tile, 2 * D * (1 - r):2 * D * (1 - r) + D], None, ye_dram[0:SLOTS - CAP * (1 - r), :],
                            bass.IndirectOffsetOnAxis(ap=from_slot[r][:, tile:tile + 1], axis=0)).then_inc(rows_in[r][b], 16)
            for r in range(2):
                for b in range(B):
                    pool.wait_ge(rows_in[r][b], 16 * TB)

        @block.scalar
        def _(act):
            def copy(dst, src):
                return nc.scalar.activation(dst, src, ACT.Copy)

            act.wait_ge(c_in, 16)
            nc.scalar.activation(c_exp[:], c_sb[:], ACT.Exp, scale=-1.0).then_inc(exp_c, 1)
            act.wait_ge(kk_spec_psum, 1)
            nc.scalar.activation(kk_spec.rearrange("p j e -> p (j e)"), ps[:, 0:4].rearrange("p a n -> p (a n)"),
                                 ACT.Copy, scale=1.0 / HALF).then_inc(kk_spec_ready, 1)
            act.wait_ge(eps_set, 1)
            with act.Fori(0, B // 2) as bb:
                for s in range(2):
                    b = bb * 2 + s
                    act.wait_ge(var_ready, b + 1)
                    nc.scalar.activation(std[:], mean_var[:, :, 1], ACT.Sqrt, bias=eps[:]).then_inc(std_ready, 1)
                    for g in range(4):
                        act.wait_ge(hT_psum, 4 * b + g + 1)
                        copy(hT_buf[s][:, g // 2, (g % 2) * BANK:(g % 2 + 1) * BANK], ps[:, g]).then_inc(hT_ready, 1)
            stage_end(act, 0)

            def spec_out(b):
                for j in range(JT):
                    act.wait_ge(spec_psum, JT * b + j + 1)
                    if j == 0:
                        act.wait_ge(prod_ready, b + 1)
                    copy(spec[:, j].rearrange("p h e -> p (h e)"), ps[:, j % 4]).then_inc(spec_ready, 1)

            def conv_out(b):
                for t in range(CT):
                    act.wait_ge(conv_psum, CT * b + t + 2)
                    halves = tile_view[:, t::CT, bass.ds(b, 1), D:2 * D].rearrange("p h o n -> p h (o n)")
                    copy(halves, ps[:, 4 + t].rearrange("p (h e) -> p h e", h=2)).then_inc(conv_ready, 1)

            spec_out(0)
            with act.Fori(0, B - 1) as b:
                spec_out(b + 1)
                conv_out(b)
            conv_out(B - 1)
            stage_end(act, 1)

            with act.Fori(0, HEADS // 2) as hh:
                for s in range(2):
                    h = hh * 2 + s
                    act.wait_ge(toep_in[s], 16 * hh + 16)
                    act.wait_ge(mix_psum, 4 * h + 1)
                    copy(toep_parts[s][0][:], backwards(toep_raw[s])).then_inc(toep_high, 1)
                    for g in range(4):
                        act.wait_ge(kv_ready, 4 * h + g + 1)
                        quarter = slice(512 * g, 512 * g + 512)
                        copy(kv_parts[s][0][:, quarter], kv_flat[s][:, quarter]).then_inc(kv_high, 1)
            stage_end(act, 2)

            with act.Fori(0, B) as b:
                act.wait_ge(yT_psum, 4 * b + 1)
                copy(y_b, rows_of(b, 0, D)).then_inc(y_b_ready, 1)
                for g in range(4):
                    act.wait_ge(yT_psum, 4 * b + g + 2)
                    copy(yT[:, g // 2, (g % 2) * BANK:(g % 2 + 1) * BANK], ps[:, 4 + g % 2]).then_inc(yT_ready, 1)
                act.wait_ge(var2_ready, b + 1)
                nc.scalar.activation(std[:], mean_var[:, :, 1], ACT.Sqrt, bias=eps[:]).then_inc(std2_ready, 1)
                act.wait_ge(h2_ready, b + 1)
                copy(rows_of(b, 2 * D, 3 * D), h2_b).then_inc(h2_kept, 1)
                for g in range(4):
                    act.wait_ge(h2T_psum, 4 * b + g + 1)
                    copy(h2T[:, g // 2, (g % 2) * BANK:(g % 2 + 1) * BANK], ps[:, 6]).then_inc(h2T_ready, 1)
            stage_end(act, 3)

            act.wait_ge(centred, 1)
            nc.scalar.activation(probs, logits, ACT.Exp).then_inc(exp_done, 1)

            def weights_high(e, q, pieces):
                for piece in pieces:
                    copy(w_piece(q, 0, piece), raw_piece(q, piece)).then_inc(w_high, 1)

            act.wait_ge(w_in[0], 48)
            weights_high(0, 0, range(PIECES))
            stage_end(act, 4)

            def pair_of_experts(pair, last):
                for k in range(PAIR):
                    q, g = k // GROUPS, k % GROUPS
                    n = pair * PAIR + k
                    for a in range(4):
                        act.wait_ge(hid_psum, 4 * n + a + 1)
                        nc.scalar.activation(hid_parts[0][:, 512 * a:512 * a + 512], ps[:, a], ACT.Relu).then_inc(hid_high, 1)
                    if not (last and k == PAIR - 1):
                        act.wait_ge(xeT_psum, n + 4)
                        copy(xeT_parts[0][:], ps[:, 6]).then_inc(xeT_high, 1)
                    if g < 4 and not (last and q == 1):
                        if g == 0:
                            act.wait_ge(w_in[1 - q], 48 * (pair + 1 + q))
                        weights_high(pair * 2 + q + 1, 1 - q, range(2 * g, 2 * g + 2))

            act.wait_ge(xeT_psum, 3)
            copy(xeT_parts[0][:], ps[:, 6]).then_inc(xeT_high, 1)
            with act.Fori(0, E // 2 - 1) as pair:
                pair_of_experts(pair, False)
            pair_of_experts(E // 2 - 1, True)

            for r in range(2):
                if r == 1:
                    stage_end(act, 5)
                for b in range(B):
                    act.wait_ge(rows_in[r][b], 16 * TB)
                    for t in range(TB):
                        tile = t * B + b
                        row = qkv[:, tile, 2 * D * (1 - r):2 * D * (1 - r) + D]
                        last = nc.scalar.activation(row, row, ACT.Copy, scale=weight[r][:, tile:tile + 1])
                    last.then_inc(weighted[r], 1)

        @block.vector
        def _(dve):
            chain = Chain(dve, chain_v)
            link = chain.link

            def tt(o, a, b_, op):
                return nc.vector.tensor_tensor(o, a, b_, op)

            def norm(x_tiles, h_tiles, var_sem, std_sem, b):
                for t in range(TB):
                    last = nc.vector.bn_stats(stats[:, t, :], x_tiles[:, t, :])
                link(last)
                dve.sem_inc(waited, 1)
                for t in range(TB):
                    last = nc.vector.bn_aggr(mean_var[:, t, :], stats[:, t, :])
                last.then_inc(var_sem, 1)
                dve.wait_ge(var_sem, b + 1)
                dve.wait_ge(std_sem, b + 1)
                link(nc.vector.reciprocal(std[:], std[:]))
                for t in range(TB):
                    last = nc.vector.tensor_scalar(h_tiles[:, t, :], x_tiles[:, t, :], mean_var[:, t, 0:1],
                                                   std[:, t:t + 1], ALU.subtract, ALU.mult)
                link(last)

            dve.sem_inc(prod_ready, 1)
            dve.sem_inc(conv_psum, 1)
            dve.sem_inc(mix_read, 8)
            dve.sem_inc(mix_psum, 5)
            dve.sem_inc(x_used, 1)
            dve.sem_inc(yT_psum, 1)
            dve.sem_inc(ye_psum, 1)
            dve.sem_inc(xeT_psum, 2)
            for s in range(2):
                dve.sem_inc(ye_out[s], 16)
                dve.sem_inc(out_stored[s], 16)
            nc.vector.memset(eps[:], EPS).then_inc(eps_set, 1)
            dve.wait_ge(exp_c, 1)
            link(nc.vector.tensor_scalar_add(c_exp[:], c_exp[:], 1.0))
            link(nc.vector.reciprocal(c_exp[:], c_exp[:]))
            tt(siluT[:], c_sb[:], c_exp[:], ALU.mult).then_inc(siluT_ready, 1)
            dve.wait_ge(kk_in, 16)
            dve.wait_ge(kD_in, 16)
            tt(kkT[0:1, 0, :], kkT[0:1, 0, :], kD_row[0:1, :], ALU.add).then_inc(kkT_ready, 1)
            dve.wait_ge(mod_psum, 3)
            link(nc.vector.tensor_copy(mod_row[0:B, :], ps[0:B, 5:8].rearrange("p a n -> p (a n)")))
            for m in (CA, CB):
                v = mod_row[0:B, m * D:(m + 1) * D]
                link(nc.vector.tensor_scalar_add(v, v, 1.0))
            for m in (GA, GB):
                v = mod_row[0:B, m * D:(m + 1) * D]
                link(nc.vector.tensor_scalar(clamp_b[0:B, :], v, -1.0, None, ALU.mult))
                link(tt(clamp_b[0:B, :], clamp_b[0:B, :], v, ALU.max))
                link(nc.vector.tensor_scalar_max(clamp_b[0:B, :], clamp_b[0:B, :], 0.25))
                link(nc.vector.tensor_scalar(clamp_a[0:B, :], v, 0.0, 2.0, ALU.is_ge, ALU.mult))
                link(nc.vector.tensor_scalar_add(clamp_a[0:B, :], clamp_a[0:B, :], -1.0))
                last = tt(v, clamp_a[0:B, :], clamp_b[0:B, :], ALU.mult)
                if m == GA:
                    link(last)
            last.then_inc(mod_ready, 1)

            def qkv_out(b):
                for t in range(TB):
                    dve.wait_ge(qkv_psum, TB * b + t + 1)
                    bank = 4 + 2 * (t % 2)
                    tt(tile_view[:, t, bass.ds(b, 1), :].rearrange("p o n -> p (o n)"),
                       ps[:, bank:bank + 2].rearrange("p a n -> p (a n)")[:, 0:3 * D], bias[:, 0:3 * D],
                       ALU.add).then_inc(qkv_ready, 1)

            dve.wait_ge(bias_in, 16)
            with chain.loop(B // 2, 2 * 4) as bb:
                for s in range(2):
                    b = bb * 2 + s
                    dve.wait_ge(x_in[s], bb * 16 + 16)
                    norm(x_buf[s], x_buf[s], var_ready, std_ready, b)
                    dve.wait_ge(mod_a_in, 16 * B)
                    link(tt(x_buf[s], x_buf[s], mod_of(mod_a, b, 1, ALL), ALU.mult))
                    tt(x_buf[s], x_buf[s], mod_of(mod_a, b, 0, ALL), ALU.add).then_inc(h_ready, 1)
                    qkv_out(b)
            stage_end(dve, 0)

            re, im = slice(0, JR), slice(JR, JT)
            PR = [P, JR, 2, D]
            with chain.loop(B, 4) as b:
                dve.wait_ge(spec_ready, JT * (b + 1))
                nc.vector.scalar_tensor_tensor(spec[:, re, 1], spec[:, im, 0], sign[:, 1:2], spec[:, re, 1], ALU.mult, ALU.add)
                link(nc.vector.scalar_tensor_tensor(spec[:, im, 1], spec[:, re, 0], sign[:, 0:1], spec[:, im, 1], ALU.mult, ALU.add))
                k_re = kk_spec[:, re].unsqueeze(2).to_broadcast(PR)
                k_im = kk_spec[:, im].unsqueeze(2).to_broadcast(PR)
                tt(tmp[0], k_re, spec[:, re], ALU.mult)
                link(tt(tmp[1], k_im, spec[:, im], ALU.mult))
                dve.wait_ge(conv_psum, CT * b + 1)
                link(tt(prod[:, re], tmp[0], tmp[1], ALU.subtract))
                tt(tmp[0], k_re, spec[:, im], ALU.mult)
                link(tt(tmp[1], k_im, spec[:, re], ALU.mult))
                tt(prod[:, im], tmp[0], tmp[1], ALU.add).then_inc(prod_ready, 1)
            stage_end(dve, 1)

            def products(h, s):
                for g in range(4):
                    tiles = slice(8 * g, 8 * g + 8)
                    k_i = qkv[:, tiles, bass.ds(h * NJ + D, NJ)].unsqueeze(3).to_broadcast([P, 8, NJ, NJ])
                    v_j = qkv[:, tiles, bass.ds(h * NJ + 2 * D, NJ)].unsqueeze(2).to_broadcast([P, 8, NJ, NJ])
                    tt(kv_buf[s][:, tiles], k_i, v_j, ALU.mult).then_inc(kv_ready, 1)

            def gate_and_sum(h, s):
                for g in range(4):
                    tiles = slice(8 * g, 8 * g + 8)
                    q_i = qkv[:, tiles, bass.ds(h * NJ, NJ)].unsqueeze(3).to_broadcast([P, 8, NJ, NJ])
                    dve.wait_ge(mix_psum, 4 * h + g + 6)
                    tt(qy[g], ps[:, 4 * s + g].rearrange("p (t i j) -> p t i j", t=8, i=NJ), q_i,
                       ALU.mult).then_inc(mix_read, 1)
                    dve.wait_ge(mix_read, 4 * h + g + 1 + 8)
                    dve.sem_inc(waited, 1)
                    nc.vector.tensor_reduce(qkv[:, tiles, bass.ds(h * NJ, NJ)],
                                            qy[g].rearrange("p t i j -> p t j i"), AX.X, ALU.add)

            products(0, 0)
            products(1, 1)
            with dve.Fori(0, HEADS // 2 - 1) as hh:
                for s in range(2):
                    gate_and_sum(hh * 2 + s, s)
                    products(hh * 2 + s + 2, s)
            for s in range(2):
                gate_and_sum(HEADS - 2 + s, s)
            stage_end(dve, 2)

            dve.wait_ge(mod_d_in, 16 * B)
            with chain.loop(B, 7) as b:
                dve.wait_ge(attn_psum, b + 1)
                att = ps[:, 0:4].rearrange("p a n -> p (a n)").rearrange("p (t d) -> p t d", t=TB)
                link(tt(x2_b, att, bias[:, 3 * D:4 * D].unsqueeze(1).to_broadcast(ALL), ALU.add))
                link(tt(x2_b, x2_b, mod_of(mod_d, b, 0, ALL), ALU.mult))
                dve.wait_ge(x_again_in, 16 * b + 16)
                tt(x2_b, x2_b, x_again, ALU.add).then_inc(x_used, 1)
                dve.wait_ge(x_used, b + 2)
                nc.vector.tensor_copy(rows_of(b, D, 2 * D), x2_b)
                norm(x2_b, h2_b, var2_ready, std2_ready, b)
                link(tt(h2_b, h2_b, mod_of(mod_d, b, 2, ALL), ALU.mult))
                tt(h2_b, h2_b, mod_of(mod_d, b, 1, ALL), ALU.add).then_inc(h2_ready, 1)
                dve.wait_ge(logit_psum, b + 1)
                dst = logits.rearrange("p (t b) e -> p t b e", b=B)[:, :, bass.ds(b, 1), :].rearrange("p t o e -> p t (o e)")
                link(nc.vector.tensor_copy(dst, ps[:, 7, 0:TB * E].rearrange("p (t e) -> p t e", t=TB)))
                dve.wait_ge(h2_kept, b + 1)
            stage_end(dve, 3)

            TE = [P, TILES, E]
            link(nc.vector.tensor_reduce(row_max, logits, AX.X, ALU.max))
            tt(logits, logits, row_max.unsqueeze(2).to_broadcast(TE), ALU.subtract).then_inc(centred, 1)
            dve.wait_ge(exp_done, 1)
            link(nc.vector.tensor_reduce(row_sum, probs, AX.X, ALU.add))
            link(nc.vector.reciprocal(row_sum, row_sum))
            link(tt(probs, probs, row_sum.unsqueeze(2).to_broadcast(TE), ALU.mult))
            for t in range(TILES):
                last = nc.vector.max(top_v[:, t, :], probs[:, t, :])
            link(last)
            for t in range(TILES):
                last = nc.vector.max_index(top_i[:, t, :], top_v[:, t, :], probs[:, t, :])
            link(last)
            link(nc.vector.tensor_copy(top_f, top_i))
            ids = expert_id[:].unsqueeze(1).to_broadcast(TE)
            for which, op in ((row_max, ALU.min), (row_sum, ALU.max)):
                last = tt(which, top_f[:, :, 0], top_f[:, :, 1], op)
            link(last)
            tt(first, ids, row_max.unsqueeze(2).to_broadcast(TE), ALU.is_equal)
            link(tt(second, ids, row_sum.unsqueeze(2).to_broadcast(TE), ALU.is_equal))
            for r, mask in enumerate((first, second)):
                link(tt(picked, probs, mask, ALU.mult))
                link(nc.vector.tensor_reduce(weight[r][:], picked, AX.X, ALU.add))
            link(tt(routed, first, second, ALU.add))
            link(tt(picked, probs, routed, ALU.mult))
            link(nc.vector.tensor_scalar_add(routed, routed, -1.0))
            def chunked(v, r):
                return v.rearrange("p (q r b) e -> p r q b e", r=2, b=B)[:, r]

            for r in range(2):
                last = tt(gate_cols[:, r].rearrange("p e b q -> p q b e"), chunked(picked, r), chunked(routed, r), ALU.add)
            last.then_inc(gate_ready, 1)
            dve.wait_ge(gateT_psum, 1)
            nc.vector.memset(theta[:], 0)
            nc.vector.memset(ones_l, 1.0)
            link(nc.vector.tensor_copy(gate_l, ps[:, 0, 0:256]))
            with chain.loop(BITS, 3) as i:
                link(tt(cand[:], theta[:], bit_int[:, bass.ds(i, 1)], ALU.bitwise_or))
                nc.vector.tensor_scalar(junk, gate_l, cand[:].bitcast(F32), None, ALU.is_ge, ALU.add,
                                        accum_out=count[:]).then_inc(count_ready, 1)
                dve.wait_ge(count_psum, i + 1)
                link(nc.vector.tensor_scalar(accepted[:], ps[:, 1, 0:1], float(CAP), bit_float[:, bass.ds(i, 1)],
                                             ALU.is_ge, ALU.mult))
                link(tt(theta[:], theta[:], accepted[:], ALU.bitwise_or))
            th = theta[:].bitcast(F32)
            nc.vector.tensor_scalar(is_gt, gate_l, th, None, ALU.is_gt, ALU.add,
                                    accum_out=count[:]).then_inc(count_ready, 1)
            link(nc.vector.tensor_scalar(is_eq, gate_l, th, None, ALU.is_equal, ALU.add, accum_out=row_total[:]))
            dve.wait_ge(count_psum, BITS + 1)
            link(nc.vector.tensor_scalar(need[:], ps[:, 1, 0:1], -1.0, float(CAP), ALU.mult, ALU.add))
            nc.vector.tensor_tensor_scan(scan, ones_l, is_eq, 0.0, ALU.mult, ALU.add).then_inc(count_ready, 1)
            dve.wait_ge(count_ready, BITS + 2)
            dve.wait_ge(count_psum, BITS + 2)
            link(nc.vector.tensor_copy(before[:], ps[:, 1, 0:1]))
            link(nc.vector.scalar_tensor_tensor(rank, scan, before[:], is_eq, ALU.add, ALU.subtract))
            link(nc.vector.scalar_tensor_tensor(rank, rank, need[:], is_eq, ALU.is_lt, ALU.mult))
            link(tt(keep, is_gt, rank, ALU.add))
            link(nc.vector.tensor_tensor_scan(scan, ones_l, keep, 0.0, ALU.mult, ALU.add))
            nc.vector.tensor_copy(row_total[:], scan[:, 255:256]).then_inc(count_ready, 1)
            dve.wait_ge(count_psum, BITS + 3)
            link(nc.vector.tensor_scalar(before[:], ps[:, 1, 0:1], slot_base[:], None, ALU.add))
            nc.vector.scalar_tensor_tensor(rank, scan, before[:], keep, ALU.add, ALU.mult).then_inc(slots_ready, 1)
            dve.wait_ge(slotT_psum, 1)
            for par in range(2):
                dst = slot_t.rearrange("p (q r b) e -> p q r b e", r=2, b=B)[:, :, par]
                src = ps[:, 2, par * P:(par + 1) * P].rearrange("p (e b q) -> p q b e", e=E, b=B)
                last = nc.vector.tensor_copy(dst, src)
            link(last)
            for r, mask in enumerate((first, second)):
                link(tt(picked, slot_t, mask, ALU.mult))
                link(nc.vector.tensor_reduce(slot[r], picked, AX.X, ALU.add))
                link(nc.vector.scalar_tensor_tensor(weight[r][:], slot[r], 0.5, weight[r][:], ALU.is_ge, ALU.mult))
                link(nc.vector.tensor_scalar(from_slot[r][:], slot[r], -1.0, 0.0, ALU.add, ALU.max))
                link(nc.vector.scalar_tensor_tensor(slot_tmp, slot[r], 0.5, trash_slot[:], ALU.is_lt, ALU.mult))
                link(tt(slot_tmp, slot_tmp, slot[r], ALU.add))
                link(nc.vector.tensor_scalar_add(to_slot[r][:], slot_tmp, -1.0))
            stage_end(dve, 4)

            def pair_of_experts(pair, last):
                for k in range(PAIR):
                    n = pair * PAIR + k
                    for a in range(4):
                        dve.wait_ge(hid_high, 4 * n + a + 1)
                        part = slice(512 * a, 512 * a + 512)
                        nc.vector.scalar_tensor_tensor(hid_parts[1][:, part], ps[:, a], 0.0, hid_parts[0][:, part].bitcast(F32),
                                                       ALU.max, ALU.subtract).then_inc(hid_low, 1)
                    if not (last and k == PAIR - 1):
                        dve.wait_ge(xeT_high, n + 2)
                        tt(xeT_parts[1][:], ps[:, 6], xeT_parts[0][:].bitcast(F32), ALU.subtract).then_inc(xeT_low, 1)
                    dve.wait_ge(ye_psum, n + 2)
                    dve.wait_ge(ye_out[k % 2], (pair * GROUPS + k // 2 + 1) * 16)
                    nc.vector.tensor_copy(y_sb[k % 2].rearrange("p t d -> p (t d)"), ps[:, 4 + k % 2]).then_inc(ye_ready, 1)

            dve.wait_ge(xeT_high, 1)
            tt(xeT_parts[1][:], ps[:, 6], xeT_parts[0][:].bitcast(F32), ALU.subtract).then_inc(xeT_low, 1)
            with dve.Fori(0, E // 2 - 1) as pair:
                pair_of_experts(pair, False)
            pair_of_experts(E // 2 - 1, True)
            stage_end(dve, 5)

            with chain.loop(B // 2, 2 * 2) as bb:
                for s in range(2):
                    b = bb * 2 + s
                    dve.wait_ge(weighted[1], b + 1)
                    dve.wait_ge(out_stored[s], bb * 16 + 16)
                    link(tt(o_buf[s], rows_of(b, 0, D), rows_of(b, 2 * D, 3 * D), ALU.add))
                    link(tt(o_buf[s], o_buf[s], mod_of(mod_d, b, 3, ALL), ALU.mult))
                    tt(o_buf[s], o_buf[s], rows_of(b, D, 2 * D), ALU.add).then_inc(out_ready, 1)
                    dve.wait_ge(out_ready, b + 1)

        @block.tensor
        def _(pe):
            mm, transpose = nc.tensor.matmul, nc.tensor.transpose
            pe.wait_ge(consts_in, 160)
            pe.wait_ge(siluT_ready, 1)
            pe.wait_ge(wmod_in, 16)
            for a in range(3):
                for dc in range(DC):
                    last = mm(ps[0:B, 5 + a, :], siluT[:, dc, :], wmod_sb[:, dc, a * BANK:(a + 1) * BANK],
                              start=dc == 0, stop=dc == DC - 1)
                last.then_inc(mod_psum, 1)
            pe.wait_ge(dft_in, 16)
            pe.wait_ge(kkT_ready, 1)
            for j in range(JT):
                for sc in range(CT):
                    last = mm(ps[:, j // 2, (j % 2) * D:(j % 2 + 1) * D], dft[:, sc, j * P:(j + 1) * P], kkT[:, sc, :],
                              start=sc == 0, stop=sc == CT - 1)
            last.then_inc(kk_spec_psum, 1)
            pe.wait_ge(kk_spec_ready, 1)
            pe.wait_ge(mod_ready, 1)
            pe.wait_ge(w_qkv_in, 32)
            with pe.Fori(0, B // 2) as bb:
                for s in range(2):
                    b = bb * 2 + s
                    pe.wait_ge(h_ready, b + 1)
                    for g in range(4):
                        for t in range(4):
                            tb = (g % 2) * 4 + t
                            last = transpose(ps[:, g, t * P:(t + 1) * P],
                                             x_buf[s][:, tb, (g // 2) * P:(g // 2 + 1) * P], ident[:])
                        last.then_inc(hT_psum, 1)
                    pe.wait_ge(hT_ready, 4 * b + 4)
                    for tb in range(TB):
                        bank = 4 + 2 * (tb % 2)
                        if tb >= 2:
                            pe.wait_ge(qkv_ready, TB * b + tb - 1)
                        for lo, hi in ((0, 512), (512, 768)):
                            for dc in range(DC):
                                last = mm(ps[:, bank + lo // BANK, 0:hi - lo], hT_buf[s][:, dc, tb * P:(tb + 1) * P],
                                          wqkvT[:, dc, lo:hi], start=dc == 0, stop=dc == DC - 1)
                        last.then_inc(qkv_psum, 1)
                    pe.wait_ge(qkv_ready, TB * b + TB)
            stage_end(pe, 0)

            pe.wait_ge(idft_in, 16)

            def forward(b):
                for j in range(JT):
                    if j >= 4:
                        pe.wait_ge(spec_ready, JT * b + j - 3)
                    for t in range(CT):
                        halves = tile_view[:, t::CT, bass.ds(b, 1), D:2 * D].rearrange("p h o n -> p h (o n)")
                        last = mm(ps[:, j % 4].rearrange("p (h e) -> p h e", h=2), dft[:, t, j * P:(j + 1) * P], halves,
                                  start=t == 0, stop=t == CT - 1)
                    last.then_inc(spec_psum, 1)

            def inverse(b):
                pe.wait_ge(prod_ready, b + 2)
                for t in range(CT):
                    for j in range(JT):
                        last = mm(ps[:, 4 + t], idft[:, j, t * P:(t + 1) * P], prod[:, j].rearrange("p h e -> p (h e)"),
                                  start=j == 0, stop=j == JT - 1)
                    last.then_inc(conv_psum, 1)

            forward(0)
            with pe.Fori(0, B - 1) as b:
                pe.wait_ge(spec_ready, JT * b + JT)
                forward(b + 1)
                inverse(b)
                pe.wait_ge(conv_ready, CT * b + CT)
            inverse(B - 1)
            stage_end(pe, 1)

            with pe.Fori(0, HEADS // 2) as hh:
                for s in range(2):
                    h = hh * 2 + s
                    pe.wait_ge(toep_low, h + 1)
                    for g in range(4):
                        pe.wait_ge(kv_low, 4 * h + g + 1)
                        pe.wait_ge(mix_read, 4 * h + g + 1)
                        steps = []
                        for o in range(OFFS):
                            lo = max(2 * g, o)
                            if lo <= 2 * g + 1:
                                steps.append((o, lo))
                        for n, (o, lo) in enumerate(steps):
                            cnt = (2 * g + 2 - lo) * B
                            src = slice((lo - o) * B * 64, (lo - o) * B * 64 + cnt * 64)
                            for i, (a, x) in enumerate(PASSES):
                                last = mm(ps[:, 4 * s + g, (lo - 2 * g) * B * 64:BANK],
                                          toep_parts[s][a][:, o * P:(o + 1) * P], kv_parts[s][x][:, src],
                                          start=n == 0 and i == 0, stop=n == len(steps) - 1 and i == 2)
                        last.then_inc(mix_psum, 1)
            stage_end(pe, 2)

            with pe.Fori(0, B) as b:
                pe.wait_ge(y_b_ready, b + 1)
                for g in range(4):
                    if g >= 2:
                        pe.wait_ge(yT_ready, 4 * b + g - 1)
                    for t in range(4):
                        tb = (g % 2) * 4 + t
                        last = transpose(ps[:, 4 + g % 2, t * P:(t + 1) * P],
                                         y_b[:, tb, (g // 2) * P:(g // 2 + 1) * P], ident[:])
                    last.then_inc(yT_psum, 1)
                pe.wait_ge(yT_ready, 4 * b + 4)
                for tb in range(TB):
                    for cc in range(DC):
                        last = mm(ps[:, tb // 2, (tb % 2) * D:(tb % 2 + 1) * D], yT[:, cc, tb * P:(tb + 1) * P], woT[:, cc, :],
                                  start=cc == 0, stop=cc == DC - 1)
                last.then_inc(attn_psum, 1)
                pe.wait_ge(h2_ready, b + 1)
                for g in range(4):
                    if g >= 1:
                        pe.wait_ge(h2T_ready, 4 * b + g)
                    for t in range(4):
                        tb = (g % 2) * 4 + t
                        last = transpose(ps[:, 6, t * P:(t + 1) * P],
                                         h2_b[:, tb, (g // 2) * P:(g // 2 + 1) * P], ident[:])
                    last.then_inc(h2T_psum, 1)
                pe.wait_ge(h2T_ready, 4 * b + 4)
                for tb in range(TB):
                    for cc in range(DC):
                        last = mm(ps[:, 7, tb * E:(tb + 1) * E], h2T[:, cc, tb * P:(tb + 1) * P], wr_sb[:, cc, :],
                                  start=cc == 0, stop=cc == DC - 1)
                last.then_inc(logit_psum, 1)
            stage_end(pe, 3)

            pe.wait_ge(gate_ready, 1)
            for par in range(2):
                cols = gate_cols[:, par].rearrange("p e b q -> p (e b q)")
                last = transpose(ps[:, 0, par * P:(par + 1) * P], cols, ident[:])
            last.then_inc(gateT_psum, 1)
            with pe.Fori(0, BITS) as i:
                pe.wait_ge(count_ready, i + 1)
                mm(ps[:, 1, 0:1], group_ones[:], count[:], start=True, stop=True).then_inc(count_psum, 1)
            pe.wait_ge(count_ready, BITS + 1)
            mm(ps[:, 1, 0:1], group_ones[:], count[:], start=True, stop=True).then_inc(count_psum, 1)
            for n in (2, 3):
                pe.wait_ge(count_ready, BITS + n)
                mm(ps[:, 1, 0:1], group_before[:], row_total[:], start=True, stop=True).then_inc(count_psum, 1)
            pe.wait_ge(slots_ready, 1)
            for par in range(2):
                last = transpose(ps[:, 2, par * P:(par + 1) * P], rank[:, par * P:(par + 1) * P], ident[:])
            last.then_inc(slotT_psum, 1)
            stage_end(pe, 4)

            def transpose_rows(count, s):
                pe.wait_ge(xe_in[s], 16 * count)
                for dc in range(DC):
                    for t in range(GT):
                        last = transpose(ps[:, 6, dc * GROUP + t * P:dc * GROUP + (t + 1) * P],
                                         xe[s][:, t, dc * P:(dc + 1) * P], ident[:])
                last.then_inc(xeT_psum, 1)

            def pair_of_experts(pair, last_pair):
                for k in range(PAIR):
                    q, g, s = k // GROUPS, k % GROUPS, k % 2
                    n = pair * PAIR + k
                    if g == 0:
                        pe.wait_ge(w_low, PIECES * (pair * 2 + q + 1))
                    pe.wait_ge(xeT_low, n + 1)
                    for f in range(FC):
                        for dc in range(DC):
                            for i, (a, x) in enumerate(PASSES):
                                last = mm(ps[:, f // 2, (f % 2) * GROUP:(f % 2 + 1) * GROUP],
                                          w1_parts[q][a][:, dc * F + f * P:dc * F + (f + 1) * P],
                                          xeT_parts[x][:, dc * GROUP:(dc + 1) * GROUP],
                                          start=dc == 0 and i == 0, stop=dc == DC - 1 and i == 2)
                        if f % 2:
                            last.then_inc(hid_psum, 1)
                    if not (last_pair and k == PAIR - 1):
                        transpose_rows(pair * GROUPS + (k + 1) // 2 + 1, (k + 1) % 2)
                    for t in range(GT):
                        for f in range(FC):
                            if t == 0 and f % 2 == 0:
                                pe.wait_ge(hid_low, 4 * n + f // 2 + 1)
                            for i, (a, x) in enumerate(PASSES):
                                last = mm(ps[:, 4 + s, t * D:(t + 1) * D],
                                          hid_parts[a][:, f * GROUP + t * P:f * GROUP + (t + 1) * P],
                                          w2_parts[q][x][:, f * D:(f + 1) * D],
                                          start=f == 0 and i == 0, stop=f == FC - 1 and i == 2)
                    last.then_inc(ye_psum, 1)

            transpose_rows(1, 0)
            with pe.Fori(0, E // 2 - 1) as pair:
                pair_of_experts(pair, False)
            pair_of_experts(E // 2 - 1, True)
            stage_end(pe, 5)


def kernel(**inputs):
    import concourse.bacc as bacc
    from concourse.bass_utils import run_bass_kernel_spmd

    nc = bacc.Bacc("TRN2", target_bir_lowering=False, num_devices=1)
    arrays, args, tables = {}, [], {}
    given = {name: np.asarray(a) for name, a in inputs.items()}
    attn = {name[8:]: a for name, a in given.items() if name.startswith("L0_attn_")}
    wo = attn["Wo"].reshape(D, NJ, HEADS).transpose(2, 1, 0).reshape(D, D)
    laid_out = {
        "u": attn["u"],
        "w_qkv": np.concatenate([attn["Wq"].T, attn["Wk"].T, attn["Wv"].T], axis=1),
        "b_all": np.concatenate([attn["bq"], attn["bk"], attn["bv"], attn["bo"]])[None, :],
        "k_taps": attn["ssm_k_kernel"].T,
        "k_skip": attn["ssm_k_D"],
        "ssm_kernel": attn["ssm_kernel"][:, ::-1],
        "ssm_skip": attn["D"],
        "w_out": wo,
        "w_router": given["L0_ffn_Wr"],
        "w1": given["L0_ffn_W1"],
        "w2": given["L0_ffn_W2"],
        "cT": given["L0_c"].T,
        "wmod": given["L0_wmod"],
    }
    for name, a in laid_out.items():
        a = np.ascontiguousarray(a)
        arrays[f"in_{name}"] = a
        args.append(nc.dram_tensor(f"in_{name}", a.shape, mybir.dt.from_np(a.dtype), kind="ExternalInput").ap())
    for name, a in constants().items():
        arrays[f"const_{name}"] = a
        tables[name] = nc.dram_tensor(f"const_{name}", a.shape, mybir.dt.from_np(a.dtype), kind="ExternalInput").ap()
    out = nc.dram_tensor("out", [B, L, D], F32, kind="ExternalOutput").ap()
    adaln_block(nc, *args, tables, out)
    r = run_bass_kernel_spmd(nc, [arrays], core_ids=[0])
    return r.results[0]["out"]
```

```python
from contextlib import ExitStack, contextmanager

import numpy as np

import concourse.bass as bass
from concourse import mybir

ALU = mybir.AluOpType
ACT = mybir.ActivationFunctionType
AX = mybir.AxisListType
F32 = mybir.dt.float32
I32 = mybir.dt.int32
U32 = mybir.dt.uint32
F32R = mybir.dt.float32r

P = 128
B, L, D = 4, 1024, 256
TB = L // P
TILES = B * TB
DC = D // P
NJ = 8
HEADS = D // NJ
TAPS = 512
HALF = TAPS
FREQS = 2 * HALF
JT = FREQS // P
JR = JT // 2
JP = JT // 2
CT = HALF // P
BY_PARITY = (*range(0, CT, 2), *range(1, CT, 2))
OFFS = TAPS // P + 1
TOEP = OFFS * P
PAD = P + TAPS + P
E, F, TOPK = 8, 1024, 2
TOKENS = B * L
CAP = -(-TOKENS * TOPK * 5 // (4 * E))
SLOTS = E * CAP
FC = F // P
GROUP = 256
GT = GROUP // P
GROUPS = CAP // GROUP
PAIRS = (E - 2) // 2
FIRST, PAIR, LAST = range(GROUPS), range(GROUPS, 3 * GROUPS), range(GROUPS, 2 * GROUPS)
PIECE = 512
PIECES = 2 * DC * F // PIECE
PASSES = ((0, 0), (0, 1), (1, 0))
ROUNDS = 5
BITS = 30
LOGIT_BANK = (6, 6, 4, 5)
MODS = 6
SA, CA, GA, SB, CB, GB = range(MODS)
EPS = 1e-5
BANK = 512
ARENA = 27648
SPLIT = 184


def constants():
    block, parity, sample = np.meshgrid(np.arange(CT // 2), np.arange(2), np.arange(P), indexing="ij")
    t = (block * 2 * P + sample * 2 + parity).reshape(HALF, 1)
    m = np.arange(HALF // 2)[None, :]
    angle = 2 * np.pi * ((2 * m + 1) * t % (4 * HALF)) / (4 * HALF)
    forward = np.concatenate([np.cos(angle), -np.sin(angle)], axis=1).astype(np.float32)
    p = np.arange(P)
    same = (p[:, None] // 16) == (p[None, :] // 16)
    token = (np.arange(B)[None, None, :] * L + np.arange(TB)[None, :, None] * P + p[:, None, None])
    return {
        "dft": forward,
        "idft": np.ascontiguousarray(forward.T),
        "ident": np.eye(P, dtype=np.float32),
        "sign": np.stack([1.0 - 2.0 * (p % 2), 2.0 * (p % 2) - 1.0], 1).astype(np.float32),
        "group_ones": same.astype(np.float32),
        "group_before": (same & (p[:, None] < p[None, :])).astype(np.float32),
        "digit_int": np.tile(np.append(4 ** np.arange(BITS // 2 - 1, -1, -1)[:, None] * np.arange(1, 4), [0, 0, 0]).astype(np.int32), (P, 1)),
        "digit_unit": np.tile((4.0 ** np.arange(BITS // 2 - 1, -1, -1)).astype(np.float32), (P, 1)),
        "expert_id": np.tile(np.arange(E, dtype=np.float32), (P, 1)),
        "slot_base": ((p // 16) * CAP).astype(np.float32)[:, None],
        "trash_slot": (token.reshape(P, TILES) + SLOTS + 1).astype(np.float32),
    }


class Chain:

    def __init__(self, eng, sem):
        self.eng, self.sem, self.base, self.n = eng, sem, 0, 0

    def link(self, instruction):
        self.n += 1
        instruction.then_inc(self.sem, 1)
        self.eng.wait_ge(self.sem, self.base + self.n)

    @contextmanager
    def loop(self, times, per):
        start = self.base + self.n
        with self.eng.Fori(0, times) as i:
            self.base, self.n = i * per + start, 0
            yield i
            assert self.n == per, (self.n, per)
        self.base, self.n = start + times * per, 0


def adaln_block(nc, u, w_qkv, b_all, k_taps, kD, ssm, sD, w_out, Wr, W1, W2, cT, wmod, K, out):
    with ExitStack() as ctx:
        def sb(name, shape, dt=F32):
            return ctx.enter_context(nc.sbuf_tensor(name, shape, dt))

        def sem(name):
            return ctx.enter_context(nc.semaphore(name))

        qkv = sb("qkv", [P, TILES, 3 * D])
        arena = sb("arena", [P, ARENA])
        arena_at = nc.sbuf_base - 4 * ARENA
        ps = ctx.enter_context(nc.psum_tensor("ps", [P, 8, BANK], F32))

        def parts(name, start, shape):
            size = int(np.prod(shape[1:]))
            return parts_at(name, (start, start + size), shape)

        def parts_at(name, starts, shape):
            return [nc.alloc_sbuf_tensor_at(f"{name}_{part}", shape, F32R, offset=arena_at + 4 * start)
                    for start, part in zip(starts, ("high", "low"))]

        def region(start, size):
            return arena[:, start:start + size]

        R1, R2, FT, IT, KK0, WO0, WQ0, MA0, BI0, T0 = (
            0, 4096, 8192, 12288, 16384, 18432, 18944, 20480, 22528, 23552)
        kkT = region(T0, 1024).rearrange("p (c e) -> p c e", c=CT)
        kk_parity = region(T0 + 1024, 2048)
        wmod_sb = [region(start, MODS * D) for start in (FT + 2048, IT + 2048)]
        ssm_pad = region(MA0, PAD)
        mod_row = region(MA0 + PAD, 4 * D)
        kD_row = region(MA0 + PAD + 4 * D, D)
        clamp_a = region(T0 + 3072, D)
        clamp_b = region(T0 + 3328, D)
        x_buf = [region(R1 + 2048 * i, 2048).rearrange("p (t d) -> p t d", t=TB) for i in range(2)]
        h_full = [region(T0 + BANK * i, BANK) for i in range(2)]
        hT_parts = [parts_at(f"hT{i}", (R2 + 2048 * i, (FT, IT)[i] + 2048), [P, DC, L]) for i in range(2)]
        wqkv_parts = [parts_at("wqkv0", (KK0, KK0 + 1536), [P, 3 * D]),
                      parts_at("wqkv1", (KK0 + 768, MA0), [P, 3 * D])]
        wqkvT = region(WQ0, 1536).rearrange("p (c n) -> p c n", c=DC)
        woT = region(WO0, 512).rearrange("p (c n) -> p c n", c=DC)
        bias = region(BI0, 1024)
        dft = region(FT, 2048).rearrange("p (c m) -> p c m", c=CT)
        idft = region(IT, 2048).rearrange("p (j t) -> p j t", j=JP)
        kk_spec = region(KK0, 2048).rearrange("p (j e) -> p j e", j=JT)
        parity_spec = region(WQ0, 4096).rearrange("p (j h e) -> p j h e", j=JT, h=2)
        spec = region(R1, 4096).rearrange("p (j h e) -> p j h e", j=JT, h=2)
        folded_even, folded_odd_0, folded_odd_1 = (region(start, 2048).rearrange("p (j h e) -> p j h e", j=JP, h=2)
                                                   for start in (R2, R2 + 2048, IT + 2048))
        tmp = [region(T0 + 2048 * i, 2048).rearrange("p (j h e) -> p j h e", j=JR, h=2) for i in range(2)]
        k_stage = region(FT + 2048, 2048).rearrange("p (c e) -> p c e", c=TB)
        kv_buf = [region(R1 + 2048 * i, 2048).rearrange("p (t i j) -> p t i j", t=TILES, i=NJ) for i in range(2)]
        kv_parts = [parts(f"kv{i}", FT + 4096 * i, [P, 2048]) for i in range(2)]
        toep_raw = [region(WQ0 + TOEP * i, TOEP) for i in range(2)]
        toep_parts = [parts(f"toep{i}", start, [P, TOEP]) for i, start in enumerate((KK0, MA0))]
        qy = [region(T0 + 512 * g, 512).rearrange("p (t i j) -> p t i j", t=2 * B, i=NJ) for g in range(4)]
        zero = region(T0 + 2048, 2048)
        mod_d = region(R2, 4096).rearrange("p (b m d) -> p b m d", b=B, m=4)
        x_again = [region(FT + 2048 * i, 2048).rearrange("p (t d) -> p t d", t=TB) for i in range(2)]
        yT = region(IT, 2048).rearrange("p (c t) -> p c t", c=DC)
        h2T = region(IT + 2048, 2048).rearrange("p (c t) -> p c t", c=DC)
        wo_gated = [region(KK0 + 512 * i, 512).rearrange("p (c n) -> p c n", c=DC) for i in range(2)]
        bo_gated = [region(KK0 + 1024 + 256 * i, 256) for i in range(2)]
        routing = region(MA0, 2048).rearrange("p (a t e) -> p a t e", a=8, t=TILES)
        logits, probs, top_v, top_f, first, second, routed, slot_t = (routing[:, a] for a in range(8))
        gate_l = region(T0, 256)
        is_gt = region(T0 + 256, 256)
        is_eq = region(T0 + 512, 256)
        scan = region(T0 + 768, 256)
        rank = region(T0 + 1024, 256)
        keep = region(T0 + 1280, 256)
        ones_l = region(T0 + 1536, 256)
        junk = [region(T0 + start, 256) for start in (1792, 3072, 3328)]
        picked = region(T0 + 2048, 256).rearrange("p (t e) -> p t e", t=TILES)
        top_i = region(T0 + 2304, 256).bitcast(U32).rearrange("p (t e) -> p t e", t=TILES)
        gate_cols = region(T0 + 2816, 256).rearrange("p (r e b q) -> p r e b q", r=2, e=E, b=B)
        row_max, row_sum, slot_tmp, slot_0, slot_1 = (region(T0 + 2560 + TILES * i, TILES) for i in range(5))
        slot = [slot_0, slot_1]
        w_raw = [qkv[:, 16 * i:16 * i + 16, 0:D] for i in range(2)]
        w1_parts = [parts(f"w1_{i}", start, [P, DC * F]) for i, start in enumerate((R1, IT))]
        w2_parts = [parts(f"w2_{i}", start, [P, FC * D]) for i, start in enumerate((FT, KK0))]
        hid_parts = parts("hidden", 20480, [P, FC * GROUP])
        xeT_parts = parts("xeT", 24576, [P, DC * GROUP])
        xe = [region(25600 + 512 * i, 512).rearrange("p (t d) -> p t d", t=GT) for i in range(2)]
        y_sb = [region(26624 + 512 * i, 512).rearrange("p (t d) -> p t d", t=GT) for i in range(2)]

        ident = sb("ident_sb", [P, P])
        group_ones = sb("group_ones_sb", [P, P])
        group_before = sb("group_before_sb", [P, P])
        sign = sb("sign_sb", [P, 2])
        eps = sb("eps", [P, 1])
        c_sb = sb("c_sb", [P, DC, B])
        c_exp = sb("c_exp", [P, DC, B])
        siluT = sb("siluT", [P, DC, B])
        modT = sb("modT", [P, 4, DC, B])
        stats = sb("stats", [P, TB, 6])
        mean_var = sb("mean_var", [P, TB, 2])
        std = sb("std", [P, TB])
        shift = sb("shift", [P, TB])
        wr_sb = sb("wr_sb", [P, DC, E])
        sD_sb = sb("sD_sb", [HEADS, 1])
        digit_int = sb("digit_int_sb", [P, 3 * BITS // 2 + 3], I32)
        digit_unit = sb("digit_unit_sb", [P, BITS // 2])
        reached = sb("reached", [P, 3])
        digit = sb("digit", [P, 1])
        expert_id = sb("expert_id_sb", [P, E])
        slot_base = sb("slot_base_sb", [P, 1])
        trash_slot = sb("trash_slot_sb", [P, TILES])
        theta = sb("theta", [P, 1], I32)
        base = sb("base", [P, 3], I32)
        cand = sb("cand", [P, 3], I32)
        accepted = sb("accepted", [P, 1], I32)
        count = sb("count", [P, 3])
        need = sb("need", [P, 1])
        row_total = sb("row_total", [P, 1])
        before = sb("before", [P, 1])
        weight = [sb(f"weight{r}", [P, TILES]) for r in range(2)]
        to_slot = [sb(f"to_slot{r}", [P, TILES], U32) for r in range(2)]
        from_slot = [sb(f"from_slot{r}", [P, TILES], U32) for r in range(2)]

        mod_dram = nc.dram_tensor("mod_scratch", [B, 4 * D], F32)
        ssm_dram = nc.dram_tensor("ssm_scratch", [HEADS, PAD], F32)
        xe_dram = nc.dram_tensor("xe_scratch", [SLOTS + TOKENS, D], F32)
        ye_dram = nc.dram_tensor("ye_scratch", [SLOTS, D], F32)

        stage_done = [sem(f"stage{k}_done") for k in range(8)]
        chain_v, chain_g = sem("vector_chain"), sem("gpsimd_chain")
        consts_in, c_in, w_qkv_in, kk_in, kD_in, ssm_in, wmod_in, bias_in, dft_in, idft_in = (
            sem(n) for n in ("consts_in", "c_in", "w_qkv_in", "kk_in", "kD_in", "ssm_in", "wmod_in",
                             "bias_in", "dft_in", "idft_in"))
        eps_set, exp_c, siluT_ready, modT_psum, modT_ready, mod_psum, mod_read, mod_ready, mod_out = (
            sem(n) for n in ("eps_set", "exp_c", "siluT_ready", "modT_psum", "modT_ready", "mod_psum", "mod_read",
                             "mod_ready", "mod_out"))
        ident_in, wo_in = sem("ident_in"), sem("wo_in")
        kkT_ready, kk_spec_psum, ssm_ready, ssm_out = (
            sem(n) for n in ("kkT_ready",
                             "kk_spec_psum", "ssm_ready", "ssm_out"))
        kk_copied, kk_spec_ready = sem("kk_copied"), sem("kk_spec_ready")
        x_in = [sem(f"x_in{i}") for i in range(2)]
        w_qkv_high, w_qkv_low, h_full_ready, hT_low = (
            sem(n) for n in ("w_qkv_high", "w_qkv_low", "h_full_ready", "hT_low"))
        var_ready, std_ready, x_shift_ready, h_ready, hT_psum, hT_high, qkv_psum, qkv_ready = (
            sem(n) for n in ("var_ready", "std_ready", "x_shift_ready", "h_ready", "hT_psum", "hT_high", "qkv_psum",
                             "qkv_ready"))
        spec_psum, spec_ready, parity_used, conv_psum, conv_ready, k_turned = (
            sem(n) for n in ("spec_psum", "spec_ready", "parity_used", "conv_psum", "conv_ready", "k_turned"))
        fold_ready = [[sem(f"fold_ready{parity}_{who}") for who in ("dve", "pool")] for parity in range(2)]
        toep_in = [sem(f"toep_in{i}") for i in range(2)]
        toep_high, toep_low, kv_ready, kv_high, kv_low, mix_psum, mix_read, zero_set, xe_zeroed, mod_d_in = (
            sem(n) for n in ("toep_high", "toep_low", "kv_ready", "kv_high", "kv_low", "mix_psum", "mix_read", "zero_set", "xe_zeroed", "mod_d_in"))
        x_again_in = [sem(f"x_again_in{i}") for i in range(2)]
        wo_ready, x_ready, yT_psum, yT_ready, attn_psum, x2_ready, var2_ready, std2_ready = (
            sem(n) for n in ("wo_ready", "x_ready", "yT_psum", "yT_ready", "attn_psum", "x2_ready",
                             "var2_ready", "std2_ready"))
        shift_ready, norm2_ready, scaled2, h2_ready, h2T_psum, h2T_ready, logit_psum, logit_ready = (
            sem(n) for n in ("shift_ready", "norm2_ready", "scaled2", "h2_ready", "h2T_psum", "h2T_ready",
                             "logit_psum", "logit_ready"))
        centred, exp_done, gate_ready, gateT_psum, count_ready, count_psum, slots_ready, slotT_psum = (
            sem(n) for n in ("centred", "exp_done", "gate_ready", "gateT_psum", "count_ready",
                             "count_psum", "slots_ready", "slotT_psum"))
        rows_out = [sem(f"rows_out{r}") for r in range(2)]
        w_high, w_low, xeT_high, xeT_low, hid_high, hid_low = (
            sem(n) for n in ("w_high", "w_low", "xeT_high", "xeT_low", "hid_high", "hid_low"))
        waited, to_slot_ready = sem("waited"), sem("to_slot_ready")
        w_in = [sem(f"w_in{i}") for i in range(2)]
        xe_in = [sem(f"xe_in{i}") for i in range(2)]
        xeT_psum, hid_psum, ye_psum, ye_ready = (sem(n) for n in ("xeT_psum", "hid_psum", "ye_psum", "ye_ready"))
        ye_out = [sem(f"ye_out{i}") for i in range(2)]
        low_rows_in = [sem(f"low_rows_in{b}") for b in range(B)]
        high_rows_in = [[sem(f"high_rows_in{b}_{half}") for half in range(2)] for b in range(B)]
        weighted, out_ready, out_stored = sem("weighted"), sem("out_ready"), sem("out_stored")

        modT_ps = ps[:, 0, 0:4 * DC * B].rearrange("p (m c b) -> p m c b", m=4, c=DC)
        tile_view = qkv[:, :, :].rearrange("p (t b) n -> p t b n", b=B)

        def rows_of(b, lo, hi):
            return tile_view[:, :, bass.ds(b, 1), lo:hi].rearrange("p t o n -> p t (o n)")

        def mod_of(table, b, m, shape):
            return table[:, bass.ds(b, 1), m, :].to_broadcast(shape)

        ALL = [P, TB, D]
        HALF_ROW = TB // 2
        u_tiles = u.rearrange("b (t p) d -> b p t d", p=P)
        out_tiles = out.rearrange("b (t p) d -> b p t d", p=P)

        def stage_end(eng, k):
            eng.drain().then_inc(stage_done[k], 1)
            eng.wait_ge(stage_done[k], 5)

        def backwards(v):
            last = v[:, v.shape[1] - 1:v.shape[1]]
            return bass.AP(last.tensor, last.offset, [last.ap[0], [-1, v.shape[1]]])

        kv_flat = [region(R1 + 2048 * i, 2048) for i in range(2)]

        def parity_tiles(v, parity):
            return v.rearrange("p (j o) h e -> p o j h e", o=2)[:, parity]

        kk_parity_view = kk_parity.rearrange("p (j h e) -> p j h e", j=JT, h=1)
        kk_view = kk_spec.unsqueeze(2)
        real, imag = slice(0, JR), slice(JR, JT)

        def join_parities(engine, dst, src, part, e):
            even, odd = (parity_tiles(src[:, part, :, e], o) for o in range(2))
            mid = part.start + JR // 2
            engine.tensor_tensor(dst[:, part.start:mid, :, e], even, odd, ALU.add)
            return engine.tensor_tensor(dst[:, mid:part.stop, :, e], even, odd, ALU.subtract)

        def folded(b, parity):
            return (folded_odd_0, folded_odd_1)[b % 2] if parity else folded_even

        def spectral_product(eng, engine, link, b, e, width):
            eng.wait_ge(spec_ready, JT * b + JT + 4)
            join_parities(engine, spec, parity_spec, real, e)
            link(join_parities(engine, spec, parity_spec, imag, e))
            eng.sem_inc(parity_used, 1)
            for i, (to, source) in enumerate(((real, imag), (imag, real))):
                factor = sign[:, 1 - i:2 - i]
                if engine is nc.vector:
                    last = engine.scalar_tensor_tensor(spec[:, to, 1, e], spec[:, source, 0, e], factor, spec[:, to, 1, e],
                                                       ALU.mult, ALU.add)
                else:
                    last = engine.tensor_scalar(tmp[i][:, :, 0, e], spec[:, source, 0, e], factor, None, ALU.mult)
            link(last)
            if engine is nc.gpsimd:
                for i, to in enumerate((real, imag)):
                    last = engine.tensor_tensor(spec[:, to, 1, e], spec[:, to, 1, e], tmp[i][:, :, 0, e], ALU.add)
                link(last)
            shape = [P, JR, 2, width]
            k_re, k_im = (kk_view[:, part, :, e].to_broadcast(shape) for part in (real, imag))
            s_re, s_im, t0, t1 = spec[:, real, :, e], spec[:, imag, :, e], tmp[0][:, :, :, e], tmp[1][:, :, :, e]
            engine.tensor_tensor(t0, k_re, s_re, ALU.mult)
            link(engine.tensor_tensor(t1, k_im, s_im, ALU.mult))
            link(engine.tensor_tensor(t0, t0, t1, ALU.subtract))
            engine.tensor_tensor(t1, k_re, s_im, ALU.mult)
            link(engine.tensor_tensor(s_re, k_im, s_re, ALU.mult))
            link(engine.tensor_tensor(s_im, t1, s_re, ALU.add))
            for parity, op in enumerate((ALU.add, ALU.subtract)):
                if b >= 1 and parity == 0:
                    eng.wait_ge(conv_psum, CT * (b - 1) + CT // 2)
                for part, v in enumerate((t0, s_im)):
                    j = part * JP // 2
                    last = engine.tensor_tensor(folded(b, parity)[:, j:j + JP // 2, :, e], v[:, 0:JP // 2], v[:, JP // 2:JP], op)
                link(last)
                eng.sem_inc(fold_ready[parity][engine is nc.gpsimd], 1)

        def w_piece(q, part, piece):
            table = (w1_parts if piece < PIECES // 2 else w2_parts)[q][part]
            start = PIECE * (piece % (PIECES // 2))
            return table[:, start:start + PIECE].rearrange("p (s f) -> p s f", f=D)

        def raw_piece(q, piece):
            return w_raw[q][:, 2 * piece:2 * piece + 2]

        block = ctx.enter_context(nc.Block())

        @block.sync
        def _(sp):
            sp.dma_start(c_sb[:], cT.rearrange("(c p) b -> p c b", p=P)).then_inc(c_in, 16)
            for dc in range(DC):
                sp.dma_start(wmod_sb[dc], wmod[dc * P:(dc + 1) * P, :]).then_inc(wmod_in, 16)
            sp.dma_start(x_buf[0], u_tiles[0]).then_inc(x_in[0], 16)
            sp.dma_start(ident[:], K["ident"]).then_inc(ident_in, 16)
            sp.dma_start(kkT.rearrange("p (c o) e -> p c (o e)", o=2),
                         k_taps.rearrange("(c p o) e -> p c (o e)", p=P, o=2)).then_inc(kk_in, 16)
            sp.dma_start(dft, K["dft"].rearrange("(c p) m -> p c m", p=P)).then_inc(dft_in, 16)
            sp.dma_start(x_buf[1], u_tiles[1]).then_inc(x_in[1], 16)
            sp.dma_start(wqkvT, w_qkv.rearrange("(c p) n -> p c n", p=P)).then_inc(w_qkv_in, 16)
            sp.dma_start(bias, b_all.to_broadcast([P, 4 * D])).then_inc(bias_in, 16)
            sp.wait_ge(ssm_ready, 2)
            sp.dma_start(ssm_dram[:, :], ssm_pad[0:HEADS, :]).then_inc(ssm_out, 16)
            sp.dma_start(idft, K["idft"].rearrange("(j p) t -> p j t", p=P)).then_inc(idft_in, 16)
            for dst, name in ((sign, "sign"), (group_ones, "group_ones"),
                              (group_before, "group_before"), (digit_int, "digit_int"),
                              (digit_unit, "digit_unit"), (expert_id, "expert_id"),
                              (slot_base, "slot_base"), (trash_slot, "trash_slot")):
                sp.dma_start(dst[:], K[name]).then_inc(consts_in, 16)
            sp.dma_start(wr_sb[:], Wr.rearrange("(c p) e -> p c e", p=P)).then_inc(consts_in, 16)
            for b in range(2, B):
                sp.wait_ge(hT_psum, 4 * (b - 1))
                sp.dma_start(x_buf[b % 2], u_tiles[b]).then_inc(x_in[b % 2], 16)
            sp.wait_ge(mod_ready, 1)
            sp.dma_start(mod_dram[:, :], mod_row[0:B, :]).then_inc(mod_out, 16)
            sp.wait_ge(ssm_out, 16)
            sp.wait_ge(mod_out, 16)
            sp.wait_ge(consts_in, 16 * 9)
            sp.wait_ge(idft_in, 16)
            stage_end(sp, 0)
            def load_toeplitz(h):
                shifted = bass.AP(ssm_dram, h * PAD, [[1, P], [1, TOEP]])
                sp.dma_start(toep_raw[h % 2], shifted).then_inc(toep_in[h % 2], 16)

            with sp.Fori(0, B) as b:
                for parity in range(2):
                    sp.wait_ge(conv_ready, CT * b + CT + (parity + 1) * CT // 2)
                    for half in range(2):
                        dst = tile_view[parity::2, half::2, bass.ds(b, 1), 2 * D:3 * D].rearrange("p t o n -> p t (o n)")
                        sp.dma_start(dst, k_stage[half * P // 2:(half + 1) * P // 2, parity::2]).then_inc(k_turned, 16)
            sp.wait_ge(parity_used, 2 * B + 2)
            load_toeplitz(0)
            load_toeplitz(1)
            sp.wait_ge(k_turned, 64 * (B + 1))
            stage_end(sp, 1)

            for h in range(HEADS):
                if h >= 2:
                    sp.wait_ge(toep_low, h - 1)
                    load_toeplitz(h)
                if h == 1:
                    sp.dma_start(woT, w_out.rearrange("(c p) n -> p c n", p=P)).then_inc(wo_in, 16)
                    for b in range(B):
                        sp.dma_start(mod_d[:, b].rearrange("p m d -> p (m d)"),
                                     mod_dram[b:b + 1, :].to_broadcast([P, 4 * D])).then_inc(mod_d_in, 16)
                    sp.wait_ge(zero_set, 1)
                if 1 <= h <= 10:
                    r = SLOTS // 10
                    sp.dma_start(xe_dram[(h - 1) * r:h * r, :].rearrange("(p n) d -> p (n d)", p=P),
                                 zero).then_inc(xe_zeroed, 16)
            sp.wait_ge(xe_zeroed, 160)
            stage_end(sp, 2)

            for b in range(B):
                if b >= 2:
                    sp.wait_ge(x2_ready, b - 1)
                sp.dma_start(x_again[b % 2], u_tiles[b]).then_inc(x_again_in[b % 2], 16)
            stage_end(sp, 3)
            xe_rows = xe_dram[0:SLOTS, :].rearrange("(n t p) d -> n p t d", t=GT, p=P)
            ye_rows = ye_dram[:, :].rearrange("(n t p) d -> n p t d", t=GT, p=P)
            w1_rows = W1.rearrange("e (c p) (s f) -> e p c s f", p=P, f=D)
            w2_rows = W2.rearrange("e (c p) n -> e p c n", p=P)

            def load_weights(e, q):
                for c in range(DC):
                    sp.dma_start(w_raw[q][:, 4 * c:4 * c + 4],
                                 w1_rows[bass.ds(e, 1), :, c].rearrange("o p s f -> (o p) s f")).then_inc(w_in[q], 16)
                sp.dma_start(w_raw[q][:, 8:16],
                             w2_rows[bass.ds(e, 1)].rearrange("o p c n -> (o p) c n")).then_inc(w_in[q], 16)

            def load_rows(n, s):
                sp.wait_ge(xeT_psum, n + 1)
                sp.dma_start(xe[s], xe_rows[bass.ds(n, 1)].rearrange("o p t d -> (o p) t d")).then_inc(xe_in[s], 16)

            def store_rows(n, s):
                sp.wait_ge(ye_ready, n + 1)
                sp.dma_start(ye_rows[bass.ds(n, 1)].rearrange("o p t d -> (o p) t d"), y_sb[s]).then_inc(ye_out[s], 16)

            def groups(pair, ks):
                for k in ks:
                    e, n = pair * 2 + k // GROUPS, pair * 2 * GROUPS + k
                    if ks is PAIR and k % GROUPS == 0:
                        sp.wait_ge(w_low, PIECES * e)
                        load_weights(e + 1, (k // GROUPS + 1) % 2)
                    if ks is FIRST and k + 2 == GROUPS:
                        sp.wait_ge(rows_out[1], 16 * TILES)
                    if ks is not LAST or k + 2 < 2 * GROUPS:
                        load_rows(n + 2, k % 2)
                    store_rows(n, k % 2)

            for e in range(2):
                load_weights(e, e)
            stage_end(sp, 4)
            sp.wait_ge(rows_out[0], 16 * TILES)
            load_rows(0, 0)
            load_rows(1, 1)
            groups(0, FIRST)
            with sp.Fori(0, PAIRS) as pair:
                groups(pair, PAIR)
            groups(PAIRS, LAST)

            for b in range(B):
                for half in range(2):
                    sp.wait_ge(out_ready, 2 * b + half + 1)
                    tiles = slice(half * HALF_ROW, (half + 1) * HALF_ROW)
                    sp.dma_start(out_tiles[b, :, tiles], tile_view[:, tiles, b, 0:D]).then_inc(out_stored, 16)
            sp.wait_ge(out_stored, 16 * 2 * B)

        @block.gpsimd
        def _(pool):
            chain = Chain(pool, chain_g)
            chain.link(nc.gpsimd.memset(ssm_pad[0:HEADS, :], 0.0))
            pool.dma_start(ssm_pad[0:HEADS, P:P + TAPS], ssm).then_inc(ssm_in, 16)
            pool.dma_start(sD_sb[:], sD.rearrange("(h o) -> h o", o=1)).then_inc(ssm_in, 16)
            pool.dma_start(kD_row[0:1, :], kD.rearrange("(o d) -> o d", o=1)).then_inc(kD_in, 16)
            pool.wait_ge(ssm_in, 32)
            nc.gpsimd.tensor_tensor(ssm_pad[0:HEADS, TOEP - 1:TOEP], ssm_pad[0:HEADS, TOEP - 1:TOEP], sD_sb[:],
                                    ALU.add).then_inc(ssm_ready, 2)
            pool.wait_ge(kk_in, 16)
            pool.wait_ge(kD_in, 16)
            nc.gpsimd.tensor_tensor(kkT[0:1, 0, :], kkT[0:1, 0, :], kD_row[0:1, :], ALU.add).then_inc(kkT_ready, 1)
            for dc in range(DC):
                pool.wait_ge(w_qkv_high, dc + 1)
                if dc == 1:
                    pool.wait_ge(ssm_out, 16)
                nc.gpsimd.tensor_tensor(wqkv_parts[dc][1][:], wqkvT[:, dc], wqkv_parts[dc][0][:].bitcast(F32),
                                        ALU.subtract).then_inc(w_qkv_low, 1)
            for b in range(B):
                for g in range(4):
                    high, low = (hT_parts[b % 2][a][:, g % 2, g // 2 * BANK:(g // 2 + 1) * BANK] for a in range(2))
                    pool.wait_ge(hT_high, 4 * b + g + 1)
                    nc.gpsimd.tensor_tensor(low, h_full[g % 2], high.bitcast(F32), ALU.subtract).then_inc(hT_low, 1)
            stage_end(pool, 0)
            pool.wait_ge(kk_spec_ready, 1)
            for b in range(B):
                spectral_product(pool, nc.gpsimd, chain.link, b, slice(SPLIT, D), D - SPLIT)
            stage_end(pool, 1)
            nc.gpsimd.memset(zero, 0.0).then_inc(zero_set, 1)

            with pool.Fori(0, HEADS // 2) as hh:
                for s in range(2):
                    h = hh * 2 + s
                    pool.wait_ge(toep_high, h + 1)
                    nc.gpsimd.tensor_tensor(toep_parts[s][1][:], backwards(toep_raw[s]), toep_parts[s][0][:].bitcast(F32),
                                            ALU.subtract).then_inc(toep_low, 1)
                    for g in range(4):
                        pool.wait_ge(kv_high, 4 * h + g + 1)
                        quarter = slice(512 * g, 512 * g + 512)
                        nc.gpsimd.tensor_tensor(kv_parts[s][1][:, quarter], kv_flat[s][:, quarter],
                                                kv_parts[s][0][:, quarter].bitcast(F32), ALU.subtract).then_inc(kv_low, 1)
            stage_end(pool, 2)

            def prepare_row(b):
                s = b % 2
                if b >= 2:
                    pool.wait_ge(x2_ready, b - 1)
                nc.gpsimd.tensor_tensor(wo_gated[s], woT, mod_d[:, b, 0:1, :].to_broadcast([P, DC, D]), ALU.mult).then_inc(wo_ready, 1)
                nc.gpsimd.tensor_tensor(bo_gated[s], bias[:, 3 * D:4 * D], mod_d[:, b, 0, :], ALU.mult).then_inc(wo_ready, 1)
                pool.wait_ge(wo_ready, 2 * b + 2)
                pool.wait_ge(x_again_in[s], 16 * (b // 2 + 1))
                nc.gpsimd.tensor_tensor(x_again[s], x_again[s], bo_gated[s].unsqueeze(1).to_broadcast(ALL), ALU.add).then_inc(x_ready, 1)

            pool.wait_ge(mod_d_in, 16 * B)
            pool.wait_ge(wo_in, 16)
            prepare_row(0)
            prepare_row(1)
            def shift_rows(b):
                pool.wait_ge(scaled2, b + 1)
                h2 = rows_of(b, 2 * D, 3 * D)
                nc.gpsimd.tensor_tensor(h2, h2, mod_d[:, b, 1:2, :].to_broadcast(ALL), ALU.add).then_inc(h2_ready, 1)

            for b in range(B):
                if b + 2 < B:
                    prepare_row(b + 2)
                if b + 1 < B:
                    shift_rows(b)
            stage_end(pool, 3)
            shift_rows(B - 1)

            def weights_low(e, q, pieces):
                for piece in pieces:
                    pool.wait_ge(w_high, PIECES * e + piece + 1)
                    nc.gpsimd.tensor_tensor(w_piece(q, 1, piece), raw_piece(q, piece), w_piece(q, 0, piece).bitcast(F32),
                                            ALU.subtract).then_inc(w_low, 1)

            for e in range(2):
                weights_low(e, e, range(PIECES))
            pool.wait_ge(xe_zeroed, 160)
            pool.wait_ge(h2_ready, B)
            for r in range(2):
                pool.wait_ge(to_slot_ready, r + 1)
                for tile in range(TILES):
                    nc.gpsimd.indirect_dma_start(
                        xe_dram[:, :], bass.IndirectOffsetOnAxis(ap=to_slot[r][:, tile:tile + 1], axis=0),
                        qkv[:, tile, 2 * D:3 * D], None).then_inc(rows_out[r], 16)
                if r == 0:
                    stage_end(pool, 4)

            with pool.Fori(0, PAIRS) as pair:
                for q in range(2):
                    weights_low(pair * 2 + q + 2, q, range(PIECES))

            def gather(r, tile, source, signal):
                nc.gpsimd.indirect_dma_start(
                    qkv[:, tile, 2 * D * (1 - r):2 * D * (1 - r) + D], None, source,
                    bass.IndirectOffsetOnAxis(ap=from_slot[r][:, tile:tile + 1], axis=0)).then_inc(signal, 16)

            def wait_stored(groups):
                for s in range(2):
                    pool.wait_ge(ye_out[s], 16 * ((groups + 1 - s) // 2 + 1))

            wait_stored((E - 1) * GROUPS)
            pool.wait_ge(rows_out[0], 16 * TILES)
            pool.wait_ge(rows_out[1], 16 * TILES)
            for b in range(B):
                for t in range(TB):
                    gather(0, t * B + b, ye_dram[0:SLOTS - CAP, :], low_rows_in[b])
            assert L <= CAP - GROUP
            wait_stored(E * GROUPS - 1)
            for t in range(TB):
                gather(1, t * B, ye_dram[0:SLOTS - GROUP, :], high_rows_in[0][t // HALF_ROW])
            wait_stored(E * GROUPS)
            for b in range(1, B):
                for t in range(TB):
                    gather(1, t * B + b, ye_dram[:, :], high_rows_in[b][t // HALF_ROW])
            for b in range(B):
                pool.wait_ge(low_rows_in[b], 16 * TB)
                for half in range(2):
                    pool.wait_ge(high_rows_in[b][half], 16 * HALF_ROW)

        @block.scalar
        def _(act):
            def copy(dst, src):
                return nc.scalar.activation(dst, src, ACT.Copy)

            act.wait_ge(c_in, 16)
            nc.scalar.activation(c_exp[:], c_sb[:], ACT.Exp, scale=-1.0).then_inc(exp_c, 1)
            act.wait_ge(eps_set, 1)
            def normalize_x(b):
                x = x_buf[b % 2]
                act.wait_ge(var_ready, b + 1)
                nc.scalar.activation(std[:], mean_var[:, :, 1], ACT.Sqrt, bias=eps[:]).then_inc(std_ready, 1)
                act.wait_ge(x_shift_ready, b + 1)
                for t in range(TB):
                    last = nc.scalar.activation(x[:, t, :], x[:, t, :], ACT.Identity,
                                                scale=std[:, t:t + 1], bias=shift[:, t:t + 1])
                last.then_inc(h_ready, 1)

            def h_high(b):
                for g in range(4):
                    half, dc = g // 2, g % 2
                    act.wait_ge(h_full_ready, 4 * b + g + 1)
                    copy(hT_parts[b % 2][0][:, dc, half * BANK:(half + 1) * BANK], h_full[g % 2]).then_inc(hT_high, 1)

            normalize_x(0)
            act.wait_ge(w_qkv_in, 16)
            for dc in range(DC):
                copy(wqkv_parts[dc][0][:], wqkvT[:, dc]).then_inc(w_qkv_high, 1)
            for half in range(2):
                act.wait_ge(kk_spec_psum, half + 1)
                nc.scalar.activation(kk_parity[:, 1024 * half:1024 * half + 1024],
                                     ps[:, 4 + 2 * half:6 + 2 * half].rearrange("p a n -> p (a n)"),
                                     ACT.Copy, scale=1.0 / HALF).then_inc(kk_copied, 1)
            for b in range(B):
                h_high(b)
                if b + 1 < B:
                    normalize_x(b + 1)
            stage_end(act, 0)

            def spec_out(b):
                for j in range(JT):
                    act.wait_ge(spec_psum, JT * b + j + 1)
                    if j == 0:
                        act.wait_ge(parity_used, 2 * b + 2)
                    copy(parity_spec[:, j].rearrange("p h e -> p (h e)"), ps[:, j % 4]).then_inc(spec_ready, 1)

            def conv_out(b):
                for i, c in enumerate(BY_PARITY):
                    act.wait_ge(conv_psum, CT * b + i + 1)
                    if i == 0:
                        act.wait_ge(k_turned, 64 * b + 64)
                    copy(k_stage[:, c::CT], ps[:, 4 + c].rearrange("p (h e) -> p h e", h=2)).then_inc(conv_ready, 1)

            spec_out(0)
            spec_out(1)
            conv_out(0)
            spec_out(2)
            spec_out(3)
            for b in range(1, B):
                conv_out(b)
            stage_end(act, 1)

            with act.Fori(0, HEADS // 2) as hh:
                for s in range(2):
                    h = hh * 2 + s
                    act.wait_ge(toep_in[s], 16 * hh + 16)
                    act.wait_ge(mix_psum, 4 * h + 1)
                    copy(toep_parts[s][0][:], backwards(toep_raw[s])).then_inc(toep_high, 1)
                    for g in range(4):
                        act.wait_ge(kv_ready, 4 * h + g + 1)
                        quarter = slice(512 * g, 512 * g + 512)
                        copy(kv_parts[s][0][:, quarter], kv_flat[s][:, quarter]).then_inc(kv_high, 1)
            stage_end(act, 2)

            def y_turned(b):
                for g in range(4):
                    act.wait_ge(yT_psum, 4 * b + g + 1)
                    copy(yT[:, g // 2, (g % 2) * BANK:(g % 2 + 1) * BANK], ps[:, 4 + g % 2]).then_inc(yT_ready, 1)

            def normalize(b):
                act.wait_ge(var2_ready, b + 1)
                nc.scalar.activation(std[:], mean_var[:, :, 1], ACT.Sqrt, bias=eps[:]).then_inc(std2_ready, 1)
                act.wait_ge(shift_ready, b + 1)
                for t in range(TB):
                    last = nc.scalar.activation(tile_view[:, t, b, 2 * D:3 * D], tile_view[:, t, b, D:2 * D], ACT.Identity,
                                                scale=std[:, t:t + 1], bias=shift[:, t:t + 1])
                last.then_inc(norm2_ready, 1)

            def h2_turned(b):
                for g in range(4):
                    dc = g // 2
                    act.wait_ge(h2T_psum, 4 * b + g + 1)
                    nc.scalar.activation(h2T[:, dc, (g % 2) * BANK:(g % 2 + 1) * BANK], ps[:, 6 + g % 2], ACT.Identity,
                                         scale=modT[:, 3, dc, b:b + 1], bias=modT[:, 1, dc, b:b + 1]).then_inc(h2T_ready, 1)

            def exponentials(b):
                act.wait_ge(centred, b + 1)
                of_row = [v.rearrange("p (t b) e -> p t b e", b=B)[:, :, b] for v in (probs, logits)]
                nc.scalar.activation(*of_row, ACT.Exp).then_inc(exp_done, 1)

            y_turned(0)
            y_turned(1)
            normalize(0)
            for b in range(B):
                h2_turned(b)
                if b + 2 < B:
                    y_turned(b + 2)
                if b + 1 < B:
                    normalize(b + 1)
                if b + 2 < B:
                    exponentials(b)
            for b in (B - 2, B - 1):
                exponentials(b)
            stage_end(act, 3)


            def weights_high(e, q, pieces):
                for piece in pieces:
                    copy(w_piece(q, 0, piece), raw_piece(q, piece)).then_inc(w_high, 1)

            for e in range(2):
                act.wait_ge(w_in[e], 48)
                weights_high(e, e, range(PIECES))
            stage_end(act, 4)

            def weight_rows(b):
                act.wait_ge(low_rows_in[b], 16 * TB)
                for t in range(TB):
                    tile = t * B + b
                    row = qkv[:, tile, 2 * D:3 * D]
                    last = nc.scalar.activation(row, row, ACT.Copy, scale=weight[0][:, tile:tile + 1])
                last.then_inc(weighted, 1)

            def groups(pair, ks):
                for k in ks:
                    e, g, n = pair * 2 + k // GROUPS, k % GROUPS, pair * 2 * GROUPS + k
                    for a in range(4):
                        act.wait_ge(hid_psum, 4 * n + a + 1)
                        nc.scalar.activation(hid_parts[0][:, 512 * a:512 * a + 512], ps[:, a], ACT.Relu).then_inc(hid_high, 1)
                    if ks is not LAST or g < GROUPS - 1:
                        act.wait_ge(xeT_psum, n + 4)
                        copy(xeT_parts[0][:], ps[:, 6]).then_inc(xeT_high, 1)
                    if ks is PAIR and g < 4:
                        q = (k // GROUPS + 1) % 2
                        if g == 0:
                            act.wait_ge(w_in[q], 48 * (pair + (k // GROUPS + 1) // 2 + 1))
                        weights_high(e + 1, q, range(2 * g, 2 * g + 2))
                    if ks is LAST:
                        for b in {2: (0,), 3: (1, 2), 4: (3,)}.get(g, ()):
                            weight_rows(b)

            act.wait_ge(xeT_psum, 3)
            copy(xeT_parts[0][:], ps[:, 6]).then_inc(xeT_high, 1)
            groups(0, FIRST)
            with act.Fori(0, PAIRS) as pair:
                groups(pair, PAIR)
            groups(PAIRS, LAST)

        @block.vector
        def _(dve):
            chain = Chain(dve, chain_v)
            link = chain.link

            def tt(o, a, b_, op):
                return nc.vector.tensor_tensor(o, a, b_, op)

            def tile_stats(b, t):
                return nc.vector.bn_stats(stats[:, t, :], x_buf[b % 2][:, t, :])

            def row_stats(b):
                dve.wait_ge(x_in[b % 2], 16 * (b // 2 + 1))
                for t in range(TB):
                    last = tile_stats(b, t)
                link(last)

            def finish_stats(b):
                if b >= 1:
                    dve.wait_ge(h_ready, b)
                for t in range(TB):
                    last = nc.vector.bn_aggr(mean_var[:, t, :], stats[:, t, :])
                last.then_inc(var_ready, 1)
                dve.wait_ge(std_ready, b + 1)
                link(nc.vector.reciprocal(std[:], std[:]))
                dve.wait_ge(var_ready, b + 1)
                nc.vector.scalar_tensor_tensor(shift[:], mean_var[:, :, 0], -1.0, std[:], ALU.mult, ALU.mult).then_inc(x_shift_ready, 1)
                dve.wait_ge(x_shift_ready, b + 1)

            def h_rows(b):
                for g in range(4):
                    dc = g % 2
                    dve.wait_ge(hT_psum, 4 * b + g + 1)
                    if 4 * b + g >= 2:
                        dve.wait_ge(hT_low, 4 * b + g - 1)
                    nc.vector.tensor_scalar(h_full[g % 2], ps[:, g], modT[:, 2, dc, b:b + 1], modT[:, 0, dc, b:b + 1],
                                            ALU.mult, ALU.add).then_inc(h_full_ready, 1)

            def clamp(m):
                v = mod_row[0:B, m * D:(m + 1) * D]
                link(nc.vector.tensor_scalar(clamp_b[0:B, :], v, -1.0, None, ALU.mult))
                nc.vector.tensor_scalar(clamp_a[0:B, :], v, 0.0, 2.0, ALU.is_ge, ALU.mult)
                link(tt(clamp_b[0:B, :], clamp_b[0:B, :], v, ALU.max))
                nc.vector.tensor_scalar_max(clamp_b[0:B, :], clamp_b[0:B, :], 0.25)
                link(nc.vector.tensor_scalar_add(clamp_a[0:B, :], clamp_a[0:B, :], -1.0))
                link(tt(v, clamp_a[0:B, :], clamp_b[0:B, :], ALU.mult))

            def qkv_out(b):
                for t in range(TB):
                    if t == TB // 4 and b >= 2:
                        clamp((GA - 2, GB - 2)[b - 2])
                    if t == TB // 2 and b + 1 < B:
                        h_rows(b + 1)
                    dve.wait_ge(qkv_psum, TB * b + t + 1)
                    bank = 4 + 2 * (t % 2)
                    tt(qkv[:, t * B + b, :], ps[:, bank:bank + 2].rearrange("p a n -> p (a n)")[:, 0:3 * D], bias[:, 0:3 * D],
                       ALU.add).then_inc(qkv_ready, 1)
                    if b + 2 < B:
                        if t == 0:
                            dve.wait_ge(x_in[b % 2], 16 * (b // 2 + 2))
                        last = tile_stats(b + 2, t)
                if b + 2 < B:
                    link(last)

            dve.sem_inc(spec_ready, 4)
            dve.sem_inc(parity_used, 2)
            dve.sem_inc(k_turned, 64)
            dve.sem_inc(conv_ready, CT)
            dve.sem_inc(mix_read, 8)
            dve.sem_inc(mix_psum, 5)
            dve.sem_inc(ye_psum, 1)
            dve.sem_inc(xeT_psum, 2)
            for s in range(2):
                dve.sem_inc(ye_out[s], 16)
            nc.vector.memset(eps[:], EPS).then_inc(eps_set, 1)
            dve.wait_ge(exp_c, 1)
            link(nc.vector.tensor_scalar_add(c_exp[:], c_exp[:], 1.0))
            link(nc.vector.reciprocal(c_exp[:], c_exp[:]))
            tt(siluT[:], c_sb[:], c_exp[:], ALU.mult).then_inc(siluT_ready, 1)
            row_stats(0)
            finish_stats(0)
            dve.wait_ge(modT_psum, 1)
            nc.vector.tensor_copy(modT[:, 0:2], modT_ps[:, 0:2]).then_inc(modT_ready, 1)
            nc.vector.tensor_scalar_add(modT[:, 2:4], modT_ps[:, 2:4], 1.0).then_inc(modT_ready, 1)
            dve.wait_ge(mod_psum, 2)
            nc.vector.tensor_copy(mod_row[0:B, :], ps[0:B, 1:3].rearrange("p a n -> p (a n)")).then_inc(mod_read, 1)
            dve.wait_ge(mod_read, 1)
            row_stats(1)
            h_rows(0)
            finish_stats(1)
            v = mod_row[0:B, 2 * D:3 * D]
            link(nc.vector.tensor_scalar_add(v, v, 1.0))
            dve.wait_ge(bias_in, 16)
            for b in range(B):
                qkv_out(b)
                if b + 2 < B:
                    finish_stats(b + 2)
            dve.sem_inc(mod_ready, 1)
            stage_end(dve, 0)

            for part in (real, imag):
                last = join_parities(nc.vector, kk_view, kk_parity_view, part, slice(0, D))
            link(last)
            dve.sem_inc(kk_spec_ready, 1)
            for b in range(B):
                spectral_product(dve, nc.vector, link, b, slice(0, SPLIT), SPLIT)
            stage_end(dve, 1)

            def products(h, s):
                for g in range(4):
                    tiles = slice(8 * g, 8 * g + 8)
                    k_i = qkv[:, tiles, bass.ds(h * NJ + 2 * D, NJ)].unsqueeze(3).to_broadcast([P, 8, NJ, NJ])
                    v_j = qkv[:, tiles, bass.ds(h * NJ + D, NJ)].unsqueeze(2).to_broadcast([P, 8, NJ, NJ])
                    tt(kv_buf[s][:, tiles], k_i, v_j, ALU.mult).then_inc(kv_ready, 1)

            def gate_and_sum(h, s):
                for g in range(4):
                    tiles = slice(8 * g, 8 * g + 8)
                    q_i = qkv[:, tiles, bass.ds(h * NJ, NJ)].unsqueeze(3).to_broadcast([P, 8, NJ, NJ])
                    dve.wait_ge(mix_psum, 4 * h + g + 6)
                    tt(qy[g], ps[:, 4 * s + g].rearrange("p (t i j) -> p t i j", t=8, i=NJ), q_i,
                       ALU.mult).then_inc(mix_read, 1)
                    dve.wait_ge(mix_read, 4 * h + g + 1 + 8)
                    dve.sem_inc(waited, 1)
                    nc.vector.tensor_reduce(qkv[:, tiles, bass.ds(h * NJ, NJ)],
                                            qy[g].rearrange("p t i j -> p t j i"), AX.X, ALU.add)

            products(0, 0)
            products(1, 1)
            with dve.Fori(0, HEADS // 2 - 1) as hh:
                for s in range(2):
                    gate_and_sum(hh * 2 + s, s)
                    products(hh * 2 + s + 2, s)
            for s in range(2):
                gate_and_sum(HEADS - 2 + s, s)
            stage_end(dve, 2)

            def residual(b):
                dve.wait_ge(attn_psum, b + 1)
                dve.wait_ge(x_ready, b + 1)
                att = ps[:, 0:4].rearrange("p a n -> p (a n)").rearrange("p (t d) -> p t d", t=TB)
                tt(rows_of(b, D, 2 * D), att, x_again[b % 2], ALU.add).then_inc(x2_ready, 1)
                dve.wait_ge(x2_ready, b + 1)
                if b >= 1:
                    dve.wait_ge(norm2_ready, b)
                for t in range(TB):
                    last = nc.vector.bn_stats(stats[:, t, :], tile_view[:, t, b, D:2 * D])
                link(last)
                for t in range(TB):
                    last = nc.vector.bn_aggr(mean_var[:, t, :], stats[:, t, :])
                last.then_inc(var2_ready, 1)
                dve.wait_ge(std2_ready, b + 1)
                link(nc.vector.reciprocal(std[:], std[:]))
                dve.wait_ge(var2_ready, b + 1)
                nc.vector.scalar_tensor_tensor(shift[:], mean_var[:, :, 0], -1.0, std[:], ALU.mult, ALU.mult).then_inc(shift_ready, 1)
                dve.wait_ge(shift_ready, b + 1)

            def scale_rows(b):
                dve.wait_ge(h2T_psum, 4 * b + 4)
                h2 = rows_of(b, 2 * D, 3 * D)
                tt(h2, h2, mod_d[:, b, 2:3, :].to_broadcast(ALL), ALU.mult).then_inc(scaled2, 1)

            def of_row(v, b):
                return v.rearrange("p (t b) e -> p t b e", b=B)[:, :, b] if len(v.shape) == 3 else v.rearrange("p (t b) -> p t b", b=B)[:, :, b]

            ROW = [P, TB, E]

            def centre_logits(b):
                row, greatest = of_row(logits, b), of_row(row_max, b)
                dve.wait_ge(logit_psum, b + 1)
                nc.vector.tensor_copy(row, ps[:, LOGIT_BANK[b], 0:TB * E].rearrange("p (t e) -> p t e", t=TB)).then_inc(logit_ready, 1)
                dve.wait_ge(logit_ready, b + 1)
                link(nc.vector.tensor_reduce(greatest, row, AX.X, ALU.max))
                tt(row, row, greatest.unsqueeze(2).to_broadcast(ROW), ALU.subtract).then_inc(centred, 1)

            def choose_experts(b):
                prob, total, lower = of_row(probs, b), of_row(row_sum, b), of_row(row_max, b)
                dve.wait_ge(exp_done, b + 1)
                link(nc.vector.tensor_reduce(total, prob, AX.X, ALU.add))
                link(nc.vector.reciprocal(total, total))
                link(tt(prob, prob, total.unsqueeze(2).to_broadcast(ROW), ALU.mult))
                for t in range(b, TILES, B):
                    last = nc.vector.max(top_v[:, t, :], probs[:, t, :])
                link(last)
                for t in range(b, TILES, B):
                    last = nc.vector.max_index(top_i[:, t, :], top_v[:, t, :], probs[:, t, :])
                link(last)
                index = of_row(top_f, b)
                link(nc.vector.tensor_copy(index, of_row(top_i, b)))
                ids = expert_id[:].unsqueeze(1).to_broadcast(ROW)
                for which, op in ((lower, ALU.min), (total, ALU.max)):
                    last = tt(which, index[:, :, 0], index[:, :, 1], op)
                link(last)
                for which, mask in ((lower, first), (total, second)):
                    last = tt(of_row(mask, b), ids, which.unsqueeze(2).to_broadcast(ROW), ALU.is_equal)
                link(last)
                gate, mark = of_row(picked, b), of_row(routed, b)
                for r, mask in enumerate((first, second)):
                    link(tt(gate, prob, of_row(mask, b), ALU.mult))
                    link(nc.vector.tensor_reduce(of_row(weight[r][:], b), gate, AX.X, ALU.add))
                link(tt(mark, of_row(first, b), of_row(second, b), ALU.add))
                link(tt(gate, prob, mark, ALU.mult))
                link(nc.vector.tensor_scalar_add(mark, mark, -1.0))
                for r in range(2):
                    last = tt(gate_cols[:, r, :, b].rearrange("p e q -> p q e"), gate[:, r::2], mark[:, r::2], ALU.add)
                last.then_inc(gate_ready, 1)

            dve.wait_ge(mod_d_in, 16 * B)
            residual(0)
            residual(1)
            for b in range(B):
                scale_rows(b)
                if b == B - 1:
                    choose_experts(b - 1)
                centre_logits(b)
                if b + 2 < B:
                    residual(b + 2)
                    choose_experts(b)
            choose_experts(B - 1)
            stage_end(dve, 3)

            nc.vector.memset(theta[:], 0)
            nc.vector.memset(ones_l, 1.0)
            nc.vector.memset(accepted[:], 0)
            nc.vector.tensor_copy(base[:], digit_int[:, 0:3])
            dve.wait_ge(gateT_psum, 1)
            link(nc.vector.tensor_copy(gate_l, ps[:, 0, 0:256]))
            with chain.loop(BITS // 2 // ROUNDS, 4 * ROUNDS) as turn:
                for i in range(ROUNDS):
                    n = turn * ROUNDS + i
                    link(tt(cand[:], base[:], accepted[:].to_broadcast([P, 3]), ALU.bitwise_or))
                    for d in range(3):
                        last = nc.vector.tensor_scalar(junk[d], gate_l, cand[:, d:d + 1].bitcast(F32), None, ALU.is_ge, ALU.add,
                                                       accum_out=count[:, d:d + 1])
                    last.then_inc(count_ready, 1)
                    link(tt(theta[:], theta[:], accepted[:], ALU.bitwise_or))
                    tt(base[:], theta[:].to_broadcast([P, 3]), digit_int[:, bass.ds(n * 3 + 3, 3)], ALU.bitwise_or)
                    dve.wait_ge(count_psum, n + 1)
                    link(nc.vector.tensor_scalar(reached[:], ps[:, 1, 0:3], float(CAP), None, ALU.is_ge, ALU.add, accum_out=digit[:]))
                    link(nc.vector.tensor_scalar(accepted[:], digit[:], digit_unit[:, bass.ds(n, 1)], None, ALU.mult))
            link(tt(theta[:], theta[:], accepted[:], ALU.bitwise_or))
            th = theta[:].bitcast(F32)
            nc.vector.tensor_scalar(is_gt, gate_l, th, None, ALU.is_gt, ALU.add,
                                    accum_out=count[:, 0:1]).then_inc(count_ready, 1)
            link(nc.vector.tensor_scalar(is_eq, gate_l, th, None, ALU.is_equal, ALU.add, accum_out=row_total[:]))
            dve.wait_ge(count_psum, BITS // 2 + 1)
            link(nc.vector.tensor_scalar(need[:], ps[:, 1, 0:1], -1.0, float(CAP), ALU.mult, ALU.add))
            nc.vector.tensor_tensor_scan(scan, ones_l, is_eq, 0.0, ALU.mult, ALU.add).then_inc(count_ready, 1)
            dve.wait_ge(count_ready, BITS // 2 + 2)
            dve.wait_ge(count_psum, BITS // 2 + 2)
            link(nc.vector.tensor_copy(before[:], ps[:, 1, 0:1]))
            link(nc.vector.scalar_tensor_tensor(rank, scan, before[:], is_eq, ALU.add, ALU.subtract))
            link(nc.vector.scalar_tensor_tensor(rank, rank, need[:], is_eq, ALU.is_lt, ALU.mult))
            link(tt(keep, is_gt, rank, ALU.add))
            link(nc.vector.tensor_tensor_scan(scan, ones_l, keep, 0.0, ALU.mult, ALU.add))
            nc.vector.tensor_copy(row_total[:], scan[:, 255:256]).then_inc(count_ready, 1)
            dve.wait_ge(count_psum, BITS // 2 + 3)
            link(nc.vector.tensor_scalar(before[:], ps[:, 1, 0:1], slot_base[:], None, ALU.add))
            nc.vector.scalar_tensor_tensor(rank, scan, before[:], keep, ALU.add, ALU.mult).then_inc(slots_ready, 1)
            dve.wait_ge(slotT_psum, 1)
            for par in range(2):
                dst = slot_t.rearrange("p (q r b) e -> p q r b e", r=2, b=B)[:, :, par]
                src = ps[:, 2, par * P:(par + 1) * P].rearrange("p (e b q) -> p q b e", e=E, b=B)
                last = nc.vector.tensor_copy(dst, src)
            link(last)
            for r, mask in enumerate((first, second)):
                link(tt(picked, slot_t, mask, ALU.mult))
                link(nc.vector.tensor_reduce(slot[r], picked, AX.X, ALU.add))
                link(nc.vector.scalar_tensor_tensor(slot_tmp, slot[r], 0.5, trash_slot[:], ALU.is_lt, ALU.mult))
                link(tt(slot_tmp, slot_tmp, slot[r], ALU.add))
                nc.vector.tensor_scalar_add(to_slot[r][:], slot_tmp, -1.0).then_inc(to_slot_ready, 1)
                dve.wait_ge(to_slot_ready, r + 1)
            for r in range(2):
                nc.vector.scalar_tensor_tensor(weight[r][:], slot[r], 0.5, weight[r][:], ALU.is_ge, ALU.mult)
                last = nc.vector.tensor_scalar(from_slot[r][:], slot[r], -1.0, 0.0, ALU.add, ALU.max)
            link(last)
            stage_end(dve, 4)

            def add_low_rows(b):
                dve.wait_ge(weighted, b + 1)
                rows, x2 = rows_of(b, 2 * D, 3 * D), rows_of(b, D, 2 * D)
                link(tt(rows, rows, mod_of(mod_d, b, 3, ALL), ALU.mult))
                link(tt(x2, x2, rows, ALU.add))

            def groups(pair, ks):
                for k in ks:
                    n = pair * 2 * GROUPS + k
                    for a in range(4):
                        dve.wait_ge(hid_high, 4 * n + a + 1)
                        part = slice(512 * a, 512 * a + 512)
                        nc.vector.scalar_tensor_tensor(hid_parts[1][:, part], ps[:, a], 0.0, hid_parts[0][:, part].bitcast(F32),
                                                       ALU.max, ALU.subtract).then_inc(hid_low, 1)
                    if ks is not LAST or k < 2 * GROUPS - 1:
                        dve.wait_ge(xeT_high, n + 2)
                        tt(xeT_parts[1][:], ps[:, 6], xeT_parts[0][:].bitcast(F32), ALU.subtract).then_inc(xeT_low, 1)
                    dve.wait_ge(ye_psum, n + 2)
                    dve.wait_ge(ye_out[k % 2], (pair * GROUPS + k // 2 + 1) * 16)
                    nc.vector.tensor_copy(y_sb[k % 2].rearrange("p t d -> p (t d)"), ps[:, 4 + k % 2]).then_inc(ye_ready, 1)
                    if ks is LAST:
                        for b in {7: (0,), 8: (1,), 9: (2, 3)}.get(k, ()):
                            add_low_rows(b)

            dve.wait_ge(xeT_high, 1)
            tt(xeT_parts[1][:], ps[:, 6], xeT_parts[0][:].bitcast(F32), ALU.subtract).then_inc(xeT_low, 1)
            groups(0, FIRST)
            with dve.Fori(0, PAIRS) as pair:
                groups(pair, PAIR)
            groups(PAIRS, LAST)

            for b in range(B):
                for half in range(2):
                    dve.wait_ge(high_rows_in[b][half], 16 * HALF_ROW)
                    for t in range(half * HALF_ROW, (half + 1) * HALF_ROW):
                        tile = t * B + b
                        row = qkv[:, tile, 0:D]
                        last = nc.vector.scalar_tensor_tensor(row, row, weight[1][:, tile:tile + 1], mod_d[:, b, 3, :],
                                                              ALU.mult, ALU.mult)
                    link(last)
                    tiles = slice(half * HALF_ROW, (half + 1) * HALF_ROW)
                    rows = tile_view[:, tiles, b, 0:D]
                    tt(rows, rows, tile_view[:, tiles, b, D:2 * D], ALU.add).then_inc(out_ready, 1)

        @block.tensor
        def _(pe):
            mm, transpose = nc.tensor.matmul, nc.tensor.transpose
            pe.wait_ge(siluT_ready, 1)
            pe.wait_ge(wmod_in, 32)
            for i, m in enumerate((SA, SB, CA, CB)):
                for dc in range(DC):
                    for c in range(DC):
                        last = mm(modT_ps[:, i, dc], wmod_sb[c][:, m * D + dc * P:m * D + (dc + 1) * P], siluT[:, c, :],
                                  start=c == 0, stop=c == DC - 1)
            last.then_inc(modT_psum, 1)
            for a in range(2):
                for c in range(DC):
                    last = mm(ps[0:B, 1 + a, :], siluT[:, c, :], wmod_sb[c][:, (1 + a) * BANK:(2 + a) * BANK],
                              start=c == 0, stop=c == DC - 1)
                last.then_inc(mod_psum, 1)

            def h_transposes(b):
                pe.wait_ge(h_ready, b + 1)
                for g in range(4):
                    half, dc = g // 2, g % 2
                    if b >= 1:
                        pe.wait_ge(h_full_ready, 4 * (b - 1) + g + 1)
                    for t in range(4):
                        last = transpose(ps[:, g, t * P:(t + 1) * P],
                                         x_buf[b % 2][:, half * 4 + t, dc * P:(dc + 1) * P], ident[:])
                    last.then_inc(hT_psum, 1)

            def qkv_products(b, half):
                pe.wait_ge(hT_low, 4 * b + 2 * half + 2)
                for tb in range(half * TB // 2, (half + 1) * TB // 2):
                    bank = 4 + 2 * (tb % 2)
                    if b >= 1 or tb >= 2:
                        pe.wait_ge(qkv_ready, TB * b + tb - 1)
                    elif b == 0:
                        pe.wait_ge(kk_copied, tb + 1)
                    in_order = slice(tb * P, (tb + 1) * P)
                    every_other = slice(tb // 2 * 2 * P + tb % 2, tb // 2 * 2 * P + 2 * P, 2)
                    for lo, hi, times in ((0, 512, in_order), (512, 768, every_other)):
                        for dc in range(DC):
                            for i, (a, x) in enumerate(PASSES):
                                last = mm(ps[:, bank + lo // BANK, 0:hi - lo], hT_parts[b % 2][a][:, dc, times],
                                          wqkv_parts[dc][x][:, lo:hi], start=dc == 0 and i == 0, stop=dc == DC - 1 and i == 2)
                    last.then_inc(qkv_psum, 1)

            pe.wait_ge(dft_in, 16)
            pe.wait_ge(kkT_ready, 1)
            for j in range(JP):
                for parity in range(2):
                    for c in range(parity, CT, 2):
                        last = mm(ps[:, 4 + j, parity * D:(parity + 1) * D], dft[:, c, j * P:(j + 1) * P], kkT[:, c, :],
                                  start=c == parity, stop=c == CT - 2 + parity)
                if j % 2:
                    last.then_inc(kk_spec_psum, 1)
            pe.wait_ge(ident_in, 16)
            pe.wait_ge(modT_ready, 2)
            pe.wait_ge(mod_read, 1)
            h_transposes(0)
            pe.wait_ge(w_qkv_low, 2)
            for b in range(B):
                qkv_products(b, 0)
                if b + 1 < B:
                    h_transposes(b + 1)
                qkv_products(b, 1)
            stage_end(pe, 0)

            pe.wait_ge(idft_in, 16)

            def forward(b, groups=range(JT)):
                for n in groups:
                    j, parity = n // 2, n % 2
                    pe.wait_ge(spec_ready, JT * b + n + 1)
                    for c in range(parity, CT, 2):
                        halves = tile_view[:, c::CT, bass.ds(b, 1), 2 * D:3 * D].rearrange("p h o n -> p h (o n)")
                        last = mm(ps[:, n % 4].rearrange("p (h e) -> p h e", h=2), dft[:, c, j * P:(j + 1) * P], halves,
                                  start=c == parity, stop=c == CT - 2 + parity)
                    last.then_inc(spec_psum, 1)

            def inverse(b):
                for i, c in enumerate(BY_PARITY):
                    if i % 2 == 0:
                        for who in range(2):
                            pe.wait_ge(fold_ready[i // 2][who], b + 1)
                    pe.wait_ge(conv_ready, CT * b + i + 1)
                    for j in range(JP):
                        last = mm(ps[:, 4 + c], idft[:, j, c * P:(c + 1) * P], folded(b, c % 2)[:, j].rearrange("p h e -> p (h e)"),
                                  start=j == 0, stop=j == JP - 1)
                    last.then_inc(conv_psum, 1)

            forward(0)
            forward(1)
            forward(2, range(JT // 2))
            inverse(0)
            forward(2, range(JT // 2, JT))
            forward(3)
            for b in range(1, B):
                inverse(b)
            stage_end(pe, 1)

            with pe.Fori(0, HEADS // 2) as hh:
                for s in range(2):
                    h = hh * 2 + s
                    pe.wait_ge(toep_low, h + 1)
                    for g in range(4):
                        pe.wait_ge(kv_low, 4 * h + g + 1)
                        pe.wait_ge(mix_read, 4 * h + g + 1)
                        steps = []
                        for o in range(OFFS):
                            lo = max(2 * g, o)
                            if lo <= 2 * g + 1:
                                steps.append((o, lo))
                        for n, (o, lo) in enumerate(steps):
                            cnt = (2 * g + 2 - lo) * B
                            src = slice((lo - o) * B * 64, (lo - o) * B * 64 + cnt * 64)
                            for i, (a, x) in enumerate(PASSES):
                                last = mm(ps[:, 4 * s + g, (lo - 2 * g) * B * 64:BANK],
                                          toep_parts[s][a][:, o * P:(o + 1) * P], kv_parts[s][x][:, src],
                                          start=n == 0 and i == 0, stop=n == len(steps) - 1 and i == 2)
                        last.then_inc(mix_psum, 1)
            stage_end(pe, 2)

            def y_transposes(b):
                for g in range(4):
                    if g >= 2:
                        pe.wait_ge(yT_ready, 4 * b + g - 1)
                    for t in range(4):
                        tb = (g % 2) * 4 + t
                        last = transpose(ps[:, 4 + g % 2, t * P:(t + 1) * P],
                                         tile_view[:, tb, b, (g // 2) * P:(g // 2 + 1) * P], ident[:])
                    last.then_inc(yT_psum, 1)

            def attention_out(b):
                pe.wait_ge(yT_ready, 4 * b + 4)
                pe.wait_ge(wo_ready, 2 * b + 1)
                if b >= 1:
                    pe.wait_ge(x2_ready, b)
                for tb in range(TB):
                    for cc in range(DC):
                        last = mm(ps[:, tb // 2, (tb % 2) * D:(tb % 2 + 1) * D], yT[:, cc, tb * P:(tb + 1) * P],
                                  wo_gated[b % 2][:, cc, :], start=cc == 0, stop=cc == DC - 1)
                last.then_inc(attn_psum, 1)

            def h2_transposes(b):
                pe.wait_ge(norm2_ready, b + 1)
                if 1 <= b < B - 1:
                    pe.wait_ge(logit_ready, b)
                for g in range(4):
                    if g >= 2:
                        pe.wait_ge(h2T_ready, 4 * b + g - 1)
                    for t in range(4):
                        tb = (g % 2) * 4 + t
                        last = transpose(ps[:, 6 + g % 2, t * P:(t + 1) * P],
                                         tile_view[:, tb, b, 2 * D + (g // 2) * P:2 * D + (g // 2 + 1) * P], ident[:])
                    last.then_inc(h2T_psum, 1)

            def router(b):
                pe.wait_ge(h2T_ready, 4 * b + 4)
                for tb in range(TB):
                    for cc in range(DC):
                        last = mm(ps[:, LOGIT_BANK[b], tb * E:(tb + 1) * E], h2T[:, cc, tb * P:(tb + 1) * P], wr_sb[:, cc, :],
                                  start=cc == 0, stop=cc == DC - 1)
                last.then_inc(logit_psum, 1)

            for b in range(2):
                y_transposes(b)
                attention_out(b)
            for b in range(B):
                h2_transposes(b)
                if b + 2 < B:
                    y_transposes(b + 2)
                router(b)
                if b + 2 < B:
                    attention_out(b + 2)
            stage_end(pe, 3)

            pe.wait_ge(gate_ready, B)
            for par in range(2):
                cols = gate_cols[:, par].rearrange("p e b q -> p (e b q)")
                last = transpose(ps[:, 0, par * P:(par + 1) * P], cols, ident[:])
            last.then_inc(gateT_psum, 1)
            with pe.Fori(0, BITS // 2) as i:
                pe.wait_ge(count_ready, i + 1)
                mm(ps[:, 1, 0:3], group_ones[:], count[:], start=True, stop=True).then_inc(count_psum, 1)
            pe.wait_ge(count_ready, BITS // 2 + 1)
            mm(ps[:, 1, 0:1], group_ones[:], count[:, 0:1], start=True, stop=True).then_inc(count_psum, 1)
            for n in (2, 3):
                pe.wait_ge(count_ready, BITS // 2 + n)
                mm(ps[:, 1, 0:1], group_before[:], row_total[:], start=True, stop=True).then_inc(count_psum, 1)
            pe.wait_ge(slots_ready, 1)
            for par in range(2):
                last = transpose(ps[:, 2, par * P:(par + 1) * P], rank[:, par * P:(par + 1) * P], ident[:])
            last.then_inc(slotT_psum, 1)
            stage_end(pe, 4)

            def transpose_rows(count, s):
                pe.wait_ge(xe_in[s], 16 * count)
                for dc in range(DC):
                    for t in range(GT):
                        last = transpose(ps[:, 6, dc * GROUP + t * P:dc * GROUP + (t + 1) * P],
                                         xe[s][:, t, dc * P:(dc + 1) * P], ident[:])
                last.then_inc(xeT_psum, 1)

            def groups(pair, ks):
                for k in ks:
                    q, g, s = k // GROUPS % 2, k % GROUPS, k % 2
                    e, n = pair * 2 + k // GROUPS, pair * 2 * GROUPS + k
                    if g == 0:
                        pe.wait_ge(w_low, PIECES * (e + 1))
                    pe.wait_ge(xeT_low, n + 1)
                    for f in range(FC):
                        for dc in range(DC):
                            for i, (a, x) in enumerate(PASSES):
                                last = mm(ps[:, f // 2, (f % 2) * GROUP:(f % 2 + 1) * GROUP],
                                          w1_parts[q][a][:, dc * F + f * P:dc * F + (f + 1) * P],
                                          xeT_parts[x][:, dc * GROUP:(dc + 1) * GROUP],
                                          start=dc == 0 and i == 0, stop=dc == DC - 1 and i == 2)
                        if f % 2:
                            last.then_inc(hid_psum, 1)
                    if ks is not LAST or g < GROUPS - 1:
                        transpose_rows(pair * GROUPS + (k + 1) // 2 + 1, (k + 1) % 2)
                    for t in range(GT):
                        for f in range(FC):
                            if t == 0 and f % 2 == 0:
                                pe.wait_ge(hid_low, 4 * n + f // 2 + 1)
                            for i, (a, x) in enumerate(PASSES):
                                last = mm(ps[:, 4 + s, t * D:(t + 1) * D],
                                          hid_parts[a][:, f * GROUP + t * P:f * GROUP + (t + 1) * P],
                                          w2_parts[q][x][:, f * D:(f + 1) * D],
                                          start=f == 0 and i == 0, stop=f == FC - 1 and i == 2)
                    last.then_inc(ye_psum, 1)

            transpose_rows(1, 0)
            groups(0, FIRST)
            with pe.Fori(0, PAIRS) as pair:
                groups(pair, PAIR)
            groups(PAIRS, LAST)


def kernel(**inputs):
    import concourse.bacc as bacc
    from concourse.bass_utils import run_bass_kernel_spmd

    nc = bacc.Bacc("TRN2", target_bir_lowering=False, num_devices=1)
    arrays, args, tables = {}, [], {}
    given = {name: np.asarray(a) for name, a in inputs.items()}
    attn = {name[8:]: a for name, a in given.items() if name.startswith("L0_attn_")}
    wo = attn["Wo"].reshape(D, NJ, HEADS).transpose(2, 1, 0).reshape(D, D)
    laid_out = {
        "u": attn["u"],
        "w_qkv": np.concatenate([attn["Wq"].T, attn["Wv"].T, attn["Wk"].T], axis=1),
        "b_all": np.concatenate([attn["bq"], attn["bv"], attn["bk"], attn["bo"]])[None, :],
        "k_taps": attn["ssm_k_kernel"].T,
        "k_skip": attn["ssm_k_D"],
        "ssm_kernel": attn["ssm_kernel"][:, ::-1],
        "ssm_skip": attn["D"],
        "w_out": wo,
        "w_router": given["L0_ffn_Wr"],
        "w1": given["L0_ffn_W1"],
        "w2": given["L0_ffn_W2"],
        "cT": given["L0_c"].T,
        "wmod": given["L0_wmod"],
    }
    for name, a in laid_out.items():
        a = np.ascontiguousarray(a)
        arrays[f"in_{name}"] = a
        args.append(nc.dram_tensor(f"in_{name}", a.shape, mybir.dt.from_np(a.dtype), kind="ExternalInput").ap())
    for name, a in constants().items():
        arrays[f"const_{name}"] = a
        tables[name] = nc.dram_tensor(f"const_{name}", a.shape, mybir.dt.from_np(a.dtype), kind="ExternalInput").ap()
    out = nc.dram_tensor("out", [B, L, D], F32, kind="ExternalOutput").ap()
    adaln_block(nc, *args, tables, out)
    r = run_bass_kernel_spmd(nc, [arrays], core_ids=[0])
    return r.results[0]["out"]
```
